# Optimizing a Trainium2 kernel written in Bass

```python
import numpy as np
import jax
import jax.numpy as jnp

def _softmax(x, axis=-1):
    return jax.nn.softmax(x, axis=axis)

def _gelu(x):
    return jax.nn.gelu(x, approximate=True)

def _silu(x):
    return jax.nn.silu(x)

def _sigmoid(x):
    return jax.nn.sigmoid(x)

def _layernorm(x, axis=-1, eps=1e-05):
    m = jnp.mean(x, axis=axis, keepdims=True)
    v = jnp.var(x, axis=axis, keepdims=True)
    return (x - m) / jnp.sqrt(v + eps)

def _scatter_add(tgt, idx, src, axis=0):
    return tgt.at[idx].add(src)

def _segment_sum(src, seg, n):
    return jax.ops.segment_sum(src, seg, n)
kernel_name = 'mk_seq_postln_d2_jaxref_r8_e1a34d'

def setup_inputs(seed: int=0):
    np.random.seed(seed)
    _w = jnp.asarray

    def _L0_attn_setup():
        import jax, jax.numpy as jnp
        import numpy as np
        import math
        N_HEAD = 16
        ATTN_THRESHOLD = -0.1
        EPS = 1e-06
        key = jax.random.key(seed)
        ks = jax.random.split(key, 5)
        B, T, C = (2, 256, 256)
        s = 1.0 / math.sqrt(C)
        return {'x': jax.random.normal(ks[0], (B, T, C), dtype=jnp.float32), 'Wq': jax.random.normal(ks[1], (C, C), dtype=jnp.float32) * s, 'Wk': jax.random.normal(ks[2], (C, C), dtype=jnp.float32) * s, 'Wv': jax.random.normal(ks[3], (C, C), dtype=jnp.float32) * s, 'Wo': jax.random.normal(ks[4], (C, C), dtype=jnp.float32) * s}
    _L0_attn_in = _L0_attn_setup()

    def _L0_ffn_setup():
        import jax, jax.numpy as jnp
        import numpy as np
        HIDDEN = 256
        INTER = 1024
        SCALE = 64.0

        def fwht(x):
            orig_shape = x.shape
            n = orig_shape[-1]
            x = x.reshape(-1, n)
            h = 1
            while h < n:
                x = x.reshape(-1, n // (2 * h), 2, h)
                a, b = (x[:, :, 0, :], x[:, :, 1, :])
                x = jnp.stack([a + b, a - b], axis=2).reshape(-1, n)
                h *= 2
            return (x / jnp.sqrt(jnp.asarray(n, x.dtype))).reshape(orig_shape)
        key = jax.random.key(seed)
        ks = jax.random.split(key, 8)
        inp = jax.random.normal(ks[0], (4, 256, HIDDEN), dtype=jnp.float32)
        SU_ug = jnp.where(jax.random.bernoulli(ks[1], 0.5, (HIDDEN,)), 1.0, -1.0).astype(jnp.float32)
        SU_dp = jnp.where(jax.random.bernoulli(ks[2], 0.5, (INTER,)), 1.0, -1.0).astype(jnp.float32)
        Wscale_ug = jax.random.uniform(ks[3], (2 * INTER,), jnp.float32, 0.5, 1.5)
        Wscale_dp = jax.random.uniform(ks[4], (HIDDEN,), jnp.float32, 0.5, 1.5)
        W_up = jax.random.normal(ks[5], (INTER, HIDDEN), dtype=jnp.float32) * 0.02
        W_gate = jax.random.normal(ks[6], (INTER, HIDDEN), dtype=jnp.float32) * 0.02
        W_down = jax.random.normal(ks[7], (HIDDEN, INTER), dtype=jnp.float32) * 0.02
        return {'input': inp, 'SU_ug': SU_ug, 'SU_dp': SU_dp, 'Wscale_ug': Wscale_ug, 'Wscale_dp': Wscale_dp, 'W_up': W_up, 'W_gate': W_gate, 'W_down': W_down}
    _L0_ffn_in = _L0_ffn_setup()

    def _L1_attn_setup():
        import jax, jax.numpy as jnp
        import numpy as np
        N_HEADS = 32
        N_KV_HEADS = 8
        HEAD_DIM = 64
        D_MODEL = 256
        SLIDING_WINDOW = 64
        ROPE_THETA = 10000.0
        PAST_LENGTH = 0
        EPS = 1e-06

        def _rms_norm(x, w):
            xf = x.astype(jnp.float32)
            rms = jax.lax.rsqrt(jnp.mean(xf * xf, axis=-1, keepdims=True) + EPS)
            return (xf * rms).astype(x.dtype) * w

        def _rope(q, k, past_length):
            s, d = (q.shape[2], q.shape[3])
            inv_freq = 1.0 / ROPE_THETA ** (jnp.arange(0, d, 2, dtype=jnp.float32) / d)
            pos = jnp.arange(s, dtype=jnp.float32) + past_length
            ang = pos[:, None] * inv_freq[None, :]
            emb = jnp.concatenate([ang, ang], axis=-1)
            cos, sin = (jnp.cos(emb), jnp.sin(emb))

            def rot_half(x):
                x1, x2 = jnp.split(x, 2, axis=-1)
                return jnp.concatenate([-x2, x1], axis=-1)
            q = q * cos + rot_half(q) * sin
            k = k * cos + rot_half(k) * sin
            return (q, k)

        def _sliding_mask(seq_len, total_len, past_length):
            q_idx = jnp.arange(seq_len)[:, None]
            k_idx = jnp.arange(total_len)[None, :]
            causal = q_idx + past_length >= k_idx
            window = q_idx + past_length - k_idx < SLIDING_WINDOW
            keep = causal & window
            return jnp.where(keep, 0.0, -jnp.inf).astype(jnp.float32)[None, None]
        key = jax.random.key(seed)
        k1, k2, k3 = jax.random.split(key, 3)
        B, S = (1, 256)
        q_size = N_HEADS * HEAD_DIM
        kv_size = N_KV_HEADS * HEAD_DIM
        return {'x': jax.random.normal(k1, (B, S, D_MODEL), dtype=jnp.float32), 'w_qkv': jax.random.normal(k2, (q_size + 2 * kv_size, D_MODEL), dtype=jnp.float32) * D_MODEL ** (-0.5), 'w_out': jax.random.normal(k3, (D_MODEL, q_size), dtype=jnp.float32) * q_size ** (-0.5), 'q_norm_w': jnp.ones((HEAD_DIM,), dtype=jnp.float32), 'k_norm_w': jnp.ones((HEAD_DIM,), dtype=jnp.float32)}
    _L1_attn_in = _L1_attn_setup()

    def _L1_ffn_setup():
        import jax, jax.numpy as jnp
        import numpy as np
        DIM_IN = 256
        DIM_HIDDEN = 1024
        key = jax.random.key(seed)
        k_x, k_g, k_u, k_d = jax.random.split(key, 4)
        s_in = 1.0 / np.sqrt(DIM_IN)
        s_hid = 1.0 / np.sqrt(DIM_HIDDEN)
        x = jax.random.normal(k_x, (4, 256, DIM_IN), dtype=jnp.float32)
        w_gate = jax.random.uniform(k_g, (DIM_HIDDEN, DIM_IN), jnp.float32, -s_in, s_in)
        w_up = jax.random.uniform(k_u, (DIM_HIDDEN, DIM_IN), jnp.float32, -s_in, s_in)
        w_down = jax.random.uniform(k_d, (DIM_IN, DIM_HIDDEN), jnp.float32, -s_hid, s_hid)
        return {'x': x, 'w_gate': w_gate, 'w_up': w_up, 'w_down': w_down}
    _L1_ffn_in = _L1_ffn_setup()
    _d = {'L0_attn_x': _L0_attn_in['x'], 'L0_attn_Wq': _L0_attn_in['Wq'], 'L0_attn_Wk': _L0_attn_in['Wk'], 'L0_attn_Wv': _L0_attn_in['Wv'], 'L0_attn_Wo': _L0_attn_in['Wo'], 'L0_ffn_SU_ug': _L0_ffn_in['SU_ug'], 'L0_ffn_SU_dp': _L0_ffn_in['SU_dp'], 'L0_ffn_Wscale_ug': _L0_ffn_in['Wscale_ug'], 'L0_ffn_Wscale_dp': _L0_ffn_in['Wscale_dp'], 'L0_ffn_W_up': _L0_ffn_in['W_up'], 'L0_ffn_W_gate': _L0_ffn_in['W_gate'], 'L0_ffn_W_down': _L0_ffn_in['W_down'], 'L1_attn_w_qkv': _L1_attn_in['w_qkv'], 'L1_attn_w_out': _L1_attn_in['w_out'], 'L1_attn_q_norm_w': _L1_attn_in['q_norm_w'], 'L1_attn_k_norm_w': _L1_attn_in['k_norm_w'], 'L1_ffn_w_gate': _L1_ffn_in['w_gate'], 'L1_ffn_w_up': _L1_ffn_in['w_up'], 'L1_ffn_w_down': _L1_ffn_in['w_down']}
    _x0 = _d['L0_attn_x']
    _d['L0_attn_x'] = jax.random.normal(jax.random.fold_in(jax.random.key(seed), 1), (2, 512, 256), dtype=_x0.dtype)
    del _x0
    return _d

def reference(L0_attn_x, L0_attn_Wq, L0_attn_Wk, L0_attn_Wv, L0_attn_Wo, L0_ffn_SU_ug, L0_ffn_SU_dp, L0_ffn_Wscale_ug, L0_ffn_Wscale_dp, L0_ffn_W_up, L0_ffn_W_gate, L0_ffn_W_down, L1_attn_w_qkv, L1_attn_w_out, L1_attn_q_norm_w, L1_attn_k_norm_w, L1_ffn_w_gate, L1_ffn_w_up, L1_ffn_w_down):

    def _L0_attn_ref(x, Wq, Wk, Wv, Wo):
        import jax, jax.numpy as jnp
        import numpy as np
        import math
        N_HEAD = 16
        ATTN_THRESHOLD = -0.1
        EPS = 1e-06
        B, T, C = x.shape
        H = N_HEAD
        hd = C // H
        scale = 1.0 / math.sqrt(hd)

        def proj(W):
            return jnp.einsum('btc,oc->bto', x, W).reshape(B, T, H, hd).swapaxes(1, 2)
        q, k, v = (proj(Wq), proj(Wk), proj(Wv))
        scores = jnp.einsum('bhqd,bhkd->bhqk', q, k) * scale
        causal = jnp.tril(jnp.ones((T, T), dtype=bool))
        w = jnp.where(causal, jax.nn.relu(scores - ATTN_THRESHOLD), 0.0)
        w = w / (jnp.sum(w, axis=-1, keepdims=True) + EPS)
        out = jnp.einsum('bhqk,bhkd->bhqd', w, v)
        out = out.swapaxes(1, 2).reshape(B, T, C)
        return jnp.einsum('btc,oc->bto', out, Wo)

    def _L0_ffn_ref(input, SU_ug, SU_dp, Wscale_ug, Wscale_dp, W_up, W_gate, W_down):
        import jax, jax.numpy as jnp
        import numpy as np
        HIDDEN = 256
        INTER = 1024
        SCALE = 64.0

        def fwht(x):
            orig_shape = x.shape
            n = orig_shape[-1]
            x = x.reshape(-1, n)
            h = 1
            while h < n:
                x = x.reshape(-1, n // (2 * h), 2, h)
                a, b = (x[:, :, 0, :], x[:, :, 1, :])
                x = jnp.stack([a + b, a - b], axis=2).reshape(-1, n)
                h *= 2
            return (x / jnp.sqrt(jnp.asarray(n, x.dtype))).reshape(orig_shape)
        n = SU_ug.shape[0]
        x = input.reshape(-1, n)
        x = fwht(x * SU_ug) / SCALE
        x_up = x @ W_up.T * (Wscale_ug[:INTER] * SCALE)
        x_gate = x @ W_gate.T * (Wscale_ug[INTER:] * SCALE)
        x = jax.nn.silu(x_gate) * x_up
        x = fwht(x * SU_dp) / SCALE
        x = x @ W_down.T * (Wscale_dp * SCALE)
        return x.reshape(input.shape)

    def _L1_attn_ref(x, w_qkv, w_out, q_norm_w, k_norm_w):
        import jax, jax.numpy as jnp
        import numpy as np
        N_HEADS = 32
        N_KV_HEADS = 8
        HEAD_DIM = 64
        D_MODEL = 256
        SLIDING_WINDOW = 64
        ROPE_THETA = 10000.0
        PAST_LENGTH = 0
        EPS = 1e-06

        def _rms_norm(x, w):
            xf = x.astype(jnp.float32)
            rms = jax.lax.rsqrt(jnp.mean(xf * xf, axis=-1, keepdims=True) + EPS)
            return (xf * rms).astype(x.dtype) * w

        def _rope(q, k, past_length):
            s, d = (q.shape[2], q.shape[3])
            inv_freq = 1.0 / ROPE_THETA ** (jnp.arange(0, d, 2, dtype=jnp.float32) / d)
            pos = jnp.arange(s, dtype=jnp.float32) + past_length
            ang = pos[:, None] * inv_freq[None, :]
            emb = jnp.concatenate([ang, ang], axis=-1)
            cos, sin = (jnp.cos(emb), jnp.sin(emb))

            def rot_half(x):
                x1, x2 = jnp.split(x, 2, axis=-1)
                return jnp.concatenate([-x2, x1], axis=-1)
            q = q * cos + rot_half(q) * sin
            k = k * cos + rot_half(k) * sin
            return (q, k)

        def _sliding_mask(seq_len, total_len, past_length):
            q_idx = jnp.arange(seq_len)[:, None]
            k_idx = jnp.arange(total_len)[None, :]
            causal = q_idx + past_length >= k_idx
            window = q_idx + past_length - k_idx < SLIDING_WINDOW
            keep = causal & window
            return jnp.where(keep, 0.0, -jnp.inf).astype(jnp.float32)[None, None]
        b, s, _ = x.shape
        n_rep = N_HEADS // N_KV_HEADS
        q_size = N_HEADS * HEAD_DIM
        kv_size = N_KV_HEADS * HEAD_DIM
        qkv = jnp.einsum('bsd,od->bso', x, w_qkv)
        q, k, v = jnp.split(qkv, [q_size, q_size + kv_size], axis=-1)
        q = q.reshape(b, s, N_HEADS, HEAD_DIM).transpose(0, 2, 1, 3)
        k = k.reshape(b, s, N_KV_HEADS, HEAD_DIM).transpose(0, 2, 1, 3)
        v = v.reshape(b, s, N_KV_HEADS, HEAD_DIM).transpose(0, 2, 1, 3)
        q = _rms_norm(q, q_norm_w)
        k = _rms_norm(k, k_norm_w)
        q, k = _rope(q, k, PAST_LENGTH)
        k_rep = jnp.repeat(k, n_rep, axis=1)
        v_rep = jnp.repeat(v, n_rep, axis=1)
        scale = HEAD_DIM ** (-0.5)
        scores = jnp.einsum('bhqd,bhkd->bhqk', q, k_rep) * scale
        scores = scores + _sliding_mask(s, s, PAST_LENGTH)
        probs = jax.nn.softmax(scores, axis=-1)
        attn = jnp.einsum('bhqk,bhkd->bhqd', probs, v_rep)
        attn = attn.transpose(0, 2, 1, 3).reshape(b, s, q_size)
        return jnp.einsum('bso,do->bsd', attn, w_out)

    def _L1_ffn_ref(x, w_gate, w_up, w_down):
        import jax, jax.numpy as jnp
        import numpy as np
        DIM_IN = 256
        DIM_HIDDEN = 1024
        gate = jnp.einsum('bsd,hd->bsh', x, w_gate)
        up = jnp.einsum('bsd,hd->bsh', x, w_up)
        gated = jax.nn.silu(gate) * up
        return jnp.einsum('bsh,dh->bsd', gated, w_down)
    x = L0_attn_x
    x = _layernorm(x + _L0_attn_ref(x, L0_attn_Wq, L0_attn_Wk, L0_attn_Wv, L0_attn_Wo), axis=-1)
    x = _layernorm(x + _L0_ffn_ref(x, L0_ffn_SU_ug, L0_ffn_SU_dp, L0_ffn_Wscale_ug, L0_ffn_Wscale_dp, L0_ffn_W_up, L0_ffn_W_gate, L0_ffn_W_down), axis=-1)
    x = _layernorm(x + _L1_attn_ref(x, L1_attn_w_qkv, L1_attn_w_out, L1_attn_q_norm_w, L1_attn_k_norm_w), axis=-1)
    x = _layernorm(x + _L1_ffn_ref(x, L1_ffn_w_gate, L1_ffn_w_up, L1_ffn_w_down), axis=-1)
    return x

_drawn_inputs = setup_inputs


def setup_inputs(seed=0):
    import zlib

    import numpy as np

    out = dict(_drawn_inputs(seed))
    spreads = {'L1_attn_q_norm_w': (1.0, 0.2), 'L1_attn_k_norm_w': (1.0, 0.2)}
    factors = {'L0_ffn_Wscale_ug': 3.777, 'L0_ffn_Wscale_dp': 5.271}
    for name, (base, spread) in spreads.items():
        noise = np.random.default_rng([zlib.crc32(name.encode()), seed]).standard_normal(out[name].shape)
        drawn = base * np.exp(spread * noise) if base else spread * noise
        out[name] = jnp.asarray(drawn.astype(out[name].dtype))
    for name, factor in factors.items():
        out[name] = (out[name] * factor).astype(out[name].dtype)
    return out
```

```python
from contextlib import ExitStack

import numpy as np

import concourse.bass as bass
from concourse import mybir

ALU = mybir.AluOpType
ACT = mybir.ActivationFunctionType
AX = mybir.AxisListType
F32 = mybir.dt.float32
F32R = mybir.dt.float32r
BF16 = mybir.dt.bfloat16

P = 128
B, T, C = 2, 512, 256
KB = C // P
TT = T // P
LN_EPS = 1e-5
H0, HD0 = 16, 16
HG = 4
NHG = H0 // HG
ATTN_THRESHOLD, ATTN_EPS = -0.1, 1e-6
W0_AT = [0, 512, 896, 1152]
W0_COLS = 1280
INTER = 1024
NI = INTER // P
KV, REP, HD1 = 8, 4, 64
WIN = 64
NQ = T // WIN
GW = (REP + 1) * HD1
GV = GW + HD1
RMS_EPS = 1e-6
MASKED = -1e30
NIT = B * KV
RING = 6

CHUNKS = ([("x", 0, "split", "dve"), ("w0", 0, "split", "dve"), ("sel", 0, "copy", "dve"),
           ("sel", 1, "copy", "dve"), ("w0", 1, "split", "dve"), ("x", 1, "split", "dve"),
           ("had", 0, "copy", "dve"), ("down0", 0, "tree", "pool"), ("down0", 1, "tree", "pool")]
          + [("ug0", c, "split", "pool") for c in range(4)]
          + [("msk", 0, "copy", "dve")]
          + [("qkv", g, "split", "pool") for g in range(KV)]
          + [("wout", i, "split", "pool") for i in range(NIT)]
          + [("ug1", c, "split", "pool") for c in range(4)]
          + [("down1", c, "split", "pool") for c in range(2)])
LOADS = [k for k, ch in enumerate(CHUNKS) if ch[2] != "tree"]
CHUNK_NO = {(name, c): k for k, (name, c, _, _) in enumerate(CHUNKS)}
CHUNK_COLS = {"x": 1024, "w0": 1024, "sel": 1024, "had": 256, "down0": 1024, "ug0": 1024, "msk": 1152,
              "qkv": KB * GV, "wout": 512, "ug1": 1024, "down1": 1024}


def counted(k, wanted):
    return sum(1 for ch in CHUNKS[:k + 1] if wanted(ch))


def program_steps():
    s = [("chunk", ("x", 0)), ("chunk", ("w0", 0)), ("qk0", 0), ("chunk", ("sel", 0)), ("chunk", ("sel", 1)),
         ("chunk", ("w0", 1)), ("v0", 0), ("chunk", ("x", 1)), ("chunk", ("had", 0)), ("tree",)]
    for b in range(B):
        if b:
            s += [("qk0", b), ("v0", b)]
        for hg in range(NHG + 2):
            if hg < NHG:
                s += [("stack0", b, hg), ("scores0", b, hg)]
            if b == 0 and hg < 2:
                s += [("chunk", ("down0", hg)), ("prep_down", hg)]
            if b == 0 and hg >= 2:
                s += [("chunk", ("ug0", hg - 2)), ("prep_ug", hg - 2)]
            if 1 <= hg <= NHG:
                s += [("pv0", b, hg - 1)]
            if hg >= 2:
                s += [("turn0", b, hg - 2)]
        s += [("at0", b), ("wo0", b), ("ln", 0, b), ("xt", 1, b)]
    s += [("chunk", ("msk", 0)), ("rope_tables",)]
    for b in range(B):
        s += [("ffn", 0, b, i) for i in range(NI + 1)] + [("ln", 1, b), ("xt", 2, b)]
    for k in range(NIT + 2):
        if k < NIT:
            s.append(("proj1", k))
        if 1 <= k <= NIT:
            s.append(("turn1", k - 1))
        if k >= 2:
            s.append(("pv1", k - 2))
        if k < NIT:
            s.append(("rms1", k))
        if 1 <= k <= NIT:
            s.append(("scores1", k - 1))
        if k < NIT:
            s.append(("rope1", k))
        if k < NIT:
            s.append(("chunk", ("wout", k)))
        if k >= 2:
            s.append(("out1", k - 2))
            if (k - 2) % KV == KV - 1:
                b = (k - 2) // KV
                s += [("ln", 2, b), ("xt", 3, b)]
        if k == NIT:
            s += [("chunk", ("ug1", c)) for c in range(4)] + [("chunk", ("down1", c)) for c in range(2)]
    for b in range(B):
        s += [("ffn", 1, b, i) for i in range(NI + 1)] + [("ln", 3, b)]
    at = [n for n, x in enumerate(s) if x == ("ffn", 0, 0, 0)][0]
    for g in range(KV):
        s.insert(at + 2 + 2 * g, ("chunk", ("qkv", g)))
    return s


STEPS = program_steps()
assert [k for k in (CHUNK_NO[s[1]] for s in STEPS if s[0] == "chunk")] == list(range(len(CHUNKS)))


def post_ln_two_layers(nc, dram, out):
    with ExitStack() as ctx:
        def sem(name):
            return ctx.enter_context(nc.semaphore(name))

        def place(scope, name, shape, dt):
            return scope.enter_context(nc.sbuf_tensor(name, [P] + shape, dt))

        def keep(name, shape, dt=F32):
            return place(ctx, name, shape, dt)

        xh = keep("x_t_high", [B, KB, T], F32R)
        xl = keep("x_t_low", [B, KB, T], F32R)
        xn = keep("x_rows", [B * TT, C])
        raw = keep("raw_chunks", [2, 1152])
        ident = keep("identity", [P])
        had = keep("hadamard", [2, P], F32R)
        tri = keep("causal_block", [P])
        eye2 = keep("eye_twice", [P], BF16)
        wmask = keep("window_mask", [2, 512], BF16)
        sign_ug = keep("sign_ug", [KB])
        sign_dp = keep("sign_dp", [NI])
        scale_ug = keep("scale_ug", [2 * NI])
        scale_dp = keep("scale_dp", [C])
        bias0 = keep("bias_threshold", [1])
        half = keep("minus_half", [REP * (REP + 1)])
        stats = keep("ln_stats", [TT, 6])
        mv = keep("ln_mean_var", [TT, 2])
        var_eps = keep("ln_var_eps", [TT])
        rstd = keep("ln_rstd", [TT])
        rs0 = keep("row_sums0", [TT, HG])
        ri0 = keep("row_inverse0", [TT, HG])

        with ExitStack() as s:
            ug0h = place(s, "ug0_high", [4, 1024], F32R)
            ug0l = place(s, "ug0_low", [4, 1024], F32R)
            dn0h = place(s, "down0_high", [2, 1024], F32R)
            dn0l = place(s, "down0_low", [2, 1024], F32R)
            end_a = nc.sbuf_base
        with ExitStack() as s:
            place(s, "below_tree", [4096], F32)
            tree = place(s, "down_tree", [2, NI, C], F32)
        with ExitStack() as s:
            qraw = place(s, "qkv_rows", [2, TT, GV], F32)
            rot1 = place(s, "rope_cos_part", [TT, GW], F32)
            rot2 = place(s, "rope_sin_part", [TT, GW], F32)
            qn = place(s, "squares_then_roped", [TT, GW], F32)
            qhl = place(s, "q_rows_high_low", [TT, REP, 2, HD1], F32R)
            khl = place(s, "k_rows_high_low", [TT, 2, 2, HD1], F32R)
            end_b = nc.sbuf_base
        hold_a = keep("place_a", [(max(end_a, end_b) - nc.sbuf_base + 3) // 4])
        with ExitStack() as s:
            wt = place(s, "weights_t", [2, HG, W0_COLS], F32)
            sel = place(s, "selectors", [2, 1024], F32R)
            end_a = nc.sbuf_base
        with ExitStack() as s:
            qkvh = place(s, "qkv_high", [KV, KB * GV], F32R)
            qkvl = place(s, "qkv_low", [KV, KB * GV], F32R)
            end_b = nc.sbuf_base
        with ExitStack() as s:
            ug1h = place(s, "ug1_high", [4, 1024], F32R)
            ug1l = place(s, "ug1_low", [4, 1024], F32R)
            dn1h = place(s, "down1_high", [2, 1024], F32R)
            dn1l = place(s, "down1_low", [2, 1024], F32R)
            end_c = nc.sbuf_base
        hold_b = keep("place_b", [(max(end_a, end_b, end_c) - nc.sbuf_base + 3) // 4])
        base_c = nc.sbuf_base
        with ExitStack() as s:
            w0h = place(s, "w0_high", [2, KB, 512], F32R)
            w0l = place(s, "w0_low", [2, KB, 512], F32R)
            qkh = place(s, "qk0_high", [2, KB, T], F32R)
            qkl = place(s, "qk0_low", [2, KB, T], F32R)
            stk = place(s, "qk0_stacks", [2, 2, 2, T], F32R)
            vaug = place(s, "v0_and_ones", [TT, H0, 32], F32)
            osb = place(s, "out0_t", [T], F32)
            an = place(s, "out0_rows", [TT, C], F32)
            prep_at = (nc.sbuf_base - base_c) // 4
            ath = place(s, "out0_t_high", [KB, T], F32R)
            atl = place(s, "out0_t_low", [KB, T], F32R)
            dtmp = place(s, "down_scaled", [512], F32)
        with ExitStack() as s:
            place(s, "below_prep", [prep_at], F32)
            ph = place(s, "prep_high", [1024], F32R)
            pl = place(s, "prep_low", [1024], F32R)
        with ExitStack() as s:
            sg = place(s, "silu_gate", [2, T], F32)
            hf = place(s, "hidden", [2, T], F32)
            hh = place(s, "hidden_high", [3, T], F32R)
            hl = place(s, "hidden_low", [3, T], F32R)
        with ExitStack() as s:
            qst = place(s, "q_stack", [2, NQ, P], F32R)
            kst = place(s, "k_stack", [2, T], F32R)
            v1 = place(s, "v1_rows", [3, 2, TT, HD1], F32)
            pr = place(s, "probs", [4, 4, P], F32)
            prt = place(s, "probs_t", [4, 512], F32)
            ah = place(s, "out1_t_high", [2, T], F32R)
            al = place(s, "out1_t_low", [2, T], F32R)
            woh = place(s, "wout_high", [3, 2, C], F32R)
            wol = place(s, "wout_low", [3, 2, C], F32R)
            cos5 = place(s, "cos_weighted", [TT, GW], F32)
            sin5 = place(s, "sin_weighted", [TT, GW], F32)
            ctab = place(s, "cos_sin_table", [2, TT, HD1], F32)
            nw = place(s, "norm_weights", [2, GW], F32)
            ssq = place(s, "square_sums", [TT * (REP + 1)], F32)
            rr = place(s, "rms_inverse", [TT * (REP + 1)], F32)
            negm = place(s, "minus_max", [4, 4], F32)
            mx = place(s, "row_max", [4, 4], F32)
            psum1 = place(s, "prob_sums", [4, 4], F32)
            pinv = place(s, "prob_inverse", [4, 4], F32)

        ps = ctx.enter_context(nc.psum_tensor("psum", [P, 8, 512], F32))

        full = [sem(f"bank{i}_full") for i in range(8)]
        emptied_ = [sem(f"bank{i}_emptied") for i in range(8)]
        ch_in = [sem(f"chunk_in{i}") for i in range(2)]
        ch_hi = sem("chunk_high")
        ch_lo = {"dve": sem("chunk_low_dve"), "pool": sem("chunk_low_pool")}
        consts_in = sem("consts_in")
        rows_in = sem("x_rows_in")
        tree_in = sem("tree_in")
        tables_in = sem("tables_in")
        stored = sem("rows_stored")
        bias_set = sem("bias_set")
        vaug_zero = sem("v0_zeroed")
        vaug_set = sem("v0_ones_set")
        half_set = sem("minus_half_set")
        vlink = sem("dve_own_order")
        plink = sem("pool_own_order")
        ln_var = sem("ln_var_ready")
        ln_rstd = sem("ln_rstd_ready")
        xn_done = sem("x_rows_ready")
        hi_done = sem("high_of_bank")
        w_mask = sem("weights0_masked")
        tree_done = sem("tree_done")
        prep_hi = sem("tree_high_done")
        dn_scaled = sem("down0_scaled")
        dn_hi = sem("down0_high_done")
        dn_lo = sem("down0_low_done")
        hh_done, hl_done = sem("hidden_high_done"), sem("hidden_low_done")
        tabs_done = sem("rope_tables_done")
        sq_done, ss_done, rr_done = sem("squares_done"), sem("square_sums_done"), sem("rms_inverse_done")
        sin_done = sem("sin_part_done")
        qn_done = sem("roped_done")
        rows_hi, rows_lo = sem("qk_rows_high"), sem("qk_rows_low")
        v1_done = sem("v1_done")
        mx_done, pr_done = sem("minus_max_done"), sem("probs_done")

        job = {}
        fills = [0] * 8
        ring_at = [0]

        def chunk_wait(eng, key):
            k = CHUNK_NO[key]
            kind, low = CHUNKS[k][2:]
            if kind == "split":
                eng.wait_ge(ch_hi, counted(k, lambda c: c[2] == "split"))
            eng.wait_ge(ch_lo[low], counted(k, lambda c: c[3] == low))

        def emptied(eng, *keys):
            for key in keys:
                bank, n = job[key]
                eng.wait_ge(emptied_[bank], n + 1)

        hi_no = {}

        block = ctx.enter_context(nc.Block())

        @block.tensor
        def _(pe):
            def claim(key, bank=None):
                if bank is None:
                    bank = ring_at[0] % RING
                    ring_at[0] += 1
                job[key] = (bank, fills[bank])
                if fills[bank]:
                    pe.wait_ge(emptied_[bank], fills[bank])
                fills[bank] += 1
                return ps[:, bank, :], full[bank]

            def three(o, a, b_, first, last, **kw):
                (ah_, al_), (bh_, bl_) = a, b_
                nc.tensor.matmul(o, ah_, bh_, start=first, stop=False, **kw)
                nc.tensor.matmul(o, ah_, bl_, start=False, stop=False, **kw)
                return nc.tensor.matmul(o, al_, bh_, start=False, stop=last, **kw)

            def x_ready(layer, b):
                if layer == 0:
                    chunk_wait(pe, ("x", b))
                else:
                    emptied(pe, *[("xt", layer, b, kb) for kb in range(KB)])

            def qk0(b):
                x_ready(0, b)
                chunk_wait(pe, ("w0", 0))
                for z in range(2):
                    for m in range(KB):
                        o, done = claim(("qk0", b, z, m))
                        for kb in range(KB):
                            at = z * C + m * P
                            mm = three(o, (w0h[:, 0, kb, at:at + P], w0l[:, 0, kb, at:at + P]),
                                       (xh[:, b, kb, :], xl[:, b, kb, :]), kb == 0, kb == KB - 1)
                        mm.then_inc(done, 1)

            def v0(b):
                chunk_wait(pe, ("w0", 1))
                for half_ in range(2):
                    o, done = claim(("v0", b, half_))
                    for t2 in range(2):
                        t = 2 * half_ + t2
                        for kb in range(KB):
                            mm = three(o[:, t2 * C:(t2 + 1) * C],
                                       (xh[:, b, kb, t * P:(t + 1) * P], xl[:, b, kb, t * P:(t + 1) * P]),
                                       (w0h[:, 1, kb, 0:C], w0l[:, 1, kb, 0:C]), kb == 0, kb == KB - 1)
                    mm.then_inc(done, 1)

            def stack0(b, hg):
                chunk_wait(pe, ("sel", 1))
                for z in range(2):
                    emptied(pe, ("qk0", b, z, hg // 2))
                    for j2 in range(2):
                        j = (2 * hg + j2) % 4
                        o, done = claim(("stack0", b, hg, z, j2))
                        sv = sel[:].rearrange("p z (j l m) -> p z j l m", j=4, l=2)
                        nc.tensor.matmul(o, sv[:, z, j, 0, :], qkh[:, z, hg // 2, :], start=True, stop=False)
                        nc.tensor.matmul(o, sv[:, z, j, 1, :], qkl[:, z, hg // 2, :], start=False,
                                         stop=True).then_inc(done, 1)

            def scores0(b, hg):
                emptied(pe, *[("stack0", b, hg, z, j2) for z in range(2) for j2 in range(2)])
                for part in range(3):
                    for h4 in range(HG):
                        o, done = claim(("scores0", b, hg, part, h4))
                        r = slice(64 * (h4 % 2), 64 * (h4 % 2) + 64)
                        at = 0
                        for kb in ([0], [1], [2, 3])[part]:
                            w = T - kb * P
                            mm = nc.tensor.matmul(o[:, at:at + w], stk[r, hg % 2, 1, h4 // 2, kb * P:(kb + 1) * P],
                                                  stk[r, hg % 2, 0, h4 // 2, kb * P:T], start=True, stop=True)
                            at += w
                        mm.then_inc(done, 1)

            def pv0(b, hg):
                n = b * NHG + hg
                o, done = claim(("pv0", b, hg), 6)
                emptied(pe, ("v0", b, 0), ("v0", b, 1))
                pe.wait_ge(vaug_set, 1)
                for kb in range(TT):
                    pe.wait_ge(w_mask, TT * n + kb + 1)
                    for h4 in range(HG):
                        w = T - kb * P
                        mm = nc.tensor.matmul(o[32 * h4:32 * h4 + 32, kb * P:T], vaug[:, kb, HG * hg + h4, :],
                                              wt[:, hg % 2, h4, W0_AT[kb]:W0_AT[kb] + w],
                                              start=kb == 0, stop=kb == TT - 1)
                mm.then_inc(done, 1)

            def turn0(b, hg):
                emptied(pe, ("pv0", b, hg))
                o, done = claim(("turn0", b, hg), 7)
                for t in range(TT):
                    mm = nc.tensor.transpose(o[:, t * P:(t + 1) * P], osb[:, t * P:(t + 1) * P], ident[:])
                mm.then_inc(done, 1)

            def at0(b):
                emptied(pe, *[("turn0", b, hg) for hg in range(NHG)])
                for kb in range(KB):
                    o, done = claim(("at0", b, kb))
                    for t in range(TT):
                        mm = nc.tensor.transpose(o[:, t * P:(t + 1) * P], an[:, t, kb * P:(kb + 1) * P], ident[:])
                    mm.then_inc(done, 1)

            def wo0(b):
                emptied(pe, *[("at0", b, kb) for kb in range(KB)])
                for half_ in range(2):
                    o, done = claim(("y", 0, b, half_))
                    for t2 in range(2):
                        t = 2 * half_ + t2
                        for kb in range(KB):
                            mm = three(o[:, t2 * C:(t2 + 1) * C],
                                       (ath[:, kb, t * P:(t + 1) * P], atl[:, kb, t * P:(t + 1) * P]),
                                       (w0h[:, 1, kb, C:2 * C], w0l[:, 1, kb, C:2 * C]), kb == 0, kb == KB - 1)
                    mm.then_inc(done, 1)

            def xt(layer, b):
                pe.wait_ge(xn_done, (layer - 1) * B + b + 1)
                for kb in range(KB):
                    o, done = claim(("xt", layer, b, kb))
                    for t in range(TT):
                        mm = nc.tensor.transpose(o[:, t * P:(t + 1) * P], xn[:, b * TT + t, kb * P:(kb + 1) * P],
                                                 ident[:])
                    mm.then_inc(done, 1)

            def prep_ug(c):
                chunk_wait(pe, ("ug0", c))
                for m in range(KB):
                    o, done = claim(("prep_ug", c, m))
                    for kb in range(KB):
                        hm = had[:, 1 if (m and kb) else 0, :]
                        nc.tensor.matmul(o, hm, ph[:, kb * 512:(kb + 1) * 512], start=kb == 0, stop=False)
                        mm = nc.tensor.matmul(o, hm, pl[:, kb * 512:(kb + 1) * 512], start=False, stop=kb == 1)
                    mm.then_inc(done, 1)

            def prep_down(c):
                chunk_wait(pe, ("had", 0))
                pe.wait_ge(prep_hi, 1 + c)
                pe.wait_ge(ch_lo["pool"], counted(CHUNK_NO[("down0", c)], lambda x: x[3] == "pool"))
                for m in range(2):
                    o, done = claim(("prep_down", c, m))
                    nc.tensor.matmul(o, had[:, 0, :], ph[:, m * 512:(m + 1) * 512], start=True, stop=False)
                    nc.tensor.matmul(o, had[:, 0, :], pl[:, m * 512:(m + 1) * 512], start=False,
                                     stop=True).then_inc(done, 1)

            acc = {}

            def ffn(layer, b, i):
                wh, wl, dh, dl = (ug0h, ug0l, dn0h, dn0l) if layer == 0 else (ug1h, ug1l, dn1h, dn1l)
                if i < NI:
                    if i == 0:
                        x_ready(1 + 2 * layer, b)
                    if layer == 0:
                        emptied(pe, *[("prep_ug", i // 2, m) for m in range(KB)])
                    else:
                        chunk_wait(pe, ("ug1", i // 2))
                    for u in (1, 0):
                        o, done = claim(("ffn", layer, b, i, u))
                        for kb in range(KB):
                            at = kb * 512 + (i % 2) * 256 + u * P
                            mm = three(o, (wh[:, i // 2, at:at + P], wl[:, i // 2, at:at + P]),
                                       (xh[:, b, kb, :], xl[:, b, kb, :]), kb == 0, kb == KB - 1)
                        mm.then_inc(done, 1)
                if i >= 1:
                    i -= 1
                    n = (layer * B + b) * NI + i
                    if i == 0:
                        for half_ in range(2):
                            acc[half_] = claim(("y", 1 + 2 * layer, b, half_), 6 + half_)
                    if layer == 0:
                        pe.wait_ge(dn_lo, i // 2 + 1)
                    else:
                        chunk_wait(pe, ("down1", i // 4))
                    pe.wait_ge(hl_done, n + 1)
                    for t in range(TT):
                        o, done = acc[t // 2]
                        at = (i % 4) * C
                        mm = three(o[:, (t % 2) * C:(t % 2) * C + C],
                                   (hh[:, n % 3, t * P:(t + 1) * P], hl[:, n % 3, t * P:(t + 1) * P]),
                                   (dh[:, i // 4, at:at + C], dl[:, i // 4, at:at + C]),
                                   i == 0 and t % 2 == 0, i == NI - 1, skip_group_check=True)
                        if i == NI - 1 and t % 2:
                            mm.then_inc(done, 1)

            def proj1(k):
                b, g = divmod(k, KV)
                if g == 0:
                    x_ready(2, b)
                chunk_wait(pe, ("qkv", g))
                for t in range(TT):
                    o, done = claim(("proj1", k, t))
                    for kb in range(KB):
                        mm = three(o[:, 0:GV], (xh[:, b, kb, t * P:(t + 1) * P], xl[:, b, kb, t * P:(t + 1) * P]),
                                   (qkvh[:, g, kb * GV:(kb + 1) * GV], qkvl[:, g, kb * GV:(kb + 1) * GV]),
                                   kb == 0, kb == KB - 1)
                    mm.then_inc(done, 1)

            def turn1(k):
                pe.wait_ge(rows_hi, k + 1)
                pe.wait_ge(rows_lo, k + 1)
                for t in range(TT):
                    o, done = claim(("turn1q", k, t))
                    ov = o.rearrange("p (hp qb h w) -> p hp qb h w", hp=2, qb=2, h=2)
                    for h in range(REP):
                        mm = nc.tensor.transpose(ov[:, h // 2, :, h % 2, :],
                                                 qhl[:, t, h, :, :].rearrange("p a d -> p (a d)").bitcast(F32),
                                                 ident[:])
                    mm.then_inc(done, 1)
                for t2 in range(2):
                    o, done = claim(("turn1k", k, t2))
                    for z in range(2):
                        for t in range(2):
                            mm = nc.tensor.transpose(
                                o[:, z * 256 + t * P:z * 256 + (t + 1) * P],
                                khl[:, 2 * t2 + t, z, :, :].rearrange("p a d -> p (a d)").bitcast(F32), ident[:])
                    mm.then_inc(done, 1)

            def scores1(k):
                chunk_wait(pe, ("msk", 0))
                for c in range(4):
                    o, done = claim(("scores1", k, c))
                    emptied(pe, ("turn1q", k, c), ("turn1k", k, c // 2))
                    nc.tensor.matmul(o, eye2[0:64, :], wmask[0:64, 0 if c == 0 else 1, :], start=True, stop=False,
                                     skip_group_check=True)
                    for q2 in range(2):
                        qb = 2 * c + q2
                        k0 = max(0, (qb - 1) * WIN)
                        k1 = (qb + 1) * WIN
                        for hp in range(2):
                            at = (2 * q2 + hp) * P + P - (k1 - k0)
                            for z in range(2):
                                mm = nc.tensor.matmul(o[:, at:at + k1 - k0], qst[:, hp, qb, :], kst[:, z, k0:k1],
                                                      start=False, stop=z == 1, skip_group_check=True)
                    mm.then_inc(done, 1)

            def pv1(k):
                for c in range(4):
                    pe.wait_ge(pr_done, 4 * k + c + 1)
                    o, done = claim(("turn1p", k, c))
                    for q in range(4):
                        mm = nc.tensor.transpose(o[:, q * P:(q + 1) * P], pr[:, c, q, :], ident[:])
                    mm.then_inc(done, 1)
                pe.wait_ge(v1_done, k + 1)
                for half_ in range(2):
                    o, done = claim(("pv1", k, half_))
                    emptied(pe, ("turn1p", k, 2 * half_), ("turn1p", k, 2 * half_ + 1))
                    for c2 in range(2):
                        pv = prt[:, 2 * half_ + c2, :].rearrange("p (qb hp h w) -> p qb hp h w", qb=2, hp=2, h=2)
                        for q2 in range(2):
                            for h2 in range(2):
                                at = (2 * c2 + q2) * P
                                mm = nc.tensor.matmul(o[64 * h2:64 * h2 + 64, at:at + P],
                                                      v1[:, k % 3, 1 - q2, 2 * half_ + c2, :],
                                                      pv[:, q2, :, h2, :], start=True, stop=True)
                    mm.then_inc(done, 1)

            acc1 = {}

            def out1(k):
                b, g = divmod(k, KV)
                if g == 0:
                    for half_ in range(2):
                        acc1[half_] = claim(("y", 2, b, half_), 6 + half_)
                chunk_wait(pe, ("wout", k))
                emptied(pe, ("pv1", k, 0), ("pv1", k, 1))
                for t in range(TT):
                    o, done = acc1[t // 2]
                    for hp in range(2):
                        mm = three(o[:, (t % 2) * C:(t % 2) * C + C],
                                   (ah[:, hp, t * P:(t + 1) * P], al[:, hp, t * P:(t + 1) * P]),
                                   (woh[:, k % 3, hp, :], wol[:, k % 3, hp, :]),
                                   g == 0 and hp == 0 and t % 2 == 0, g == KV - 1 and hp == 1,
                                   skip_group_check=True)
                    if g == KV - 1 and t % 2:
                        mm.then_inc(done, 1)

            do = dict(qk0=qk0, v0=v0, stack0=stack0, scores0=scores0, pv0=pv0, turn0=turn0, at0=at0, wo0=wo0, xt=xt,
                      prep_ug=prep_ug, prep_down=prep_down, ffn=ffn, proj1=proj1, turn1=turn1, scores1=scores1,
                      pv1=pv1, out1=out1)
            pe.wait_ge(consts_in, 16 * 6)
            for step, *args in STEPS:
                if step in do:
                    do[step](*args)

        def take(eng, key):
            bank, n = job[key]
            eng.wait_ge(full[bank], n + 1)
            return ps[:, bank, :], emptied_[bank]

        def filled(eng, key):
            bank, n = job[key]
            eng.wait_ge(full[bank], n + 1)

        def raw_chunk(eng, k):
            n = LOADS.index(k)
            eng.wait_ge(ch_in[n % 2], 16 * (n // 2 + 1))
            return raw[:, n % 2, 0:CHUNK_COLS[CHUNKS[k][0]]]

        def chunk_target(name, c):
            if name == "x":
                return [a[:, c].rearrange("p k t -> p (k t)") for a in (xh, xl)]
            if name == "w0":
                return [a[:, c].rearrange("p k t -> p (k t)") for a in (w0h, w0l)]
            if name in ("ug0", "down0"):
                return [ph[:], pl[:]]
            if name == "wout":
                return [a[:, c % 3].rearrange("p k t -> p (k t)") for a in (woh, wol)]
            return [a[:, c, :] for a in {"qkv": (qkvh, qkvl), "ug1": (ug1h, ug1l), "down1": (dn1h, dn1l)}[name]]

        @block.sync
        def _(sp):
            def load_chunk(n):
                k = LOADS[n]
                name, c = CHUNKS[k][:2]
                if n >= 2:
                    chunk_wait(sp, CHUNKS[LOADS[n - 2]][:2])
                sp.dma_start(raw[:, n % 2, 0:CHUNK_COLS[name]],
                             dram[name][:, c % KV if name == "wout" else c, :]).then_inc(ch_in[n % 2], 16)

            load_chunk(0)
            load_chunk(1)
            for tile, name in ((ident, "identity"), (tri, "causal"), (sign_ug, "sign_ug"), (sign_dp, "sign_dp"),
                               (scale_ug, "scale_ug"), (scale_dp, "scale_dp")):
                sp.dma_start(tile[:], dram[name]).then_inc(consts_in, 16)
            load_chunk(2)
            sp.dma_start(tree[:, 0].rearrange("p a b -> p (a b)"),
                         dram["down0"].rearrange("p c n -> p (c n)")).then_inc(tree_in, 16)
            sp.dma_start(xn[:], dram["x_rows"]).then_inc(rows_in, 16)
            for n in range(3, len(LOADS)):
                if CHUNKS[LOADS[n]][0] == "msk":
                    filled(sp, ("y", 0, B - 1, 1))
                    sp.dma_start(ctab[:], dram["cos_sin"]).then_inc(tables_in, 16)
                    sp.dma_start(nw[:], dram["norm_w"]).then_inc(tables_in, 16)
                load_chunk(n)
            for b in range(B):
                sp.wait_ge(xn_done, 3 * B + b + 1)
                sp.dma_start(out[:, b * TT:(b + 1) * TT, :], xn[:, b * TT:(b + 1) * TT, :]).then_inc(stored, 16)
            sp.wait_ge(stored, 16 * B)

        @block.scalar
        def _(act):
            def high(key, dst, **scale):
                o, _ = take(act, key)
                hi_no[key] = len(hi_no) + 1
                if scale:
                    nc.scalar.activation(dst, o, ACT.Copy, **scale).then_inc(hi_done, 1)
                else:
                    nc.scalar.copy(dst, o).then_inc(hi_done, 1)

            def chunk(key):
                k = CHUNK_NO[key]
                name, c, kind, low = CHUNKS[k]
                if kind == "split":
                    nc.scalar.copy(chunk_target(name, c)[0], raw_chunk(act, k)).then_inc(ch_hi, 1)
                elif kind == "tree":
                    act.wait_ge(tree_done, 1)
                    nc.scalar.copy(ph[:], tree[:, 1, 4 * c:4 * c + 4, :].rearrange("p a b -> p (a b)")).then_inc(
                        prep_hi, 1)

            def qk0(b):
                for z in range(2):
                    for m in range(KB):
                        high(("qk0", b, z, m), qkh[:, z, m, :])

            def v0(b):
                act.wait_ge(vaug_zero, 1)
                for half_ in range(2):
                    o, done = take(act, ("v0", b, half_))
                    nc.scalar.copy(vaug[:, 2 * half_:2 * half_ + 2, :, 0:HD0],
                                   o.rearrange("p (t h d) -> p t h d", t=2, h=H0)).then_inc(done, 1)

            def stack0(b, hg):
                for j2 in range(2):
                    o, done = take(act, ("stack0", b, hg, 0, j2))
                    nc.scalar.copy(stk[:, hg % 2, 0, j2, :], o).then_inc(done, 1)

            def scores0(b, hg):
                act.wait_ge(bias_set, 1)
                for part in range(3):
                    at, w = [(0, 512), (512, 384), (896, 384)][part]
                    for h4 in (0, 2):
                        o, done = take(act, ("scores0", b, hg, part, h4))
                        nc.scalar.activation(wt[:, hg % 2, h4, at:at + w], o[:, 0:w], ACT.Relu,
                                             bias=bias0[:]).then_inc(done, 1)

            def pv0(b, hg):
                o, done = take(act, ("pv0", b, hg))
                n = b * NHG + hg
                if n:
                    filled(act, ("turn0",) + divmod(n - 1, NHG))
                nc.scalar.copy(osb[:], o).then_inc(done, 1)

            def at0(b):
                for kb in range(KB):
                    high(("at0", b, kb), ath[:, kb, :])

            def xt(layer, b):
                for kb in range(KB):
                    high(("xt", layer, b, kb), xh[:, b, kb, :])

            def prep_ug(c):
                for m in range(KB):
                    high(("prep_ug", c, m), ug0h[:, c, m * 512:(m + 1) * 512], scale=sign_ug[:, m:m + 1])

            def prep_down(c):
                for m in range(2):
                    act.wait_ge(dn_scaled, 2 * c + m + 1)
                    nc.scalar.copy(dn0h[:, c, m * 512:(m + 1) * 512], dtmp[:]).then_inc(dn_hi, 1)

            def ffn(layer, b, i):
                if i == NI:
                    return
                n = (layer * B + b) * NI + i
                o, done = take(act, ("ffn", layer, b, i, 1))
                if i >= 2:
                    emptied(act, ("ffn", layer, b, i - 2, 0))
                kw = dict(scale=scale_ug[:, NI + i:NI + i + 1]) if layer == 0 else {}
                nc.scalar.activation(sg[:, i % 2, :], o, ACT.Silu, **kw).then_inc(done, 1)
                emptied(act, ("ffn", layer, b, i, 0))
                nc.scalar.copy(hh[:, n % 3, :], hf[:, n % 2, :]).then_inc(hh_done, 1)

            def proj1(k):
                if k >= 2:
                    act.wait_ge(qn_done, k - 1)
                for t in range(TT):
                    o, done = take(act, ("proj1", k, t))
                    nc.scalar.copy(qraw[:, k % 2, t, :], o[:, 0:GV]).then_inc(done, 1)

            def turn1(k):
                for t in (0, 2):
                    o, done = take(act, ("turn1q", k, t))
                    nc.scalar.copy(qst[:, :, 2 * t:2 * t + 2, :],
                                   o.rearrange("p (hp q w) -> p hp q w", hp=2, q=2)).then_inc(done, 1)
                o, done = take(act, ("turn1k", k, 0))
                nc.scalar.copy(kst[:, :, 0:256], o.rearrange("p (z t) -> p z t", z=2)).then_inc(done, 1)

            def scores1(k):
                for c in range(4):
                    o, done = take(act, ("scores1", k, c))
                    act.wait_ge(mx_done, 4 * k + c + 1)
                    for q in range(4):
                        e = nc.scalar.activation(pr[:, c, q, :], o[:, q * P:(q + 1) * P], ACT.Exp,
                                                 bias=negm[:, c, q:q + 1], scale=float(HD1) ** -0.5,
                                                 accum_out=psum1[:, c, q:q + 1])
                    e.then_inc(done, 1)

            def rope1(k):
                act.wait_ge(qn_done, k + 1)
                if k:
                    filled(act, ("turn1k", k - 1, 1))
                nc.scalar.copy(qhl[:, :, :, 0, :], qn[:, :, 0:REP * HD1].rearrange("p t (h d) -> p t h d", h=REP))
                nc.scalar.copy(khl[:, :, 0, :, :],
                               qn[:, :, REP * HD1:GW].rearrange("p t (a d) -> p t a d", a=1).to_broadcast(
                                   [P, TT, 2, HD1])).then_inc(rows_hi, 1)

            def pv1(k):
                for c in (0, 2):
                    o, done = take(act, ("turn1p", k, c))
                    nc.scalar.copy(prt[:, c, :], o).then_inc(done, 1)
                for half_ in range(2):
                    o, _ = take(act, ("pv1", k, half_))
                    hi_no[("pv1", k, half_)] = len(hi_no) + 1
                    nc.scalar.copy(ah[:, :, half_ * 256:(half_ + 1) * 256].rearrange("p hp (q w) -> p q hp w", q=4),
                                   o.rearrange("p (q hp w) -> p q hp w", q=4, hp=2)).then_inc(hi_done, 1)

            do = dict(chunk=chunk, qk0=qk0, v0=v0, stack0=stack0, scores0=scores0, pv0=pv0, at0=at0, xt=xt,
                      prep_ug=prep_ug, prep_down=prep_down, ffn=ffn, proj1=proj1, turn1=turn1, scores1=scores1,
                      rope1=rope1, pv1=pv1)
            act.wait_ge(consts_in, 16 * 6)
            for step, *args in STEPS:
                if step in do:
                    do[step](*args)

        @block.vector
        def _(dve):
            links = [0]

            def link(ins):
                links[0] += 1
                ins.then_inc(vlink, 1)
                dve.wait_ge(vlink, links[0])

            def low(key, dst, hi, o=None):
                o_, done = take(dve, key)
                dve.wait_ge(hi_done, hi_no[key])
                nc.vector.tensor_tensor(dst, o_ if o is None else o(o_), hi.bitcast(F32), ALU.subtract).then_inc(
                    done, 1)

            def chunk(key):
                k = CHUNK_NO[key]
                name, c, kind, lo = CHUNKS[k]
                if lo != "dve":
                    return
                r = raw_chunk(dve, k)
                if kind == "split":
                    dve.wait_ge(ch_hi, counted(k, lambda x: x[2] == "split"))
                    hi, dst = chunk_target(name, c)
                    last = nc.vector.tensor_tensor(dst, r, hi.bitcast(F32), ALU.subtract)
                elif name == "sel":
                    last = nc.vector.tensor_copy(sel[:, c, :], r)
                elif name == "had":
                    last = nc.vector.tensor_copy(had[:].rearrange("p a b -> p (a b)"), r)
                else:
                    nc.vector.tensor_copy(wmask[:].rearrange("p a b -> p (a b)"), r[:, 0:1024])
                    last = nc.vector.tensor_copy(eye2[:], r[:, 1024:1152])
                last.then_inc(ch_lo["dve"], 1)

            def qk0(b):
                for z in range(2):
                    for m in range(KB):
                        low(("qk0", b, z, m), qkl[:, z, m, :], qkh[:, z, m, :])

            def stack0(b, hg):
                for j2 in range(2):
                    o, done = take(dve, ("stack0", b, hg, 1, j2))
                    nc.vector.tensor_copy(stk[:, hg % 2, 1, j2, :], o).then_inc(done, 1)

            def scores0(b, hg):
                for part in range(3):
                    at, w = [(0, 512), (512, 384), (896, 384)][part]
                    for h4 in (1, 3):
                        o, done = take(dve, ("scores0", b, hg, part, h4))
                        nc.vector.tensor_scalar(wt[:, hg % 2, h4, at:at + w], o[:, 0:w], -ATTN_THRESHOLD, 0.0,
                                                ALU.add, ALU.max).then_inc(done, 1)

            def turn0(b, hg):
                o, done = take(dve, ("turn0", b, hg))
                ov = o.rearrange("p (t h w) -> p t h w", t=TT, h=HG)
                link(nc.vector.tensor_scalar(rs0[:], ov[:, :, :, HD0], ATTN_EPS, None, ALU.add))
                link(nc.vector.reciprocal(ri0[:], rs0[:]))
                nc.vector.tensor_tensor(
                    an[:, :, 64 * hg:64 * hg + 64].rearrange("p t (h d) -> p t h d", h=HG), ov[:, :, :, 0:HD0],
                    ri0[:].rearrange("p t (h a) -> p t h a", a=1).to_broadcast([P, TT, HG, HD0]),
                    ALU.mult).then_inc(done, 1)

            def at0(b):
                for kb in range(KB):
                    low(("at0", b, kb), atl[:, kb, :], ath[:, kb, :])

            def xt(layer, b):
                for kb in range(KB):
                    low(("xt", layer, b, kb), xl[:, b, kb, :], xh[:, b, kb, :])

            def ln(layer, b):
                if layer == 0:
                    dve.wait_ge(rows_in, 16)
                for half_ in range(2):
                    o, done = take(dve, ("y", layer, b, half_))
                    at = b * TT + 2 * half_
                    nc.vector.tensor_tensor(xn[:, at:at + 2, :], o.rearrange("p (t c) -> p t c", t=2),
                                            xn[:, at:at + 2, :], ALU.add).then_inc(done, 1)
                    emptied(dve, ("y", layer, b, half_))
                    nc.vector.bn_stats(stats[:, 2 * half_, :], xn[:, at, :])
                    link(nc.vector.bn_stats(stats[:, 2 * half_ + 1, :], xn[:, at + 1, :]))
                    for t in (2 * half_, 2 * half_ + 1):
                        last = nc.vector.bn_aggr(mv[:, t, :], stats[:, t, :])
                last.then_inc(ln_var, 1)
                dve.wait_ge(ln_var, layer * B + b + 1)
                dve.wait_ge(ln_rstd, layer * B + b + 1)
                for t in range(TT):
                    at = b * TT + t
                    last = nc.vector.tensor_scalar(xn[:, at, :], xn[:, at, :], mv[:, t, 0:1], rstd[:, t:t + 1],
                                                   ALU.subtract, ALU.mult)
                last.then_inc(xn_done, 1)

            def prep_ug(c):
                for m in range(KB):
                    key = ("prep_ug", c, m)
                    o, done = take(dve, key)
                    dve.wait_ge(hi_done, hi_no[key])
                    cols = slice(m * 512, (m + 1) * 512)
                    nc.vector.scalar_tensor_tensor(out=ug0l[:, c, cols], in0=o, scalar=sign_ug[:, m:m + 1],
                                                   in1=ug0h[:, c, cols].bitcast(F32), op0=ALU.mult,
                                                   op1=ALU.subtract).then_inc(done, 1)

            def prep_down(c):
                for m in range(2):
                    o, done = take(dve, ("prep_down", c, m))
                    if 2 * c + m:
                        dve.wait_ge(dn_lo, 2 * c + m)
                    for j in range(2):
                        i = 4 * c + 2 * m + j
                        last = nc.vector.scalar_tensor_tensor(
                            out=dtmp[:, j * C:(j + 1) * C], in0=o[:, j * C:(j + 1) * C], scalar=sign_dp[:, i:i + 1],
                            in1=scale_dp[:], op0=ALU.mult, op1=ALU.mult)
                    last.then_inc(done, 1)
                    emptied(dve, ("prep_down", c, m))
                    dve.sem_inc(dn_scaled, 1)

            def ffn(layer, b, i):
                if i == NI:
                    return
                n = (layer * B + b) * NI + i
                o, done = take(dve, ("ffn", layer, b, i, 0))
                emptied(dve, ("ffn", layer, b, i, 1))
                if n >= 2:
                    dve.wait_ge(hl_done, n - 1)
                sc = scale_ug[:, i:i + 1] if layer == 0 else 1.0
                nc.vector.scalar_tensor_tensor(out=hf[:, n % 2, :], in0=o, scalar=sc, in1=sg[:, i % 2, :],
                                               op0=ALU.mult, op1=ALU.mult).then_inc(done, 1)

            def rope_tables():
                dve.wait_ge(tables_in, 32)
                for z, tab in enumerate((cos5, sin5)):
                    for t in range(TT):
                        last = nc.vector.tensor_tensor(
                            tab[:, t, :].rearrange("p (h d) -> p h d", h=REP + 1),
                            nw[:, z, :].rearrange("p (h d) -> p h d", h=REP + 1),
                            ctab[:, z, t, :].rearrange("p (a d) -> p a d", a=1).to_broadcast([P, REP + 1, HD1]),
                            ALU.mult)
                last.then_inc(tabs_done, 1)

            def rms1(k):
                s3 = k % 3
                for t in range(TT):
                    emptied(dve, ("proj1", k, t))
                if k == 0:
                    dve.wait_ge(tabs_done, 1)
                if k < 3:
                    nc.vector.memset(v1[0:HD1, s3, 1, 0, :], 0.0)
                r = qraw[:, k % 2]
                nc.vector.tensor_copy(v1[:, s3, 0, :, :], r[:, :, GW:GV])
                nc.vector.tensor_copy(v1[0:64, s3, 1, 1:TT, :], r[64:128, 0:TT - 1, GW:GV])
                nc.vector.tensor_copy(v1[64:128, s3, 1, :, :], r[0:64, :, GW:GV]).then_inc(v1_done, 1)
                nc.vector.tensor_tensor(rot1[:], r[:, :, 0:GW], cos5[:], ALU.mult)
                dve.wait_ge(sq_done, k + 1)
                nc.vector.tensor_reduce(ssq[:].rearrange("p (t h) -> p t h", t=TT),
                                        qn[:].rearrange("p t (h d) -> p t h d", d=HD1), AX.X, ALU.add).then_inc(
                                            ss_done, 1)

            def rope1(k):
                dve.wait_ge(sin_done, k + 1)
                dve.wait_ge(ss_done, k + 1)
                link(nc.vector.tensor_tensor(rot1[:], rot1[:], rot2[:], ALU.add))
                dve.wait_ge(rr_done, k + 1)
                nc.vector.tensor_tensor(
                    qn[:].rearrange("p t (h d) -> p t h d", d=HD1), rot1[:].rearrange("p t (h d) -> p t h d", d=HD1),
                    rr[:].rearrange("p (t h a) -> p t h a", t=TT, a=1).to_broadcast([P, TT, REP + 1, HD1]),
                    ALU.mult).then_inc(qn_done, 1)

            def turn1(k):
                for t in (1, 3):
                    o, done = take(dve, ("turn1q", k, t))
                    nc.vector.tensor_copy(qst[:, :, 2 * t:2 * t + 2, :],
                                          o.rearrange("p (hp q w) -> p hp q w", hp=2, q=2)).then_inc(done, 1)
                o, done = take(dve, ("turn1k", k, 1))
                nc.vector.tensor_copy(kst[:, :, 256:512], o.rearrange("p (z t) -> p z t", z=2)).then_inc(done, 1)

            def probs(k, c):
                emptied(dve, ("scores1", k, c))
                link(nc.vector.reciprocal(pinv[:, c, :], psum1[:, c, :]))
                nc.vector.tensor_tensor(pr[:, c], pr[:, c],
                                        pinv[:, c, :].rearrange("p (q a) -> p q a", a=1).to_broadcast([P, 4, P]),
                                        ALU.mult).then_inc(pr_done, 1)

            def scores1(k):
                for c in range(4):
                    o, done = take(dve, ("scores1", k, c))
                    link(nc.vector.tensor_reduce(mx[:, c, :], o.rearrange("p (q w) -> p q w", q=4), AX.X, ALU.max))
                    nc.vector.tensor_scalar(negm[:, c, :], mx[:, c, :], -float(HD1) ** -0.5, None,
                                            ALU.mult).then_inc(mx_done, 1)
                    if c:
                        probs(k, c - 1)
                probs(k, 3)

            def pv1(k):
                for c in (1, 3):
                    o, done = take(dve, ("turn1p", k, c))
                    nc.vector.tensor_copy(prt[:, c, :], o).then_inc(done, 1)
                for half_ in range(2):
                    cols = slice(half_ * 256, (half_ + 1) * 256)
                    low(("pv1", k, half_), al[:, :, cols].rearrange("p hp (q w) -> p q hp w", q=4),
                        ah[:, :, cols].rearrange("p hp (q w) -> p q hp w", q=4),
                        lambda o: o.rearrange("p (q hp w) -> p q hp w", q=4, hp=2))

            do = dict(chunk=chunk, qk0=qk0, stack0=stack0, scores0=scores0, turn0=turn0, at0=at0, xt=xt, ln=ln,
                      prep_ug=prep_ug, prep_down=prep_down, ffn=ffn, rope_tables=rope_tables, rms1=rms1,
                      rope1=rope1, turn1=turn1, scores1=scores1, pv1=pv1)
            nc.vector.memset(bias0[:], -ATTN_THRESHOLD).then_inc(bias_set, 1)
            nc.vector.memset(vaug[:], 0.0).then_inc(vaug_zero, 1)
            dve.wait_ge(vaug_zero, 1)
            nc.vector.memset(vaug[:, :, :, HD0:HD0 + 1], 1.0).then_inc(vaug_set, 1)
            dve.wait_ge(consts_in, 16 * 6)
            link(nc.vector.tensor_scalar(scale_ug[:], scale_ug[:], float(C) ** -0.5, None, ALU.mult))
            link(nc.vector.tensor_scalar(scale_dp[:], scale_dp[:], float(INTER) ** -0.5, None, ALU.mult))
            for step, *args in STEPS:
                if step in do:
                    do[step](*args)

        @block.gpsimd
        def _(pool):
            links = [0]

            def link(ins):
                links[0] += 1
                ins.then_inc(plink, 1)
                pool.wait_ge(plink, links[0])

            def tree_step():
                pool.wait_ge(tree_in, 16)
                for n, st in enumerate((4, 2, 1)):
                    a = tree[:, n % 2].rearrange("p (g z s) c -> p g z (s c)", z=2, s=st)
                    o = tree[:, 1 - n % 2].rearrange("p (g z s) c -> p g z (s c)", z=2, s=st)
                    nc.gpsimd.tensor_tensor(o[:, :, 0, :], a[:, :, 0, :], a[:, :, 1, :], ALU.add)
                    last = nc.gpsimd.tensor_tensor(o[:, :, 1, :], a[:, :, 0, :], a[:, :, 1, :], ALU.subtract)
                    if st > 1:
                        link(last)
                last.then_inc(tree_done, 1)

            def chunk(key):
                k = CHUNK_NO[key]
                name, c, kind, lo = CHUNKS[k]
                if lo != "pool":
                    return
                hi, dst = chunk_target(name, c)
                if kind == "tree":
                    pool.wait_ge(tree_done, 1)
                    pool.wait_ge(prep_hi, c + 1)
                    r = tree[:, 1, 4 * c:4 * c + 4, :].rearrange("p a b -> p (a b)")
                else:
                    r = raw_chunk(pool, k)
                    pool.wait_ge(ch_hi, counted(k, lambda x: x[2] == "split"))
                nc.gpsimd.tensor_tensor(dst, r, hi.bitcast(F32), ALU.subtract).then_inc(ch_lo["pool"], 1)

            def scores0(b, hg):
                n = b * NHG + hg
                for kb in range(TT):
                    if kb < 3:
                        emptied(pool, *[("scores0", b, hg, kb, h4) for h4 in range(HG)])
                    w = wt[:, hg % 2, :, W0_AT[kb]:W0_AT[kb] + P]
                    nc.gpsimd.tensor_tensor(
                        w, w, tri[:].rearrange("p (a q) -> p a q", a=1).to_broadcast([P, HG, P]),
                        ALU.mult).then_inc(w_mask, 1)

            def prep_down(c):
                for m in range(2):
                    cols = slice(m * 512, (m + 1) * 512)
                    pool.wait_ge(dn_hi, 2 * c + m + 1)
                    nc.gpsimd.tensor_tensor(dn0l[:, c, cols], dtmp[:], dn0h[:, c, cols].bitcast(F32),
                                            ALU.subtract).then_inc(dn_lo, 1)

            def ffn(layer, b, i):
                if i == NI:
                    return
                n = (layer * B + b) * NI + i
                pool.wait_ge(hh_done, n + 1)
                nc.gpsimd.tensor_tensor(hl[:, n % 3, :], hf[:, n % 2, :], hh[:, n % 3, :].bitcast(F32),
                                        ALU.subtract).then_inc(hl_done, 1)

            def ln(layer, b):
                pool.wait_ge(ln_var, layer * B + b + 1)
                link(nc.gpsimd.tensor_scalar(var_eps[:], mv[:, :, 1], LN_EPS, None, ALU.add))
                nc.gpsimd.tensor_tensor(rstd[:], var_eps[:], half[:, 0:TT], ALU.pow).then_inc(ln_rstd, 1)

            def rms1(k):
                r = qraw[:, k % 2]
                for t in range(TT):
                    emptied(pool, ("proj1", k, t))
                if k:
                    pool.wait_ge(rows_hi, k)
                    pool.wait_ge(rows_lo, k)
                nc.gpsimd.tensor_tensor(qn[:], r[:, :, 0:GW], r[:, :, 0:GW], ALU.mult).then_inc(sq_done, 1)
                if k:
                    pool.wait_ge(qn_done, k)
                else:
                    pool.wait_ge(tabs_done, 1)
                rv = r[:, :, 0:GW].rearrange("p t (h z d) -> p t h z d", h=REP + 1, z=2)
                sv = sin5[:].rearrange("p t (h z d) -> p t h z d", h=REP + 1, z=2)
                ov = rot2[:].rearrange("p t (h z d) -> p t h z d", h=REP + 1, z=2)
                for z in range(2):
                    last = nc.gpsimd.tensor_tensor(ov[:, :, :, z, :], rv[:, :, :, 1 - z, :], sv[:, :, :, z, :],
                                                   ALU.mult)
                last.then_inc(sin_done, 1)
                pool.wait_ge(ss_done, k + 1)
                link(nc.gpsimd.tensor_scalar(rr[:], ssq[:], 1.0 / HD1, RMS_EPS, ALU.mult, ALU.add))
                nc.gpsimd.tensor_tensor(rr[:], rr[:], half[:], ALU.pow).then_inc(rr_done, 1)

            def rope1(k):
                pool.wait_ge(rows_hi, k + 1)
                nc.gpsimd.tensor_tensor(qhl[:, :, :, 1, :],
                                        qn[:, :, 0:REP * HD1].rearrange("p t (h d) -> p t h d", h=REP),
                                        qhl[:, :, :, 0, :].bitcast(F32), ALU.subtract)
                nc.gpsimd.tensor_tensor(khl[:, :, 1, :, :],
                                        qn[:, :, REP * HD1:GW].rearrange("p t (a d) -> p t a d", a=1).to_broadcast(
                                            [P, TT, 2, HD1]),
                                        khl[:, :, 0, :, :].bitcast(F32), ALU.subtract).then_inc(rows_lo, 1)

            do = dict(tree=tree_step, chunk=chunk, scores0=scores0, prep_down=prep_down, ffn=ffn, ln=ln, rms1=rms1,
                      rope1=rope1)
            nc.gpsimd.memset(half[:], -0.5).then_inc(half_set, 1)
            pool.wait_ge(half_set, 1)
            pool.wait_ge(consts_in, 16 * 6)
            for step, *args in STEPS:
                if step in do:
                    do[step](*args)


def constants():
    f = np.float32
    p = np.arange(P)
    had = np.array([[(-1.0) ** bin(i & j).count("1") for j in range(P)] for i in range(P)], f)
    sel = np.zeros((P, 2, 4, 2, P), f)
    for j in range(4):
        for par in range(2):
            for copy in range(4):
                for i in range(HD0):
                    row, col = HD0 * (2 * j + par) + i, 64 * par + HD0 * copy + i
                    sel[row, 0, j, copy % 2, col] = 1.0
                    sel[row, 1, j, copy // 2, col] = float(HD0) ** -0.5
    q, j = np.arange(WIN)[:, None], np.arange(P)[None, :]
    near = (j > q) & (j <= q + WIN)
    plain = np.where(near, 0.0, MASKED).astype(f)
    first = np.where(near & (j >= WIN), 0.0, MASKED).astype(f)
    msk = np.zeros((P, 1, 1152), f)
    msk[:WIN, 0, :1024] = np.concatenate([first, first] + [plain] * 6, axis=1)
    msk[:WIN, 0, 1024:] = np.concatenate([np.eye(WIN, dtype=f)] * 2, axis=1)
    inv = (f(1.0) / f(10000.0) ** (np.arange(0, HD1, 2, dtype=f) / f(HD1))).astype(f)
    ang = np.arange(T, dtype=f)[:, None] * inv[None, :]
    emb = np.concatenate([ang, ang], axis=-1)
    sign = np.where(np.arange(HD1) < HD1 // 2, f(-1.0), f(1.0))
    tab = np.stack([np.cos(emb), np.sin(emb) * sign])
    return {
        "identity": np.eye(P, dtype=f),
        "causal": (p[None, :] >= p[:, None]).astype(f),
        "had": np.concatenate([had, -had], axis=1).reshape(P, 1, 2 * P),
        "sel": sel.reshape(P, 2, 1024),
        "msk": msk,
        "cos_sin": np.ascontiguousarray(tab.reshape(2, TT, P, HD1).transpose(2, 0, 1, 3)).astype(f),
    }


def kernel(L0_attn_x, L0_attn_Wq, L0_attn_Wk, L0_attn_Wv, L0_attn_Wo, L0_ffn_SU_ug, L0_ffn_SU_dp, L0_ffn_Wscale_ug,
           L0_ffn_Wscale_dp, L0_ffn_W_up, L0_ffn_W_gate, L0_ffn_W_down, L1_attn_w_qkv, L1_attn_w_out,
           L1_attn_q_norm_w, L1_attn_k_norm_w, L1_ffn_w_gate, L1_ffn_w_up, L1_ffn_w_down):
    import concourse.bacc as bacc
    from concourse.bass_utils import run_bass_kernel_spmd

    a = np.asarray

    def k_rows(w):
        w = a(w).T
        return w.reshape(w.shape[0] // P, P, w.shape[1]).transpose(1, 0, 2)

    def up_gate(up, gate):
        w = np.stack([k_rows(up), k_rows(gate)], axis=2)
        w = w.reshape(P, KB, 2, 4, 2, P).transpose(0, 3, 1, 4, 2, 5)
        return w.reshape(P, 4, 1024)

    nq, nk = KV * REP * HD1, KV * HD1
    qkv = k_rows(L1_attn_w_qkv)
    qkv = np.concatenate([qkv[:, :, :nq].reshape(P, KB, KV, REP * HD1),
                          qkv[:, :, nq:nq + nk].reshape(P, KB, KV, HD1),
                          qkv[:, :, nq + nk:].reshape(P, KB, KV, HD1)], axis=3)
    w0 = np.stack([np.concatenate([k_rows(L0_attn_Wq), k_rows(L0_attn_Wk)], axis=2),
                   np.concatenate([k_rows(L0_attn_Wv), k_rows(L0_attn_Wo)], axis=2)], axis=1)
    qw, kw = a(L1_attn_q_norm_w), a(L1_attn_k_norm_w)
    qr, kr = np.roll(qw, HD1 // 2), np.roll(kw, HD1 // 2)
    norm_w = np.stack([np.concatenate([qw] * REP + [kw]), np.concatenate([qr] * REP + [kr])])
    x = a(L0_attn_x)
    arrays = dict(constants())
    arrays.update({
        "x": x.reshape(B, T, KB, P).transpose(3, 0, 2, 1).reshape(P, B, KB * T),
        "w0": w0.reshape(P, 2, 1024),
        "ug0": up_gate(L0_ffn_W_up, L0_ffn_W_gate),
        "down0": k_rows(L0_ffn_W_down).reshape(P, 2, 1024),
        "qkv": qkv.transpose(0, 2, 1, 3).reshape(P, KV, KB * GV),
        "wout": k_rows(L1_attn_w_out).reshape(P, KV, 512),
        "ug1": up_gate(L1_ffn_w_up, L1_ffn_w_gate),
        "down1": k_rows(L1_ffn_w_down).reshape(P, 2, 1024),
        "sign_ug": a(L0_ffn_SU_ug).reshape(KB, P).T,
        "sign_dp": a(L0_ffn_SU_dp).reshape(NI, P).T,
        "scale_ug": a(L0_ffn_Wscale_ug).reshape(2 * NI, P).T,
        "scale_dp": np.broadcast_to(a(L0_ffn_Wscale_dp), (P, C)),
        "norm_w": np.broadcast_to(norm_w, (P, 2, GW)),
        "x_rows": x.reshape(B * TT, P, C).transpose(1, 0, 2),
    })
    nc = bacc.Bacc("TRN2", target_bir_lowering=False, num_devices=1)
    feed, dram = {}, {}
    for name, v in arrays.items():
        v = np.ascontiguousarray(v)
        feed["in_" + name] = v
        dram[name] = nc.dram_tensor("in_" + name, v.shape, mybir.dt.from_np(v.dtype), kind="ExternalInput").ap()
    out = nc.dram_tensor("out", (B, T, C), F32, kind="ExternalOutput").ap()
    post_ln_two_layers(nc, dram, out.rearrange("b (t p) c -> p (b t) c", p=P))
    r = run_bass_kernel_spmd(nc, [feed], core_ids=[0])
    return r.results[0]["out"]
```

```python
from contextlib import ExitStack

import numpy as np

import concourse.bass as bass
from concourse import mybir

ALU = mybir.AluOpType
ACT = mybir.ActivationFunctionType
AX = mybir.AxisListType
F32 = mybir.dt.float32
F32R = mybir.dt.float32r
BF16 = mybir.dt.bfloat16

P = 128
B, T, C = 2, 512, 256
KB = C // P
TT = T // P
LN_EPS = 1e-5
H0, HD0 = 16, 16
HG = 4
NHG = H0 // HG
ATTN_THRESHOLD, ATTN_EPS = -0.1, 1e-6
W0_AT = [0, 512, 896, 1152]
W0_COLS = 1280
INTER = 1024
NI = INTER // P
KV, REP, HD1 = 8, 4, 64
WIN = 64
NQ = T // WIN
GW = (REP + 1) * HD1
GV = GW + HD1
RMS_EPS = 1e-6
MASKED = -1e30
NIT = B * KV
SLOTS = 3
FLAG = 2
RING = 6

CHUNKS = ([("x", 0, "split", "dve"), ("w0", 0, "split", "dve"), ("sel", 0, "copy", "dve"),
           ("sel", 1, "copy", "dve"), ("w0", 1, "split", "dve"), ("x", 1, "split", "dve"),
           ("had", 0, "copy", "dve"), ("down0", 0, "tree", "dve"), ("down0", 1, "tree", "dve")]
          + [("ug0", c, "pair", "dve") for c in range(4)]
          + [("msk", 0, "copy", "dve"), ("eye", 0, "copy", "dve")]
          + [("qkv", g, "split", "pool") for g in range(KV)]
          + [("wout", i, "split", "pool") for i in range(NIT)]
          + [("ug1", c, "split", "pool") for c in range(4)]
          + [("down1", c, "split", "pool") for c in range(2)])
LOADS = [k for k, ch in enumerate(CHUNKS) if ch[2] != "tree"]
CHUNK_NO = {(name, c): k for k, (name, c, _, _) in enumerate(CHUNKS)}
CHUNK_COLS = {"x": 1024, "w0": 1024, "sel": 1024, "had": P, "down0": 1024, "ug0": 1024, "msk": 1024, "eye": P,
              "qkv": KB * GV, "wout": 512, "ug1": 1024, "down1": 1024}


def counted(k, wanted):
    return sum(1 for ch in CHUNKS[:k + 1] if wanted(ch))


def program_steps():
    s = [("chunk", ("x", 0)), ("chunk", ("w0", 0)), ("qk0", 0), ("chunk", ("sel", 0)), ("chunk", ("sel", 1)),
         ("stack0", 0, 0), ("chunk", ("w0", 1)), ("v0", 0), ("tree",), ("chunk", ("x", 1)), ("chunk", ("had", 0))]
    for n in range(B * NHG + 2):
        if n < B * NHG:
            s.append(("scores0",) + divmod(n, NHG))
        if n + 1 < B * NHG:
            if n + 1 == NHG:
                s.append(("qk0", 1))
            s.append(("stack0",) + divmod(n + 1, NHG))
        if 1 <= n <= 2:
            s += [("chunk", ("down0", n - 1)), ("prep_down", n - 1)]
        if 3 <= n <= 4:
            for c in (2 * n - 6, 2 * n - 5):
                s += [("chunk", ("ug0", c)), ("prep_ug", c)]
        if 1 <= n <= B * NHG:
            s.append(("pv0",) + divmod(n - 1, NHG))
        if n == NHG:
            s.append(("v0", 1))
        if n >= 2:
            s.append(("turn0",) + divmod(n - 2, NHG))
        if n == NHG + 1:
            s.append(("at0", 0))
        if n == NHG + 2:
            s += [("wo0", 0), ("ln", 0, 0)]
        if n == B * NHG - 1:
            s.append(("xt", 1, 0))
    s += [("at0", 1), ("ffn", 0, 0), ("wo0", 1), ("ln", 0, 1), ("ffn", 0, 1), ("chunk", ("msk", 0)), ("chunk", ("eye", 0)),
          ("rope_tables",)]
    for n in range(2, B * NI + 2):
        s.append(("ffn", 0, n))
        if n == 3:
            s.append(("xt", 1, 1))
        if 4 <= n < 4 + KV:
            s.append(("chunk", ("qkv", n - 4)))
        if n == NI + 1:
            s.append(("ln", 1, 0))
        if n == NI + 3:
            s.append(("xt", 2, 0))
    s.append(("ln", 1, 1))
    for k in range(NIT + 3):
        s.append(("attn1", k))
        if k == 0:
            s.append(("xt", 2, 1))
        if k >= 3 and (k - 3) % KV == KV - 1:
            s.append(("ln", 2, (k - 3) // KV))
            if k < NIT:
                s.append(("xt", 3, 0))
        if k == NIT + 1:
            s += [("chunk", ("ug1", c)) for c in range(4)]
        if k == NIT + 2:
            s += [("chunk", ("down1", c)) for c in range(2)]
    for n in range(B * NI + 2):
        s.append(("ffn", 1, n))
        if n == 2:
            s.append(("xt", 3, 1))
        if n == NI + 1:
            s.append(("ln", 3, 0))
    s.append(("ln", 3, 1))
    return s


STEPS = program_steps()


def post_ln_two_layers(nc, dram, out):
    with ExitStack() as ctx:
        def sem(name):
            return ctx.enter_context(nc.semaphore(name))

        def place(scope, name, shape, dt):
            return scope.enter_context(nc.sbuf_tensor(name, [P] + shape, dt))

        def keep(name, shape, dt=F32):
            return place(ctx, name, shape, dt)

        xh = keep("x_t_high", [B, KB, T], F32R)
        xl = keep("x_t_low", [B, KB, T], F32R)
        with ExitStack() as s:
            place(s, "below_work", [TT * C], F32)
            dtmp = place(s, "down_scaled", [512], F32)
        with ExitStack() as s:
            place(s, "below_pair", [TT * C], F32)
            pair = place(s, "ug0_sum_difference", [1024], F32)
        xn = keep("x_rows", [B * TT, C])
        raw = keep("raw_chunks", [SLOTS, 1024])
        ident = keep("identity", [P])
        identr = keep("identity_r", [P], F32R)
        had = keep("hadamard", [P], F32R)
        tri = keep("causal_block", [P])
        eye2 = keep("eye_twice", [P], BF16)
        wmask = keep("window_mask", [2, 512], BF16)
        sign_ug = keep("sign_ug", [KB])
        sign_dp = keep("sign_dp", [NI])
        scale_ug = keep("scale_ug", [2 * NI])
        scale_dp = keep("scale_dp", [C])
        bias0 = keep("bias_threshold", [1])
        half = keep("minus_half", [REP * (REP + 1)])
        stats = keep("ln_stats", [TT, 6])
        mv = keep("ln_mean_var", [TT, 2])
        var_eps = keep("ln_var_eps", [TT])
        rstd = keep("ln_rstd", [TT])
        rs0 = keep("row_sums0", [TT, HG])
        ri0 = keep("row_inverse0", [TT, HG])

        with ExitStack() as s:
            ug0h = place(s, "ug0_high", [4, 1024], F32R)
            ug0l = place(s, "ug0_low", [4, 1024], F32R)
            dn0h = place(s, "down0_high", [2, 1024], F32R)
            dn0l = place(s, "down0_low", [2, 1024], F32R)
            end_a = nc.sbuf_base
        with ExitStack() as s:
            place(s, "below_tree", [4096], F32)
            tree = place(s, "down_tree", [2, NI, C], F32)
        with ExitStack() as s:
            qraw = place(s, "qkv_rows", [2, TT, GV], F32)
            rot1 = place(s, "rope_cos_part", [TT, GW], F32)
            rot2 = place(s, "rope_sin_part", [TT, GW], F32)
            qn = place(s, "roped", [TT, GW], F32)
            sq = place(s, "squares", [TT, GW], F32)
            qhl = place(s, "q_rows_high_low", [TT, REP, 2, HD1], F32R)
            khl = place(s, "k_rows_high_low", [TT, 2, 2, HD1], F32R)
            end_b = nc.sbuf_base
        hold_a = keep("place_a", [(max(end_a, end_b) - nc.sbuf_base + 3) // 4])
        with ExitStack() as s:
            wt = place(s, "weights_t", [2, HG, W0_COLS], F32)
            sel = place(s, "selectors", [2, 1024], F32R)
            end_a = nc.sbuf_base
        with ExitStack() as s:
            qkvh = place(s, "qkv_high", [KV, KB * GV], F32R)
            qkvl = place(s, "qkv_low", [KV, KB * GV], F32R)
            end_b = nc.sbuf_base
        with ExitStack() as s:
            ug1h = place(s, "ug1_high", [4, 1024], F32R)
            ug1l = place(s, "ug1_low", [4, 1024], F32R)
            dn1h = place(s, "down1_high", [2, 1024], F32R)
            dn1l = place(s, "down1_low", [2, 1024], F32R)
            end_c = nc.sbuf_base
        hold_b = keep("place_b", [(max(end_a, end_b, end_c) - nc.sbuf_base + 3) // 4])
        base_c = nc.sbuf_base
        with ExitStack() as s:
            w0h = place(s, "w0_high", [2, KB, 512], F32R)
            w0l = place(s, "w0_low", [2, KB, 512], F32R)
            qkh = place(s, "qk0_high", [2, KB, T], F32R)
            qkl = place(s, "qk0_low", [2, KB, T], F32R)
            stk = place(s, "qk0_stacks", [2, 2, 2, T], F32R)
            vaug = place(s, "v0_and_ones", [TT, H0, 32], F32)
            osb = place(s, "out0_t", [T], F32)
            an = place(s, "out0_rows", [TT, C], F32)
            prep_at = (nc.sbuf_base - base_c) // 4
            ath = place(s, "out0_t_high", [KB, T], F32R)
            atl = place(s, "out0_t_low", [KB, T], F32R)
        with ExitStack() as s:
            place(s, "below_prep", [prep_at], F32)
            ph = place(s, "prep_high", [1024], F32R)
            pl = place(s, "prep_low", [1024], F32R)
        with ExitStack() as s:
            place(s, "below_ffn", [4096], F32)
            sg = place(s, "silu_gate", [2, T], F32)
            hf = place(s, "hidden", [2, T], F32)
            hh = place(s, "hidden_high", [3, T], F32R)
            hl = place(s, "hidden_low", [3, T], F32R)
        with ExitStack() as s:
            qst = place(s, "q_stack", [2, NQ, P], F32R)
            kst = place(s, "k_stack", [2, T], F32R)
            v1 = place(s, "v1_rows", [3, 2, TT, HD1], F32)
            pr = place(s, "probs", [4, 4, P], F32)
            prt = place(s, "probs_t", [4, 512], F32)
            ah = place(s, "out1_t_high", [2, T], F32R)
            al = place(s, "out1_t_low", [2, T], F32R)
            woh = place(s, "wout_high", [2, 2, C], F32R)
            wol = place(s, "wout_low", [2, 2, C], F32R)
            cos5 = place(s, "cos_weighted", [TT, GW], F32)
            sin5 = place(s, "sin_weighted", [TT, GW], F32)
            ctab = place(s, "cos_sin_table", [2, TT, HD1], F32)
            nw = place(s, "norm_weights", [2, GW], F32)
            ssq = place(s, "square_sums", [TT * (REP + 1)], F32)
            rr = place(s, "rms_inverse", [TT * (REP + 1)], F32)
            negm = place(s, "minus_max", [4, 4], F32)
            mx = place(s, "row_max", [4, 4], F32)
            psum1 = place(s, "prob_sums", [4, 4], F32)
            pinv = place(s, "prob_inverse", [4, 4], F32)

        ps = ctx.enter_context(nc.psum_tensor("psum", [P, 8, 512], F32))

        full = [sem(f"bank{i}_full") for i in range(8)]
        emptied_ = [sem(f"bank{i}_emptied") for i in range(8)]
        ch_in = [sem(f"chunk_in{i}") for i in range(SLOTS)]
        ch_hi = sem("chunk_high")
        ch_lo = {"dve": sem("chunk_low_dve"), "pool": sem("chunk_low_pool")}
        const_in = {name: sem("in_" + name) for name in
                    ("identity", "causal", "sign_ug", "sign_dp", "scale_ug", "scale_dp")}
        identr_set = sem("identity_r_set")
        scales_set = sem("scales_set")
        pair_done = sem("ug0_pair_done")
        rows_in = [sem(f"x_rows_in{b}") for b in range(B)]
        tree_in = sem("tree_in")
        tables_in = sem("tables_in")
        stored = sem("rows_stored")
        bias_set = sem("bias_set")
        vaug_zero = sem("v0_zeroed")
        vaug_set = sem("v0_ones_set")
        half_set = sem("minus_half_set")
        vlink = sem("dve_own_order")
        plink = sem("pool_own_order")
        ln_var = sem("ln_var_ready")
        ln_rstd = sem("ln_rstd_ready")
        xn_done = sem("x_rows_ready")
        hi_done = sem("high_of_bank")
        w_mask = sem("weights0_masked")
        tree_done = sem("tree_done")
        dn_hi = sem("down0_high_done")
        dn_lo = sem("down0_low_done")
        hh_done, hl_done = sem("hidden_high_done"), sem("hidden_low_done")
        tabs_done = sem("rope_tables_done")
        sq_done, ss_done, rr_done = sem("squares_done"), sem("square_sums_done"), sem("rms_inverse_done")
        sin_done, cos_done, rope_sum = sem("sin_part_done"), sem("cos_part_done"), sem("rope_sum_done")
        qn_done = sem("roped_done")
        rows_hi, rows_lo = sem("qk_rows_high"), sem("qk_rows_low")
        v1_done = sem("v1_done")
        mx_done, pr_done = sem("minus_max_done"), sem("probs_done")

        job = {}
        fills = [0] * 8
        ring_at = [0]

        def chunk_wait(eng, key):
            k = CHUNK_NO[key]
            kind, low = CHUNKS[k][2:]
            if kind != "copy":
                eng.wait_ge(ch_hi, counted(k, lambda c: c[2] != "copy"))
            eng.wait_ge(ch_lo[low], counted(k, lambda c: c[3] == low))

        def emptied(eng, *keys):
            for key in keys:
                bank, n = job[key]
                eng.wait_ge(emptied_[bank], n + 1)

        hi_no = {}

        block = ctx.enter_context(nc.Block())

        @block.tensor
        def _(pe):
            def claim(key, bank=None):
                if bank is None:
                    bank = ring_at[0] % RING
                    ring_at[0] += 1
                job[key] = (bank, fills[bank])
                if fills[bank]:
                    pe.wait_ge(emptied_[bank], fills[bank])
                fills[bank] += 1
                return ps[:, bank, :], full[bank]

            def three(o, a, b_, first, last, **kw):
                (ah_, al_), (bh_, bl_) = a, b_
                nc.tensor.matmul(o, ah_, bh_, start=first, stop=False, **kw)
                nc.tensor.matmul(o, ah_, bl_, start=False, stop=False, **kw)
                return nc.tensor.matmul(o, al_, bh_, start=False, stop=last, **kw)

            def x_ready(layer, b):
                if layer == 0:
                    chunk_wait(pe, ("x", b))
                else:
                    emptied(pe, *[("xt", layer, b, kb) for kb in range(KB)])

            def qk0(b):
                x_ready(0, b)
                chunk_wait(pe, ("w0", 0))
                for z in range(2):
                    for m in range(KB):
                        o, done = claim(("qk0", b, z, m))
                        for kb in range(KB):
                            at = z * C + m * P
                            mm = three(o, (w0h[:, 0, kb, at:at + P], w0l[:, 0, kb, at:at + P]),
                                       (xh[:, b, kb, :], xl[:, b, kb, :]), kb == 0, kb == KB - 1)
                        mm.then_inc(done, 1)

            def v0(b):
                chunk_wait(pe, ("w0", 1))
                for half_ in range(2):
                    o, done = claim(("v0", b, half_))
                    for t2 in range(2):
                        t = 2 * half_ + t2
                        for kb in range(KB):
                            mm = three(o[:, t2 * C:(t2 + 1) * C],
                                       (xh[:, b, kb, t * P:(t + 1) * P], xl[:, b, kb, t * P:(t + 1) * P]),
                                       (w0h[:, 1, kb, 0:C], w0l[:, 1, kb, 0:C]), kb == 0, kb == KB - 1)
                    mm.then_inc(done, 1)

            def stack0(b, hg):
                chunk_wait(pe, ("sel", 1))
                for z in range(2):
                    emptied(pe, ("qk0", b, z, hg // 2))
                    for j2 in range(2):
                        j = (2 * hg + j2) % 4
                        o, done = claim(("stack0", b, hg, z, j2))
                        sv = sel[:].rearrange("p z (j l m) -> p z j l m", j=4, l=2)
                        nc.tensor.matmul(o, sv[:, z, j, 0, :], qkh[:, z, hg // 2, :], start=True, stop=False)
                        nc.tensor.matmul(o, sv[:, z, j, 1, :], qkl[:, z, hg // 2, :], start=False,
                                         stop=True).then_inc(done, 1)

            def scores0(b, hg):
                emptied(pe, *[("stack0", b, hg, z, j2) for z in range(2) for j2 in range(2)])
                for part in range(3):
                    for h4 in range(HG):
                        o, done = claim(("scores0", b, hg, part, h4))
                        r = slice(64 * (h4 % 2), 64 * (h4 % 2) + 64)
                        at = 0
                        for kb in ([0], [1], [2, 3])[part]:
                            w = T - kb * P
                            mm = nc.tensor.matmul(o[:, at:at + w], stk[r, hg % 2, 1, h4 // 2, kb * P:(kb + 1) * P],
                                                  stk[r, hg % 2, 0, h4 // 2, kb * P:T], start=True, stop=True)
                            at += w
                        mm.then_inc(done, 1)

            def pv0(b, hg):
                n = b * NHG + hg
                o, done = claim(("pv0", b, hg), 6)
                emptied(pe, ("v0", b, 0), ("v0", b, 1))
                pe.wait_ge(vaug_set, 1)
                for kb in range(TT):
                    pe.wait_ge(w_mask, TT * n + kb + 1)
                    for h4 in range(HG):
                        w = T - kb * P
                        mm = nc.tensor.matmul(o[32 * h4:32 * h4 + 32, kb * P:T], vaug[:, kb, HG * hg + h4, :],
                                              wt[:, hg % 2, h4, W0_AT[kb]:W0_AT[kb] + w],
                                              start=kb == 0, stop=kb == TT - 1)
                mm.then_inc(done, 1)

            def turn0(b, hg):
                emptied(pe, ("pv0", b, hg))
                pe.wait_ge(const_in["identity"], 16)
                o, done = claim(("turn0", b, hg), 7)
                for t in range(TT):
                    mm = nc.tensor.transpose(o[:, t * P:(t + 1) * P], osb[:, t * P:(t + 1) * P], ident[:])
                mm.then_inc(done, 1)

            def at0(b):
                emptied(pe, *[("turn0", b, hg) for hg in range(NHG)])
                for kb in range(KB):
                    o, done = claim(("at0", b, kb))
                    for t in range(TT):
                        mm = nc.tensor.transpose(o[:, t * P:(t + 1) * P], an[:, t, kb * P:(kb + 1) * P], ident[:])
                    mm.then_inc(done, 1)

            def wo0(b):
                emptied(pe, *[("at0", b, kb) for kb in range(KB)])
                for half_ in range(2):
                    o, done = claim(("y", 0, b, half_))
                    for t2 in range(2):
                        t = 2 * half_ + t2
                        for kb in range(KB):
                            mm = three(o[:, t2 * C:(t2 + 1) * C],
                                       (ath[:, kb, t * P:(t + 1) * P], atl[:, kb, t * P:(t + 1) * P]),
                                       (w0h[:, 1, kb, C:2 * C], w0l[:, 1, kb, C:2 * C]), kb == 0, kb == KB - 1)
                    mm.then_inc(done, 1)

            def xt(layer, b):
                pe.wait_ge(xn_done, (layer - 1) * B + b + 1)
                for kb in range(KB):
                    o, done = claim(("xt", layer, b, kb))
                    for t in range(TT):
                        mm = nc.tensor.transpose(o[:, t * P:(t + 1) * P], xn[:, b * TT + t, kb * P:(kb + 1) * P],
                                                 ident[:])
                    mm.then_inc(done, 1)

            def prep_ug(c):
                chunk_wait(pe, ("ug0", c))
                for m in range(KB):
                    o, done = claim(("prep_ug", c, m))
                    nc.tensor.matmul(o, had[:], ph[:, m * 512:(m + 1) * 512], start=True, stop=False)
                    nc.tensor.matmul(o, had[:], pl[:, m * 512:(m + 1) * 512], start=False, stop=True).then_inc(done, 1)

            def prep_down(c):
                chunk_wait(pe, ("had", 0))
                chunk_wait(pe, ("down0", c))
                for m in range(2):
                    o, done = claim(("prep_down", c, m))
                    nc.tensor.matmul(o, had[:], ph[:, m * 512:(m + 1) * 512], start=True, stop=False)
                    nc.tensor.matmul(o, had[:], pl[:, m * 512:(m + 1) * 512], start=False,
                                     stop=True).then_inc(done, 1)

            acc = {}

            def ffn(layer, n):
                wh, wl, dh, dl = (ug0h, ug0l, dn0h, dn0l) if layer == 0 else (ug1h, ug1l, dn1h, dn1l)
                if n < B * NI:
                    b, i = divmod(n, NI)
                    if i == 0:
                        x_ready(1 + 2 * layer, b)
                    if layer == 0:
                        emptied(pe, *[("prep_ug", i // 2, m) for m in range(KB)])
                    else:
                        chunk_wait(pe, ("ug1", i // 2))
                    for u in (1, 0):
                        o, done = claim(("ffn", layer, n, u))
                        for kb in range(KB):
                            at = kb * 512 + (i % 2) * 256 + u * P
                            mm = three(o, (wh[:, i // 2, at:at + P], wl[:, i // 2, at:at + P]),
                                       (xh[:, b, kb, :], xl[:, b, kb, :]), kb == 0, kb == KB - 1)
                        mm.then_inc(done, 1)
                if n >= FLAG:
                    n -= FLAG
                    b, i = divmod(n, NI)
                    if i == 0:
                        for half_ in range(2):
                            acc[half_] = claim(("y", 1 + 2 * layer, b, half_), 6 + half_)
                    if layer == 0:
                        pe.wait_ge(dn_lo, i // 2 + 1)
                    else:
                        chunk_wait(pe, ("down1", i // 4))
                    pe.wait_ge(hl_done, layer * B * NI + n + 1)
                    for t in range(TT):
                        o, done = acc[t // 2]
                        at = (i % 4) * C
                        mm = three(o[:, (t % 2) * C:(t % 2) * C + C],
                                   (hh[:, n % 3, t * P:(t + 1) * P], hl[:, n % 3, t * P:(t + 1) * P]),
                                   (dh[:, i // 4, at:at + C], dl[:, i // 4, at:at + C]),
                                   i == 0 and t % 2 == 0, i == NI - 1, skip_group_check=True)
                        if i == NI - 1 and t % 2:
                            mm.then_inc(done, 1)

            def proj1(k, t):
                b, g = divmod(k, KV)
                if t == 0:
                    if g == 0:
                        x_ready(2, b)
                    chunk_wait(pe, ("qkv", g))
                o, done = claim(("proj1", k, t))
                for kb in range(KB):
                    mm = three(o[:, 0:GV], (xh[:, b, kb, t * P:(t + 1) * P], xl[:, b, kb, t * P:(t + 1) * P]),
                               (qkvh[:, g, kb * GV:(kb + 1) * GV], qkvl[:, g, kb * GV:(kb + 1) * GV]),
                               kb == 0, kb == KB - 1)
                mm.then_inc(done, 1)

            def turned(o, rows):
                return nc.tensor.matmul(o, rows.rearrange("p a d -> p (a d)"), identr[:], start=True, stop=True)

            def turn1(k):
                if k == 0:
                    pe.wait_ge(identr_set, 1)
                pe.wait_ge(rows_hi, k + 1)
                pe.wait_ge(rows_lo, k + 1)
                for t in range(TT):
                    o, done = claim(("turn1q", k, t))
                    for h in range(REP):
                        mm = turned(o[:, h * P:(h + 1) * P], qhl[:, t, h, :, :])
                    mm.then_inc(done, 1)
                for t2 in range(2):
                    o, done = claim(("turn1k", k, t2))
                    for z in range(2):
                        for t in range(2):
                            mm = turned(o[:, z * 256 + t * P:z * 256 + (t + 1) * P], khl[:, 2 * t2 + t, z, :, :])
                    mm.then_inc(done, 1)

            def scores1(k, c):
                chunk_wait(pe, ("eye", 0))
                o, done = claim(("scores1", k, c))
                emptied(pe, ("turn1q", k, c), ("turn1k", k, c // 2))
                if c == 2:
                    emptied(pe, ("turn1k", k, 0))
                nc.tensor.matmul(o, eye2[0:64, :], wmask[0:64, 0 if c == 0 else 1, :], start=True, stop=False,
                                 skip_group_check=True)
                for q2 in range(2):
                    qb = 2 * c + q2
                    k0 = max(0, (qb - 1) * WIN)
                    k1 = (qb + 1) * WIN
                    for hp in range(2):
                        at = (2 * q2 + hp) * P + P - (k1 - k0)
                        for z in range(2):
                            mm = nc.tensor.matmul(o[:, at:at + k1 - k0], qst[:, hp, qb, :], kst[:, z, k0:k1],
                                                  start=False, stop=z == 1, skip_group_check=True)
                mm.then_inc(done, 1)

            def turn_p(k):
                for c in range(4):
                    pe.wait_ge(pr_done, 4 * k + c + 1)
                    o, done = claim(("turn1p", k, c))
                    for q in range(4):
                        mm = nc.tensor.transpose(o[:, q * P:(q + 1) * P], pr[:, c, q, :], ident[:])
                    mm.then_inc(done, 1)

            def pv1(k):
                pe.wait_ge(v1_done, k + 1)
                for half_ in range(2):
                    o, done = claim(("pv1", k, half_))
                    emptied(pe, ("turn1p", k, 2 * half_), ("turn1p", k, 2 * half_ + 1))
                    for c2 in range(2):
                        pv = prt[:, 2 * half_ + c2, :].rearrange("p (qb hp h w) -> p qb hp h w", qb=2, hp=2, h=2)
                        for q2 in range(2):
                            for h2 in range(2):
                                at = (2 * c2 + q2) * P
                                mm = nc.tensor.matmul(o[64 * h2:64 * h2 + 64, at:at + P],
                                                      v1[:, k % 3, 1 - q2, 2 * half_ + c2, :],
                                                      pv[:, q2, :, h2, :], start=True, stop=True)
                    mm.then_inc(done, 1)

            acc1 = {}

            def out1(k):
                b, g = divmod(k, KV)
                if g == 0:
                    for half_ in range(2):
                        acc1[half_] = claim(("y", 2, b, half_), 6 + half_)
                chunk_wait(pe, ("wout", k))
                emptied(pe, ("pv1", k, 0), ("pv1", k, 1))
                for t in range(TT):
                    o, done = acc1[t // 2]
                    for hp in range(2):
                        mm = three(o[:, (t % 2) * C:(t % 2) * C + C],
                                   (ah[:, hp, t * P:(t + 1) * P], al[:, hp, t * P:(t + 1) * P]),
                                   (woh[:, k % 2, hp, :], wol[:, k % 2, hp, :]),
                                   g == 0 and hp == 0 and t % 2 == 0, g == KV - 1 and hp == 1,
                                   skip_group_check=True)
                    if g == KV - 1 and t % 2:
                        mm.then_inc(done, 1)

            def attn1(k):
                new, mid, old = k < NIT, 0 <= k - 2 < NIT, 0 <= k - 3 < NIT
                if mid:
                    turn1(k - 2)
                if old:
                    pv1(k - 3)
                if new:
                    proj1(k, 0)
                    proj1(k, 1)
                for j in range(4):
                    if mid:
                        scores1(k - 2, j)
                    if new and j < 2:
                        proj1(k, 2 + j)
                if old:
                    out1(k - 3)
                if mid:
                    turn_p(k - 2)

            do = dict(qk0=qk0, v0=v0, stack0=stack0, scores0=scores0, pv0=pv0, turn0=turn0, at0=at0, wo0=wo0, xt=xt,
                      prep_ug=prep_ug, prep_down=prep_down, ffn=ffn, attn1=attn1)
            for step, *args in STEPS:
                if step in do:
                    do[step](*args)

        def take(eng, key):
            bank, n = job[key]
            eng.wait_ge(full[bank], n + 1)
            return ps[:, bank, :], emptied_[bank]

        def filled(eng, key):
            bank, n = job[key]
            eng.wait_ge(full[bank], n + 1)

        def raw_chunk(eng, k):
            n = LOADS.index(k)
            eng.wait_ge(ch_in[n % SLOTS], 16 * (n // SLOTS + 1))
            return raw[:, n % SLOTS, 0:CHUNK_COLS[CHUNKS[k][0]]]

        def chunk_target(name, c):
            if name == "x":
                return [a[:, c].rearrange("p k t -> p (k t)") for a in (xh, xl)]
            if name == "w0":
                return [a[:, c].rearrange("p k t -> p (k t)") for a in (w0h, w0l)]
            if name in ("ug0", "down0"):
                return [ph[:], pl[:]]
            if name == "wout":
                return [a[:, c % 2].rearrange("p k t -> p (k t)") for a in (woh, wol)]
            return [a[:, c, :] for a in {"qkv": (qkvh, qkvl), "ug1": (ug1h, ug1l), "down1": (dn1h, dn1l)}[name]]

        def to_qst(o, t):
            dst = qst[:, :, 2 * t:2 * t + 2, :].rearrange("p hp q (h w) -> p hp h q w", h=2)
            return dst, o.rearrange("p (hp h q w) -> p hp h q w", hp=2, h=2, q=2)

        @block.sync
        def _(sp):
            def load_chunk(n):
                k = LOADS[n]
                name, c = CHUNKS[k][:2]
                if n >= SLOTS:
                    chunk_wait(sp, CHUNKS[LOADS[n - SLOTS]][:2])
                sp.dma_start(raw[:, n % SLOTS, 0:CHUNK_COLS[name]],
                             dram[name][:, c % KV if name == "wout" else c, :]).then_inc(ch_in[n % SLOTS], 16)

            def load_const(tile, name):
                sp.dma_start(tile[:], dram[name]).then_inc(const_in[name], 16)

            for n in range(SLOTS):
                load_chunk(n)
            load_const(tri, "causal")
            sp.dma_start(tree[:, 0].rearrange("p a b -> p (a b)"),
                         dram["down0"].rearrange("p c n -> p (c n)")).then_inc(tree_in, 16)
            load_chunk(SLOTS)
            for tile, name in ((ident, "identity"), (scale_dp, "scale_dp"), (sign_dp, "sign_dp"),
                               (scale_ug, "scale_ug"), (sign_ug, "sign_ug")):
                load_const(tile, name)
            load_chunk(SLOTS + 1)
            sp.dma_start(xn[:, 0:TT, :], dram["x_rows"][:, 0:TT, :]).then_inc(rows_in[0], 16)
            for n in range(SLOTS + 2, len(LOADS)):
                if CHUNKS[LOADS[n]][0] == "msk":
                    chunk_wait(sp, ("ug0", 3))
                    sp.dma_start(xn[:, TT:, :], dram["x_rows"][:, TT:, :]).then_inc(rows_in[1], 16)
                    filled(sp, ("y", 0, B - 1, 1))
                    sp.dma_start(ctab[:], dram["cos_sin"]).then_inc(tables_in, 16)
                    sp.dma_start(nw[:], dram["norm_w"]).then_inc(tables_in, 16)
                load_chunk(n)
            for b in range(B):
                sp.wait_ge(xn_done, 3 * B + b + 1)
                sp.dma_start(out[:, b * TT:(b + 1) * TT, :], xn[:, b * TT:(b + 1) * TT, :]).then_inc(stored, 16)
            sp.wait_ge(stored, 16 * B)

        @block.scalar
        def _(act):
            def high(key, dst, **scale):
                o, _ = take(act, key)
                hi_no[key] = len(hi_no) + 1
                if scale:
                    nc.scalar.activation(dst, o, ACT.Copy, **scale).then_inc(hi_done, 1)
                else:
                    nc.scalar.copy(dst, o).then_inc(hi_done, 1)

            def chunk(key):
                k = CHUNK_NO[key]
                name, c, kind, low = CHUNKS[k]
                if kind == "copy":
                    return
                if kind == "split":
                    src = raw_chunk(act, k)
                elif kind == "pair":
                    act.wait_ge(pair_done, c + 1)
                    src = pair[:]
                else:
                    act.wait_ge(tree_done, 1)
                    src = tree[:, 1, 4 * c:4 * c + 4, :].rearrange("p a b -> p (a b)")
                nc.scalar.copy(chunk_target(name, c)[0], src).then_inc(ch_hi, 1)

            def qk0(b):
                for z in range(2):
                    for m in range(KB):
                        high(("qk0", b, z, m), qkh[:, z, m, :])

            def v0(b):
                act.wait_ge(vaug_zero, 1)
                for half_ in range(2):
                    o, done = take(act, ("v0", b, half_))
                    nc.scalar.copy(vaug[:, 2 * half_:2 * half_ + 2, :, 0:HD0],
                                   o.rearrange("p (t h d) -> p t h d", t=2, h=H0)).then_inc(done, 1)

            def stack0(b, hg):
                for j2 in range(2):
                    o, done = take(act, ("stack0", b, hg, 0, j2))
                    nc.scalar.copy(stk[:, hg % 2, 0, j2, :], o).then_inc(done, 1)

            def scores0(b, hg):
                act.wait_ge(bias_set, 1)
                for part in range(3):
                    at, w = [(0, 512), (512, 384), (896, 384)][part]
                    for h4 in (0, 2):
                        o, done = take(act, ("scores0", b, hg, part, h4))
                        nc.scalar.activation(wt[:, hg % 2, h4, at:at + w], o[:, 0:w], ACT.Relu,
                                             bias=bias0[:]).then_inc(done, 1)

            def pv0(b, hg):
                o, done = take(act, ("pv0", b, hg))
                n = b * NHG + hg
                if n:
                    filled(act, ("turn0",) + divmod(n - 1, NHG))
                nc.scalar.copy(osb[:], o).then_inc(done, 1)

            def at0(b):
                for kb in range(KB):
                    high(("at0", b, kb), ath[:, kb, :])

            def xt(layer, b):
                for kb in range(KB):
                    high(("xt", layer, b, kb), xh[:, b, kb, :])

            def prep_ug(c):
                act.wait_ge(const_in["sign_ug"], 16)
                for m in range(KB):
                    high(("prep_ug", c, m), ug0h[:, c, m * 512:(m + 1) * 512], scale=sign_ug[:, m:m + 1])

            def prep_down(c):
                for m in range(2):
                    emptied(act, ("prep_down", c, m))
                    nc.scalar.copy(dn0h[:, c, m * 512:(m + 1) * 512], dtmp[:]).then_inc(dn_hi, 1)

            def ffn(layer, n):
                if n >= B * NI:
                    return
                i = n % NI
                o, done = take(act, ("ffn", layer, n, 1))
                if n >= 2:
                    emptied(act, ("ffn", layer, n - 2, 0))
                if layer == 0:
                    act.wait_ge(scales_set, 1)
                kw = dict(scale=scale_ug[:, NI + i:NI + i + 1]) if layer == 0 else {}
                nc.scalar.activation(sg[:, n % 2, :], o, ACT.Silu, **kw).then_inc(done, 1)
                emptied(act, ("ffn", layer, n, 0))
                nc.scalar.copy(hh[:, n % 3, :], hf[:, n % 2, :]).then_inc(hh_done, 1)

            def proj1(k, t):
                o, done = take(act, ("proj1", k, t))
                nc.scalar.copy(qraw[:, k % 2, t, :], o[:, 0:GV]).then_inc(done, 1)

            def squares(k):
                for t in range(TT):
                    emptied(act, ("proj1", k, t))
                if k:
                    act.wait_ge(ss_done, k)
                nc.scalar.activation(sq[:], qraw[:, k % 2, :, 0:GW], ACT.Square).then_inc(sq_done, 1)

            def turn1(k):
                for t in (0, 2):
                    o, done = take(act, ("turn1q", k, t))
                    nc.scalar.copy(*to_qst(o, t)).then_inc(done, 1)
                o, done = take(act, ("turn1k", k, 0))
                nc.scalar.copy(kst[:, :, 0:256], o.rearrange("p (z t) -> p z t", z=2)).then_inc(done, 1)

            def exps(k, c):
                o, done = take(act, ("scores1", k, c))
                act.wait_ge(mx_done, 4 * k + c + 1)
                for q in range(4):
                    e = nc.scalar.activation(pr[:, c, q, :], o[:, q * P:(q + 1) * P], ACT.Exp,
                                             bias=negm[:, c, q:q + 1], scale=float(HD1) ** -0.5,
                                             accum_out=psum1[:, c, q:q + 1])
                e.then_inc(done, 1)

            def rows_high(k):
                act.wait_ge(qn_done, k + 1)
                nc.scalar.copy(qhl[:, :, :, 0, :], qn[:, :, 0:REP * HD1].rearrange("p t (h d) -> p t h d", h=REP))
                nc.scalar.copy(khl[:, :, 0, :, :],
                               qn[:, :, REP * HD1:GW].rearrange("p t (a d) -> p t a d", a=1).to_broadcast(
                                   [P, TT, 2, HD1])).then_inc(rows_hi, 1)

            def turn_p(k):
                for c in (0, 2):
                    o, done = take(act, ("turn1p", k, c))
                    nc.scalar.copy(prt[:, c, :], o).then_inc(done, 1)

            def pv1(k):
                for half_ in range(2):
                    o, _ = take(act, ("pv1", k, half_))
                    hi_no[("pv1", k, half_)] = len(hi_no) + 1
                    nc.scalar.copy(ah[:, :, half_ * 256:(half_ + 1) * 256].rearrange("p hp (q w) -> p q hp w", q=4),
                                   o.rearrange("p (q hp w) -> p q hp w", q=4, hp=2)).then_inc(hi_done, 1)

            def attn1(k):
                new, mid, old = k < NIT, 0 <= k - 2 < NIT, 0 <= k - 3 < NIT
                if mid:
                    turn1(k - 2)
                if old:
                    pv1(k - 3)
                if new:
                    if k >= 2:
                        act.wait_ge(cos_done, k - 1)
                        act.wait_ge(sin_done, k - 1)
                    proj1(k, 0)
                    proj1(k, 1)
                if 0 <= k - 1 < NIT:
                    if k >= 2:
                        filled(act, ("turn1k", k - 2, 1))
                    rows_high(k - 1)
                for j in range(4):
                    if mid:
                        exps(k - 2, j)
                    if new and j < 2:
                        proj1(k, 2 + j)
                        if j == 1:
                            squares(k)
                if mid:
                    chunk(("wout", k - 2))
                    turn_p(k - 2)

            do = dict(chunk=chunk, qk0=qk0, v0=v0, stack0=stack0, scores0=scores0, pv0=pv0, at0=at0, xt=xt,
                      prep_ug=prep_ug, prep_down=prep_down, ffn=ffn, attn1=attn1)
            for step, *args in STEPS:
                if step in do:
                    do[step](*args)

        @block.vector
        def _(dve):
            links = [0]

            def link(ins):
                links[0] += 1
                ins.then_inc(vlink, 1)
                dve.wait_ge(vlink, links[0])

            def low(key, dst, hi, o=None):
                o_, done = take(dve, key)
                dve.wait_ge(hi_done, hi_no[key])
                nc.vector.tensor_tensor(dst, o_ if o is None else o(o_), hi.bitcast(F32), ALU.subtract).then_inc(
                    done, 1)

            def chunk(key):
                k = CHUNK_NO[key]
                name, c, kind, lo = CHUNKS[k]
                if lo != "dve":
                    return
                if kind == "tree":
                    dve.wait_ge(tree_done, 1)
                    r = tree[:, 1, 4 * c:4 * c + 4, :].rearrange("p a b -> p (a b)")
                else:
                    r = raw_chunk(dve, k)
                if kind == "pair":
                    if c:
                        dve.wait_ge(ch_hi, counted(k - 1, lambda x: x[2] != "copy"))
                    else:
                        dve.wait_ge(dn_lo, 4)
                    nc.vector.tensor_tensor(pair[:, 0:512], r[:, 0:512], r[:, 512:1024], ALU.add)
                    nc.vector.tensor_tensor(pair[:, 512:1024], r[:, 0:512], r[:, 512:1024], ALU.subtract).then_inc(
                        pair_done, 1)
                    dve.wait_ge(pair_done, c + 1)
                    r = pair[:]
                if kind != "copy":
                    dve.wait_ge(ch_hi, counted(k, lambda x: x[2] != "copy"))
                    hi, dst = chunk_target(name, c)
                    last = nc.vector.tensor_tensor(dst, r, hi.bitcast(F32), ALU.subtract)
                elif name == "sel":
                    last = nc.vector.tensor_copy(sel[:, c, :], r)
                elif name == "had":
                    last = nc.vector.tensor_copy(had[:], r)
                elif name == "eye":
                    last = nc.vector.tensor_copy(eye2[:], r)
                else:
                    last = nc.vector.tensor_copy(wmask[:].rearrange("p a b -> p (a b)"), r)
                last.then_inc(ch_lo["dve"], 1)

            def qk0(b):
                for z in range(2):
                    for m in range(KB):
                        low(("qk0", b, z, m), qkl[:, z, m, :], qkh[:, z, m, :])

            def stack0(b, hg):
                for j2 in range(2):
                    o, done = take(dve, ("stack0", b, hg, 1, j2))
                    nc.vector.tensor_copy(stk[:, hg % 2, 1, j2, :], o).then_inc(done, 1)

            def scores0(b, hg):
                for part in range(3):
                    at, w = [(0, 512), (512, 384), (896, 384)][part]
                    for h4 in (1, 3):
                        o, done = take(dve, ("scores0", b, hg, part, h4))
                        nc.vector.tensor_scalar(wt[:, hg % 2, h4, at:at + w], o[:, 0:w], -ATTN_THRESHOLD, 0.0,
                                                ALU.add, ALU.max).then_inc(done, 1)

            def turn0(b, hg):
                o, done = take(dve, ("turn0", b, hg))
                ov = o.rearrange("p (t h w) -> p t h w", t=TT, h=HG)
                link(nc.vector.tensor_scalar(rs0[:], ov[:, :, :, HD0], ATTN_EPS, None, ALU.add))
                link(nc.vector.reciprocal(ri0[:], rs0[:]))
                nc.vector.tensor_tensor(
                    an[:, :, 64 * hg:64 * hg + 64].rearrange("p t (h d) -> p t h d", h=HG), ov[:, :, :, 0:HD0],
                    ri0[:].rearrange("p t (h a) -> p t h a", a=1).to_broadcast([P, TT, HG, HD0]),
                    ALU.mult).then_inc(done, 1)

            def at0(b):
                for kb in range(KB):
                    low(("at0", b, kb), atl[:, kb, :], ath[:, kb, :])

            def xt(layer, b):
                for kb in range(KB):
                    low(("xt", layer, b, kb), xl[:, b, kb, :], xh[:, b, kb, :])

            def ln(layer, b):
                if layer == 0:
                    dve.wait_ge(rows_in[b], 16)
                for half_ in range(2):
                    o, done = take(dve, ("y", layer, b, half_))
                    at = b * TT + 2 * half_
                    nc.vector.tensor_tensor(xn[:, at:at + 2, :], o.rearrange("p (t c) -> p t c", t=2),
                                            xn[:, at:at + 2, :], ALU.add).then_inc(done, 1)
                    emptied(dve, ("y", layer, b, half_))
                    nc.vector.bn_stats(stats[:, 2 * half_, :], xn[:, at, :])
                    link(nc.vector.bn_stats(stats[:, 2 * half_ + 1, :], xn[:, at + 1, :]))
                    for t in (2 * half_, 2 * half_ + 1):
                        last = nc.vector.bn_aggr(mv[:, t, :], stats[:, t, :])
                last.then_inc(ln_var, 1)
                dve.wait_ge(ln_var, layer * B + b + 1)
                dve.wait_ge(ln_rstd, layer * B + b + 1)
                for t in range(TT):
                    at = b * TT + t
                    last = nc.vector.tensor_scalar(xn[:, at, :], xn[:, at, :], mv[:, t, 0:1], rstd[:, t:t + 1],
                                                   ALU.subtract, ALU.mult)
                last.then_inc(xn_done, 1)

            def prep_ug(c):
                dve.wait_ge(const_in["sign_ug"], 16)
                for m in range(KB):
                    key = ("prep_ug", c, m)
                    o, done = take(dve, key)
                    dve.wait_ge(hi_done, hi_no[key])
                    cols = slice(m * 512, (m + 1) * 512)
                    nc.vector.scalar_tensor_tensor(out=ug0l[:, c, cols], in0=o, scalar=sign_ug[:, m:m + 1],
                                                   in1=ug0h[:, c, cols].bitcast(F32), op0=ALU.mult,
                                                   op1=ALU.subtract).then_inc(done, 1)

            def prep_down(c):
                dve.wait_ge(const_in["sign_dp"], 16)
                dve.wait_ge(scales_set, 1)
                for m in range(2):
                    o, done = take(dve, ("prep_down", c, m))
                    if 2 * c + m:
                        dve.wait_ge(dn_lo, 2 * c + m)
                    for j in range(2):
                        i = 4 * c + 2 * m + j
                        last = nc.vector.scalar_tensor_tensor(
                            out=dtmp[:, j * C:(j + 1) * C], in0=o[:, j * C:(j + 1) * C], scalar=sign_dp[:, i:i + 1],
                            in1=scale_dp[:], op0=ALU.mult, op1=ALU.mult)
                    last.then_inc(done, 1)

            def ffn(layer, n):
                if n >= B * NI:
                    return
                i, nn = n % NI, layer * B * NI + n
                o, done = take(dve, ("ffn", layer, n, 0))
                emptied(dve, ("ffn", layer, n, 1))
                sc = scale_ug[:, i:i + 1] if layer == 0 else 1.0
                nc.vector.scalar_tensor_tensor(out=hf[:, n % 2, :], in0=o, scalar=sc, in1=sg[:, n % 2, :],
                                               op0=ALU.mult, op1=ALU.mult).then_inc(done, 1)
                dve.wait_ge(hh_done, nn + 1)
                nc.vector.tensor_tensor(hl[:, n % 3, :], hf[:, n % 2, :], hh[:, n % 3, :].bitcast(F32),
                                        ALU.subtract).then_inc(hl_done, 1)

            def rope_tables():
                dve.wait_ge(tables_in, 32)
                for z, tab in enumerate((cos5, sin5)):
                    for t in range(TT):
                        last = nc.vector.tensor_tensor(
                            tab[:, t, :].rearrange("p (h d) -> p h d", h=REP + 1),
                            nw[:, z, :].rearrange("p (h d) -> p h d", h=REP + 1),
                            ctab[:, z, t, :].rearrange("p (a d) -> p a d", a=1).to_broadcast([P, REP + 1, HD1]),
                            ALU.mult)
                last.then_inc(tabs_done, 1)

            def values1(k):
                s3, r = k % 3, qraw[:, k % 2]
                for t in range(TT):
                    emptied(dve, ("proj1", k, t))
                if k < 3:
                    nc.vector.memset(v1[0:HD1, s3, 1, 0, :], 0.0)
                nc.vector.tensor_copy(v1[:, s3, 0, :, :], r[:, :, GW:GV])
                nc.vector.tensor_copy(v1[0:64, s3, 1, 1:TT, :], r[64:128, 0:TT - 1, GW:GV])
                nc.vector.tensor_copy(v1[64:128, s3, 1, :, :], r[0:64, :, GW:GV]).then_inc(v1_done, 1)

            def cosines(k):
                if k == 0:
                    dve.wait_ge(tabs_done, 1)
                nc.vector.tensor_tensor(rot1[:], qraw[:, k % 2, :, 0:GW], cos5[:], ALU.mult).then_inc(cos_done, 1)

            def square_sums(k):
                dve.wait_ge(sq_done, k + 1)
                if k:
                    dve.wait_ge(rr_done, k)
                nc.vector.tensor_reduce(ssq[:].rearrange("p (t h) -> p t h", t=TT),
                                        sq[:].rearrange("p t (h d) -> p t h d", d=HD1), AX.X, ALU.add).then_inc(
                                            ss_done, 1)

            def normed(k):
                dve.wait_ge(rope_sum, k + 1)
                dve.wait_ge(rr_done, k + 1)
                if k:
                    dve.wait_ge(rows_lo, k)
                nc.vector.tensor_tensor(
                    qn[:].rearrange("p t (h d) -> p t h d", d=HD1), rot1[:].rearrange("p t (h d) -> p t h d", d=HD1),
                    rr[:].rearrange("p (t h a) -> p t h a", t=TT, a=1).to_broadcast([P, TT, REP + 1, HD1]),
                    ALU.mult).then_inc(qn_done, 1)

            def turn1(k):
                for t in (1, 3):
                    o, done = take(dve, ("turn1q", k, t))
                    nc.vector.tensor_copy(*to_qst(o, t)).then_inc(done, 1)
                o, done = take(dve, ("turn1k", k, 1))
                nc.vector.tensor_copy(kst[:, :, 256:512], o.rearrange("p (z t) -> p z t", z=2)).then_inc(done, 1)

            def probs(k, c):
                emptied(dve, ("scores1", k, c))
                link(nc.vector.reciprocal(pinv[:, c, :], psum1[:, c, :]))
                nc.vector.tensor_tensor(pr[:, c], pr[:, c],
                                        pinv[:, c, :].rearrange("p (q a) -> p q a", a=1).to_broadcast([P, 4, P]),
                                        ALU.mult).then_inc(pr_done, 1)

            def maxima(k, c):
                o, done = take(dve, ("scores1", k, c))
                link(nc.vector.tensor_reduce(mx[:, c, :], o.rearrange("p (q w) -> p q w", q=4), AX.X, ALU.max))
                nc.vector.tensor_scalar(negm[:, c, :], mx[:, c, :], -float(HD1) ** -0.5, None,
                                        ALU.mult).then_inc(mx_done, 1)

            def turn_p(k):
                for c in (1, 3):
                    o, done = take(dve, ("turn1p", k, c))
                    nc.vector.tensor_copy(prt[:, c, :], o).then_inc(done, 1)

            def pv1(k):
                for half_ in range(2):
                    cols = slice(half_ * 256, (half_ + 1) * 256)
                    low(("pv1", k, half_), al[:, :, cols].rearrange("p hp (q w) -> p q hp w", q=4),
                        ah[:, :, cols].rearrange("p hp (q w) -> p q hp w", q=4),
                        lambda o: o.rearrange("p (q hp w) -> p q hp w", q=4, hp=2))

            def attn1(k):
                new, mid, old = k < NIT, 0 <= k - 2 < NIT, 0 <= k - 3 < NIT
                if mid:
                    turn1(k - 2)
                if old:
                    pv1(k - 3)
                if 0 <= k - 1 < NIT:
                    normed(k - 1)
                for j in range(4):
                    if mid:
                        maxima(k - 2, j)
                        if j:
                            probs(k - 2, j - 1)
                    if new and j == 2:
                        for t in range(TT):
                            emptied(dve, ("proj1", k, t))
                        cosines(k)
                if mid:
                    probs(k - 2, 3)
                if new:
                    square_sums(k)
                    values1(k)
                if mid:
                    turn_p(k - 2)

            do = dict(chunk=chunk, qk0=qk0, stack0=stack0, scores0=scores0, turn0=turn0, at0=at0, xt=xt, ln=ln,
                      prep_ug=prep_ug, prep_down=prep_down, ffn=ffn, rope_tables=rope_tables, attn1=attn1)
            nc.vector.memset(bias0[:], -ATTN_THRESHOLD).then_inc(bias_set, 1)
            nc.vector.memset(vaug[:], 0.0).then_inc(vaug_zero, 1)
            dve.wait_ge(vaug_zero, 1)
            nc.vector.memset(vaug[:, :, :, HD0:HD0 + 1], 1.0).then_inc(vaug_set, 1)
            def tree_step():
                for name in ("identity", "scale_ug", "scale_dp"):
                    dve.wait_ge(const_in[name], 16)
                nc.vector.tensor_copy(identr[:], ident[:]).then_inc(identr_set, 1)
                nc.vector.tensor_scalar(scale_ug[:], scale_ug[:], float(C) ** -0.5, None, ALU.mult)
                nc.vector.tensor_scalar(scale_dp[:], scale_dp[:], float(INTER) ** -0.5, None,
                                        ALU.mult).then_inc(scales_set, 1)

            do["tree"] = tree_step
            for step, *args in STEPS:
                if step in do:
                    do[step](*args)

        @block.gpsimd
        def _(pool):
            links = [0]

            def link(ins):
                links[0] += 1
                ins.then_inc(plink, 1)
                pool.wait_ge(plink, links[0])

            def tree_step():
                pool.wait_ge(tree_in, 16)
                for n, st in enumerate((4, 2, 1)):
                    a = tree[:, n % 2].rearrange("p (g z s) c -> p g z (s c)", z=2, s=st)
                    o = tree[:, 1 - n % 2].rearrange("p (g z s) c -> p g z (s c)", z=2, s=st)
                    nc.gpsimd.tensor_tensor(o[:, :, 0, :], a[:, :, 0, :], a[:, :, 1, :], ALU.add)
                    last = nc.gpsimd.tensor_tensor(o[:, :, 1, :], a[:, :, 0, :], a[:, :, 1, :], ALU.subtract)
                    if st > 1:
                        link(last)
                last.then_inc(tree_done, 1)

            def chunk(key):
                k = CHUNK_NO[key]
                name, c, kind, lo = CHUNKS[k]
                if lo != "pool":
                    return
                hi, dst = chunk_target(name, c)
                r = raw_chunk(pool, k)
                pool.wait_ge(ch_hi, counted(k, lambda x: x[2] != "copy"))
                nc.gpsimd.tensor_tensor(dst, r, hi.bitcast(F32), ALU.subtract).then_inc(ch_lo["pool"], 1)

            def scores0(b, hg):
                if b + hg == 0:
                    pool.wait_ge(const_in["causal"], 16)
                for kb in range(TT):
                    if kb < 3:
                        emptied(pool, *[("scores0", b, hg, kb, h4) for h4 in range(HG)])
                    w = wt[:, hg % 2, :, W0_AT[kb]:W0_AT[kb] + P]
                    nc.gpsimd.tensor_tensor(
                        w, w, tri[:].rearrange("p (a q) -> p a q", a=1).to_broadcast([P, HG, P]),
                        ALU.mult).then_inc(w_mask, 1)

            def prep_down(c):
                for m in range(2):
                    cols = slice(m * 512, (m + 1) * 512)
                    pool.wait_ge(dn_hi, 2 * c + m + 1)
                    nc.gpsimd.tensor_tensor(dn0l[:, c, cols], dtmp[:], dn0h[:, c, cols].bitcast(F32),
                                            ALU.subtract).then_inc(dn_lo, 1)

            def ln(layer, b):
                pool.wait_ge(ln_var, layer * B + b + 1)
                link(nc.gpsimd.tensor_scalar(var_eps[:], mv[:, :, 1], LN_EPS, None, ALU.add))
                nc.gpsimd.tensor_tensor(rstd[:], var_eps[:], half[:, 0:TT], ALU.pow).then_inc(ln_rstd, 1)

            def rows_low(k):
                pool.wait_ge(rows_hi, k + 1)
                nc.gpsimd.tensor_tensor(qhl[:, :, :, 1, :],
                                        qn[:, :, 0:REP * HD1].rearrange("p t (h d) -> p t h d", h=REP),
                                        qhl[:, :, :, 0, :].bitcast(F32), ALU.subtract)
                nc.gpsimd.tensor_tensor(khl[:, :, 1, :, :],
                                        qn[:, :, REP * HD1:GW].rearrange("p t (a d) -> p t a d", a=1).to_broadcast(
                                            [P, TT, 2, HD1]),
                                        khl[:, :, 0, :, :].bitcast(F32), ALU.subtract).then_inc(rows_lo, 1)

            def attn1(k):
                if 0 <= k - 1 < NIT:
                    rows_low(k - 1)
                if k < NIT:
                    for t in range(TT):
                        emptied(pool, ("proj1", k, t))
                    if k:
                        pool.wait_ge(rope_sum, k)
                    else:
                        pool.wait_ge(tabs_done, 1)
                    rv = qraw[:, k % 2, :, 0:GW].rearrange("p t (h z d) -> p t h z d", h=REP + 1, z=2)
                    sv = sin5[:].rearrange("p t (h z d) -> p t h z d", h=REP + 1, z=2)
                    ov = rot2[:].rearrange("p t (h z d) -> p t h z d", h=REP + 1, z=2)
                    for z in range(2):
                        last = nc.gpsimd.tensor_tensor(ov[:, :, :, z, :], rv[:, :, :, 1 - z, :], sv[:, :, :, z, :],
                                                       ALU.mult)
                    last.then_inc(sin_done, 1)
                    pool.wait_ge(cos_done, k + 1)
                    pool.wait_ge(sin_done, k + 1)
                    nc.gpsimd.tensor_tensor(rot1[:], rot1[:], rot2[:], ALU.add).then_inc(rope_sum, 1)
                    pool.wait_ge(ss_done, k + 1)
                    if k:
                        pool.wait_ge(qn_done, k)
                    link(nc.gpsimd.tensor_scalar(rr[:], ssq[:], 1.0 / HD1, RMS_EPS, ALU.mult, ALU.add))
                    nc.gpsimd.tensor_tensor(rr[:], rr[:], half[:], ALU.pow).then_inc(rr_done, 1)
                if 0 <= k - 2 < NIT:
                    chunk(("wout", k - 2))

            do = dict(tree=tree_step, chunk=chunk, scores0=scores0, prep_down=prep_down, ln=ln, attn1=attn1)
            nc.gpsimd.memset(half[:], -0.5).then_inc(half_set, 1)
            pool.wait_ge(half_set, 1)
            for step, *args in STEPS:
                if step in do:
                    do[step](*args)


def constants():
    f = np.float32
    p = np.arange(P)
    had = np.array([[(-1.0) ** bin(i & j).count("1") for j in range(P)] for i in range(P)], f)
    sel = np.zeros((P, 2, 4, 2, P), f)
    for j in range(4):
        for par in range(2):
            for copy in range(4):
                for i in range(HD0):
                    row, col = HD0 * (2 * j + par) + i, 64 * par + HD0 * copy + i
                    sel[row, 0, j, copy % 2, col] = 1.0
                    sel[row, 1, j, copy // 2, col] = float(HD0) ** -0.5
    q, j = np.arange(WIN)[:, None], np.arange(P)[None, :]
    near = (j > q) & (j <= q + WIN)
    plain = np.where(near, 0.0, MASKED).astype(f)
    first = np.where(near & (j >= WIN), 0.0, MASKED).astype(f)
    msk = np.zeros((P, 1, 1024), f)
    msk[:WIN, 0] = np.concatenate([first, first] + [plain] * 6, axis=1)
    eye = np.zeros((P, 1, P), f)
    eye[:WIN, 0] = np.concatenate([np.eye(WIN, dtype=f)] * 2, axis=1)
    inv = (f(1.0) / f(10000.0) ** (np.arange(0, HD1, 2, dtype=f) / f(HD1))).astype(f)
    ang = np.arange(T, dtype=f)[:, None] * inv[None, :]
    emb = np.concatenate([ang, ang], axis=-1)
    sign = np.where(np.arange(HD1) < HD1 // 2, f(-1.0), f(1.0))
    tab = np.stack([np.cos(emb), np.sin(emb) * sign])
    return {
        "identity": np.eye(P, dtype=f),
        "causal": (p[None, :] >= p[:, None]).astype(f),
        "had": had.reshape(P, 1, P),
        "sel": sel.reshape(P, 2, 1024),
        "msk": msk,
        "eye": eye,
        "cos_sin": np.ascontiguousarray(tab.reshape(2, TT, P, HD1).transpose(2, 0, 1, 3)).astype(f),
    }


def kernel(L0_attn_x, L0_attn_Wq, L0_attn_Wk, L0_attn_Wv, L0_attn_Wo, L0_ffn_SU_ug, L0_ffn_SU_dp, L0_ffn_Wscale_ug,
           L0_ffn_Wscale_dp, L0_ffn_W_up, L0_ffn_W_gate, L0_ffn_W_down, L1_attn_w_qkv, L1_attn_w_out,
           L1_attn_q_norm_w, L1_attn_k_norm_w, L1_ffn_w_gate, L1_ffn_w_up, L1_ffn_w_down):
    import concourse.bacc as bacc
    from concourse.bass_utils import run_bass_kernel_spmd

    a = np.asarray

    def k_rows(w):
        w = a(w).T
        return w.reshape(w.shape[0] // P, P, w.shape[1]).transpose(1, 0, 2)

    def up_gate(up, gate):
        w = np.stack([k_rows(up), k_rows(gate)], axis=2)
        w = w.reshape(P, KB, 2, 4, 2, P).transpose(0, 3, 1, 4, 2, 5)
        return w.reshape(P, 4, 1024)

    nq, nk = KV * REP * HD1, KV * HD1
    qkv = k_rows(L1_attn_w_qkv)
    qkv = np.concatenate([qkv[:, :, :nq].reshape(P, KB, KV, REP * HD1),
                          qkv[:, :, nq:nq + nk].reshape(P, KB, KV, HD1),
                          qkv[:, :, nq + nk:].reshape(P, KB, KV, HD1)], axis=3)
    w0 = np.stack([np.concatenate([k_rows(L0_attn_Wq), k_rows(L0_attn_Wk)], axis=2),
                   np.concatenate([k_rows(L0_attn_Wv), k_rows(L0_attn_Wo)], axis=2)], axis=1)
    qw, kw = a(L1_attn_q_norm_w), a(L1_attn_k_norm_w)
    qr, kr = np.roll(qw, HD1 // 2), np.roll(kw, HD1 // 2)
    norm_w = np.stack([np.concatenate([qw] * REP + [kw]), np.concatenate([qr] * REP + [kr])])
    x = a(L0_attn_x)
    arrays = dict(constants())
    arrays.update({
        "x": x.reshape(B, T, KB, P).transpose(3, 0, 2, 1).reshape(P, B, KB * T),
        "w0": w0.reshape(P, 2, 1024),
        "ug0": up_gate(L0_ffn_W_up, L0_ffn_W_gate),
        "down0": k_rows(L0_ffn_W_down).reshape(P, 2, 1024),
        "qkv": qkv.transpose(0, 2, 1, 3).reshape(P, KV, KB * GV),
        "wout": k_rows(L1_attn_w_out).reshape(P, KV, 512),
        "ug1": up_gate(L1_ffn_w_up, L1_ffn_w_gate),
        "down1": k_rows(L1_ffn_w_down).reshape(P, 2, 1024),
        "sign_ug": a(L0_ffn_SU_ug).reshape(KB, P).T,
        "sign_dp": a(L0_ffn_SU_dp).reshape(NI, P).T,
        "scale_ug": a(L0_ffn_Wscale_ug).reshape(2 * NI, P).T,
        "scale_dp": np.broadcast_to(a(L0_ffn_Wscale_dp), (P, C)),
        "norm_w": np.broadcast_to(norm_w, (P, 2, GW)),
        "x_rows": x.reshape(B * TT, P, C).transpose(1, 0, 2),
    })
    nc = bacc.Bacc("TRN2", target_bir_lowering=False, num_devices=1)
    feed, dram = {}, {}
    for name, v in arrays.items():
        v = np.ascontiguousarray(v)
        feed["in_" + name] = v
        dram[name] = nc.dram_tensor("in_" + name, v.shape, mybir.dt.from_np(v.dtype), kind="ExternalInput").ap()
    out = nc.dram_tensor("out", (B, T, C), F32, kind="ExternalOutput").ap()
    post_ln_two_layers(nc, dram, out.rearrange("b (t p) c -> p (b t) c", p=P))
    r = run_bass_kernel_spmd(nc, [feed], core_ids=[0])
    return r.results[0]["out"]
```

```python
from contextlib import ExitStack

import numpy as np

import concourse.bass as bass
from concourse import mybir

ALU = mybir.AluOpType
ACT = mybir.ActivationFunctionType
AX = mybir.AxisListType
F32 = mybir.dt.float32
F32R = mybir.dt.float32r
BF16 = mybir.dt.bfloat16

P = 128
B, T, C = 2, 512, 256
KB = C // P
TT = T // P
LN_EPS = 1e-5
H0, HD0 = 16, 16
HG = 4
NHG = H0 // HG
ATTN_THRESHOLD, ATTN_EPS = -0.1, 1e-6
W0_AT = [0, 512, 896, 1152]
W0_COLS = 1280
PART_BLOCKS = [[0], [1], [2, 3]]
PART_AT = [(W0_AT[kbs[0]], sum(T - kb * P for kb in kbs)) for kbs in PART_BLOCKS]
INTER = 1024
NI = INTER // P
KV, REP, HD1 = 8, 4, 64
WIN = 64
NQ = T // WIN
GW = (REP + 1) * HD1
GV = GW + HD1
RMS_EPS = 1e-6
MASKED = -1e30
NIT = B * KV
TENSOR_PASS = [("turn1k", 4), ("out1", 6, 0), ("turn_p", 5, 0), ("turn_p", 5, 1), ("turn1q", 4, 0),
    ("turn_p", 5, 2), ("proj1", 1, 1), ("turn1q", 4, 1), ("turn1q", 4, 2), ("turn1q", 4, 3), ("turn_p", 5, 3),
    ("scores1", 4, 0), ("pv1", 5, 0), ("scores1", 4, 1), ("proj1", 1, 2), ("scores1", 4, 2), ("scores1", 4, 3),
    ("out1", 6, 1), ("pv1", 5, 1), ("proj1", 1, 3), ("proj1", 0, 0)]
SCALAR_PASS = [("turn1k", 4), ("squares", 2), ("turn_p", 5, 0), ("turn_p", 5, 1), ("turn1q", 4, 0), ("turn_p", 5, 2),
    ("proj1", 1, 1), ("turn1q", 4, 2), ("turn1q", 4, 1), ("turn1q", 4, 3), ("turn_p", 5, 3), ("wout", 5),
    ("rows_high", 3), ("pv1", 5, 0), ("exps", 4, 0), ("proj1", 1, 2), ("exps", 4, 1), ("exps", 4, 2), ("pv1", 5, 1),
    ("exps", 4, 3), ("proj1", 1, 3)]
VECTOR_PASS = [("turn1k", 4), ("probs", 5, 3), ("values1", 2), ("rope_sums", 3), ("normed", 3), ("maxima", 4, 0),
    ("square_sums", 2), ("maxima", 4, 1), ("maxima", 4, 2), ("pv1", 5, 0), ("cosines", 2), ("maxima", 4, 3),
    ("probs", 4, 0), ("probs", 4, 1), ("probs", 4, 2), ("pv1", 5, 1), ("proj1", 0, 0)]
GPSIMD_PASS = [("rms_inverses", 3), ("sines", 2), ("wout", 5), ("rows_low", 3)]
PASSES = NIT + max(step[1] for step in TENSOR_PASS + SCALAR_PASS + VECTOR_PASS + GPSIMD_PASS)
OUT_BEHIND = max(step[1] for step in TENSOR_PASS if step[0] == "out1")
EARLY_AT = [NI + 5, NI + 6, NI + 7]
EARLY = len(EARLY_AT)
SLOTS = 3
FLAG = 2
RING = 6

FFN1_CHUNKS = [("ug1", c) for c in range(4)] + [("down1", c) for c in range(2)]
WOUT_FIRST = NIT + 1 - next(step[1] for step in SCALAR_PASS if step[0] == "wout")
CHUNKS = ([("x", 0, "split", "dve"), ("w0", 0, "split", "dve"), ("sel", 0, "copy", "dve"),
           ("sel", 1, "copy", "dve"), ("w0", 1, "split", "dve"), ("x", 1, "split", "dve"),
           ("had", 0, "copy", "dve"), ("down0", 0, "tree", "dve"), ("down0", 1, "tree", "dve")]
          + [("ug0", c, "pair", "dve") for c in range(4)]
          + [("msk", 0, "copy", "dve"), ("eye", 0, "copy", "dve")]
          + [("qkv", g, "split", "pool") for g in range(KV)]
          + [("wout", i, "split", "pool") for i in range(WOUT_FIRST)]
          + [ch + ("split", "pool") for i in range(len(FFN1_CHUNKS))
             for ch in [FFN1_CHUNKS[i]] + [("wout", WOUT_FIRST + i)] * (WOUT_FIRST + i < NIT)])
LOADS = [k for k, ch in enumerate(CHUNKS) if ch[2] != "tree"]
CHUNK_NO = {(name, c): k for k, (name, c, _, _) in enumerate(CHUNKS)}
CHUNK_COLS = {"x": 1024, "w0": 1024, "sel": 1024, "had": P, "down0": 1024, "ug0": 1024, "msk": 1024, "eye": P,
              "qkv": KB * GV, "wout": 512, "ug1": 1024, "down1": 1024}


def counted(k, wanted):
    return sum(1 for ch in CHUNKS[:k + 1] if wanted(ch))


def has(i):
    return 0 <= i < NIT


def program_steps():
    s = [("chunk", ("x", 0)), ("chunk", ("w0", 0)), ("chunk", ("sel", 0)), ("chunk", ("sel", 1)), ("qk0", 0),
         ("chunk", ("w0", 1)), ("stack0", 0, 0), ("v0", 0), ("tree",), ("chunk", ("x", 1)), ("chunk", ("had", 0))]
    for n in range(B * NHG + 1):
        now, last, then = divmod(n, NHG), divmod(n - 1, NHG), divmod(n + 1, NHG)
        if n == 1:
            s.append(("chunk", ("down0", 0)))
        if 2 <= n <= 5:
            s.append(("pair", n - 2))
        for part in range(3):
            if n < B * NHG:
                s.append(("scores0",) + now + (part,))
            if n and part < 2:
                s.append(("pv0",) + last + (part,))
            if n == 1 and part == 0:
                s.append(("prep_down", 0))
        if n == 1:
            s.append(("chunk", ("down0", 1)))
        if 2 <= n <= 5:
            s.append(("chunk", ("ug0", n - 2)))
        if n + 1 < B * NHG:
            if n + 1 == NHG:
                s.append(("qk0", 1))
            s.append(("stack0",) + then)
        if n == 1:
            s.append(("prep_down", 1))
        if 2 <= n <= 5:
            s.append(("prep_ug", n - 2))
        if n == NHG:
            s.append(("v0", 1))
        if n == NHG + 1:
            s.append(("at0", 0))
        if n:
            s.append(("turn0",) + last)
        if n == B * NHG - 1:
            s += [("wo0", 0), ("ln", 0, 0)]
        if n == B * NHG:
            s.append(("xt", 1, 0))
    s += [("at0", 1), ("ffn", 0, 0), ("wo0", 1), ("ln", 0, 1), ("ffn", 0, 1), ("chunk", ("msk", 0)),
          ("chunk", ("eye", 0)), ("rope_tables",)]
    for n in range(2, B * NI + 2):
        s.append(("ffn", 0, n))
        if n == 3:
            s.append(("xt", 1, 1))
        if 4 <= n < 4 + KV:
            s.append(("chunk", ("qkv", n - 4)))
        if n == NI + 1:
            s.append(("ln", 1, 0))
        if n == NI + 3:
            s.append(("xt", 2, 0))
        if n in EARLY_AT:
            s.append(("attn1", EARLY_AT.index(n)))
    for k in range(EARLY, PASSES):
        s.append(("attn1", k))
        if k == EARLY:
            s.append(("ln", 1, 1))
        if k == EARLY + 1:
            s.append(("xt", 2, 1))
        if k == KV + OUT_BEHIND:
            s.append(("xt", 3, 0))
        if 0 <= k - NIT < len(FFN1_CHUNKS):
            s.append(("chunk", FFN1_CHUNKS[k - NIT]))
        if PASSES - 3 <= k < PASSES - 1:
            s.append(("ffn", 1, k - PASSES + 3))
        if k >= OUT_BEHIND and (k - OUT_BEHIND) % KV == KV - 1:
            s.append(("ln", 2, (k - OUT_BEHIND) // KV))
    for n in range(2, B * NI + 2):
        s.append(("ffn", 1, n))
        if n == 2:
            s.append(("xt", 3, 1))
        if n == NI + 1:
            s.append(("ln", 3, 0))
    s.append(("ln", 3, 1))
    return s


STEPS = program_steps()


def post_ln_two_layers(nc, dram, out):
    with ExitStack() as ctx:
        def sem(name):
            return ctx.enter_context(nc.semaphore(name))

        def place(scope, name, shape, dt=F32):
            return scope.enter_context(nc.sbuf_tensor(name, [P] + shape, dt))

        def keep(name, shape, dt=F32):
            return place(ctx, name, shape, dt)

        xh = keep("x_t_high", [B, KB, T], F32R)
        xl = keep("x_t_low", [B, KB, T], F32R)
        with ExitStack() as s:
            place(s, "below_work", [TT * C], F32)
            dtmp = place(s, "down_scaled", [2, 512], F32)
        with ExitStack() as s:
            place(s, "below_pair", [TT * C], F32)
            pair = place(s, "ug0_sum_difference", [1024], F32)
        xn = keep("x_rows", [B * TT, C])
        raw = keep("raw_chunks", [SLOTS, 1024])
        ident = keep("identity", [P])
        identr = keep("identity_r", [P], F32R)
        had = keep("hadamard", [P], F32R)
        tri = keep("causal_block", [P])
        eye2 = keep("eye_twice", [P], BF16)
        wmask = keep("window_mask", [2, 512], BF16)
        sign_ug = keep("sign_ug", [KB])
        sign_dp = keep("sign_dp", [NI])
        scale_ug = keep("scale_ug", [2 * NI])
        scale_dp = keep("scale_dp", [C])
        bias0 = keep("bias_threshold", [1])
        half = keep("minus_half", [REP * (REP + 1)])
        stats = keep("ln_stats", [TT, 6])
        mv = keep("ln_mean_var", [TT, 2])
        var_eps = keep("ln_var_eps", [TT])
        rstd = keep("ln_rstd", [TT])
        rs0 = keep("row_sums0", [TT, HG])
        ri0 = keep("row_inverse0", [TT, HG])

        with ExitStack() as s:
            ug0h = place(s, "ug0_high", [4, 1024], F32R)
            ug0l = place(s, "ug0_low", [4, 1024], F32R)
            dn0h = place(s, "down0_high", [2, 1024], F32R)
            dn0l = place(s, "down0_low", [2, 1024], F32R)
            end_a = nc.sbuf_base
        with ExitStack() as s:
            place(s, "below_tree", [4096], F32)
            tree = place(s, "down_tree", [2, NI, C], F32)
        with ExitStack() as s:
            qn = place(s, "roped", [TT, GW], F32)
            qhl = place(s, "q_rows_high_low", [TT, REP, 2, HD1], F32R)
            khl = place(s, "k_rows_high_low", [TT, 2, HD1], F32R)
            wol = place(s, "wout_low", [2, 2, C], F32R)
            qst = place(s, "q_stack", [2, NQ, P], F32R)
            kst = place(s, "k_stack", [2, 2, T], F32R)
            pr = place(s, "probs", [4, 4, P], F32)
            end_b = nc.sbuf_base
        hold_a = keep("place_a", [(max(end_a, end_b) - nc.sbuf_base + 3) // 4])
        with ExitStack() as s:
            wt = place(s, "weights_t", [2, HG, W0_COLS], F32)
            sel = place(s, "selectors", [2, 1024], F32R)
            end_a = nc.sbuf_base
        with ExitStack() as s:
            qkvh = place(s, "qkv_high", [KV, KB * GV], F32R)
            qkvl = place(s, "qkv_low", [KV, KB * GV], F32R)
            end_b = nc.sbuf_base
        with ExitStack() as s:
            ug1h = place(s, "ug1_high", [4, 1024], F32R)
            ug1l = place(s, "ug1_low", [4, 1024], F32R)
            dn1h = place(s, "down1_high", [2, 1024], F32R)
            dn1l = place(s, "down1_low", [2, 1024], F32R)
            end_c = nc.sbuf_base
        hold_b = keep("place_b", [(max(end_a, end_b, end_c) - nc.sbuf_base + 3) // 4])
        base_c = nc.sbuf_base
        with ExitStack() as s:
            w0h = place(s, "w0_high", [2, KB, 512], F32R)
            w0l = place(s, "w0_low", [2, KB, 512], F32R)
            w0_end = nc.sbuf_base
            qkh = place(s, "qk0_high", [2, KB, T], F32R)
            qkl = place(s, "qk0_low", [2, KB, T], F32R)
            stk = place(s, "qk0_stacks", [2, 2, 2, T], F32R)
            vaug = place(s, "v0_and_ones", [TT, H0, 32], F32)
            osb = place(s, "out0_t", [T], F32)
            an = place(s, "out0_rows", [TT, C], F32)
            prep_at = (nc.sbuf_base - base_c) // 4
            ath = place(s, "out0_t_high", [KB, T], F32R)
            atl = place(s, "out0_t_low", [KB, T], F32R)
        with ExitStack() as s:
            place(s, "below_prep", [prep_at], F32)
            ph = place(s, "prep_high", [1024], F32R)
            pl = place(s, "prep_low", [1024], F32R)
        with ExitStack() as s:
            v1 = place(s, "v1_rows", [5, 2, TT, HD1], F32)
            rot1 = place(s, "rope_cos_part", [TT, GW], F32)
            ssq = place(s, "square_sums", [TT * (REP + 1)], F32)
            rr = place(s, "rms_inverse", [2, TT * (REP + 1)], F32)
            negm = place(s, "minus_max", [4, 4], F32)
            mx = place(s, "row_max", [4, 4], F32)
            psum1 = place(s, "prob_sums", [4, 4], F32)
            pinv = place(s, "prob_inverse", [4, 4], F32)
            place(s, "until_w0_ends", [(w0_end - nc.sbuf_base) // 4])
            ffn0_at = nc.sbuf_base
            prt = place(s, "probs_t", [4, 512], F32)
            ah = place(s, "out1_t_high", [2, T], F32R)
            al = place(s, "out1_t_low", [2, T], F32R)
            woh = place(s, "wout_high", [2, 2, C], F32R)
            ffn1_at = nc.sbuf_base
            qraw = place(s, "qkv_rows", [2, TT, GV], F32)
            rot2 = place(s, "rope_sin_part", [TT, GW], F32)
            sq = place(s, "squares", [TT, GW], F32)
            cos5 = place(s, "cos_weighted", [TT, GW], F32)
            sin5 = place(s, "sin_weighted", [TT, GW], F32)
        with ExitStack() as s:
            place(s, "below_tables", [(ffn1_at - base_c) // 4])
            ctab = place(s, "cos_sin_table", [2, TT, HD1], F32)
            nw = place(s, "norm_weights", [2, GW], F32)
        ffn_buffers = []
        for layer, at in ((0, ffn0_at), (1, ffn1_at)):
            with ExitStack() as s:
                place(s, f"below_ffn{layer}", [(at - base_c) // 4])
                ffn_buffers.append((place(s, f"silu_gate{layer}", [2, T], F32), place(s, f"hidden{layer}", [2, T], F32),
                                    place(s, f"hidden_high{layer}", [3, T], F32R),
                                    place(s, f"hidden_low{layer}", [3, T], F32R)))

        ps = ctx.enter_context(nc.psum_tensor("psum", [P, 8, 512], F32))

        full = [sem(f"bank{i}_full") for i in range(8)]
        emptied_ = [sem(f"bank{i}_emptied") for i in range(8)]
        ch_in = [sem(f"chunk_in{i}") for i in range(SLOTS)]
        ch_hi = sem("chunk_high")
        ch_lo = {"dve": sem("chunk_low_dve"), "pool": sem("chunk_low_pool")}
        const_in = {name: sem("in_" + name) for name in
                    ("identity", "causal", "sign_ug", "sign_dp", "scale_ug", "scale_dp")}
        identr_set = sem("identity_r_set")
        scales_set = sem("scales_set")
        pair_done = sem("ug0_pair_done")
        rows_in = [sem(f"x_rows_in{b}") for b in range(B)]
        tree_in = sem("tree_in")
        tables_in = sem("tables_in")
        stored = sem("rows_stored")
        bias_set = sem("bias_set")
        vaug_zero = sem("v0_zeroed")
        vaug_set = sem("v0_ones_set")
        half_set = sem("minus_half_set")
        vlink = sem("dve_own_order")
        plink = sem("pool_own_order")
        ln_var = sem("ln_var_ready")
        ln_rstd = sem("ln_rstd_ready")
        xn_done = sem("x_rows_ready")
        hi_done = sem("high_of_bank")
        w_mask = sem("weights0_masked")
        tree_done = sem("tree_done")
        dn_hi = sem("down0_high_done")
        dn_lo = sem("down0_low_done")
        hh_done, hl_done = sem("hidden_high_done"), sem("hidden_low_done")
        tabs_done = sem("rope_tables_done")
        sq_done, ss_done, rr_done = sem("squares_done"), sem("square_sums_done"), sem("rms_inverse_done")
        sin_done, cos_done, rope_sum = sem("sin_part_done"), sem("cos_part_done"), sem("rope_sum_done")
        qn_done = sem("roped_done")
        rows_hi, rows_lo = sem("qk_rows_high"), sem("qk_rows_low")
        v1_done = sem("v1_done")
        mx_done = [sem(f"minus_max_done{c}") for c in range(TT)]
        pr_done = [sem(f"probs_done{c}") for c in range(TT)]

        job = {}
        fills = [0] * 8
        ring_at = [0]

        def chunk_wait(eng, key):
            k = CHUNK_NO[key]
            kind, low = CHUNKS[k][2:]
            if kind != "copy":
                eng.wait_ge(ch_hi, counted(k, lambda c: c[2] != "copy"))
            eng.wait_ge(ch_lo[low], counted(k, lambda c: c[3] == low))

        def emptied(eng, *keys):
            for key in keys:
                bank, n = job[key]
                eng.wait_ge(emptied_[bank], n + 1)

        after_out = {}
        unmarked = []
        hi_no = {}

        block = ctx.enter_context(nc.Block())

        @block.tensor
        def _(pe):
            def claim(key, bank=None):
                if bank is None:
                    bank = ring_at[0] % RING
                    ring_at[0] += 1
                job[key] = (bank, fills[bank])
                if fills[bank]:
                    pe.wait_ge(emptied_[bank], fills[bank])
                fills[bank] += 1
                for out in unmarked:
                    after_out[out] = key
                unmarked.clear()
                return ps[:, bank, :], full[bank]

            def three(o, a, b_, first, last, **kw):
                (ah_, al_), (bh_, bl_) = a, b_
                nc.tensor.matmul(o, ah_, bh_, start=first, stop=False, **kw)
                nc.tensor.matmul(o, ah_, bl_, start=False, stop=False, **kw)
                return nc.tensor.matmul(o, al_, bh_, start=False, stop=last, **kw)

            acc = {}

            def x_ready(layer, b):
                if layer == 0:
                    chunk_wait(pe, ("x", b))
                else:
                    emptied(pe, *[("xt", layer, b, kb) for kb in range(KB)])

            def qk0(b):
                x_ready(0, b)
                chunk_wait(pe, ("w0", 0))
                for z in range(2):
                    for m in range(KB):
                        o, done = claim(("qk0", b, z, m))
                        for kb in range(KB):
                            at = z * C + m * P
                            mm = three(o, (w0h[:, 0, kb, at:at + P], w0l[:, 0, kb, at:at + P]),
                                       (xh[:, b, kb, :], xl[:, b, kb, :]), kb == 0, kb == KB - 1)
                        mm.then_inc(done, 1)

            def v0(b):
                chunk_wait(pe, ("w0", 1))
                for half_ in range(2):
                    o, done = claim(("v0", b, half_))
                    for t2 in range(2):
                        t = 2 * half_ + t2
                        for kb in range(KB):
                            mm = three(o[:, t2 * C:(t2 + 1) * C],
                                       (xh[:, b, kb, t * P:(t + 1) * P], xl[:, b, kb, t * P:(t + 1) * P]),
                                       (w0h[:, 1, kb, 0:C], w0l[:, 1, kb, 0:C]), kb == 0, kb == KB - 1)
                    mm.then_inc(done, 1)

            def stack0(b, hg):
                chunk_wait(pe, ("sel", 1))
                for z in range(2):
                    emptied(pe, ("qk0", b, z, hg // 2))
                    for j2 in range(2):
                        j = (2 * hg + j2) % 4
                        o, done = claim(("stack0", b, hg, z, j2))
                        sv = sel[:].rearrange("p z (j l m) -> p z j l m", j=4, l=2)
                        nc.tensor.matmul(o, sv[:, z, j, 0, :], qkh[:, z, hg // 2, :], start=True, stop=False)
                        nc.tensor.matmul(o, sv[:, z, j, 1, :], qkl[:, z, hg // 2, :], start=False,
                                         stop=True).then_inc(done, 1)

            def scores0(b, hg, part):
                if part == 0:
                    emptied(pe, *[("stack0", b, hg, z, j2) for z in range(2) for j2 in range(2)])
                for h4 in range(HG):
                    o, done = claim(("scores0", b, hg, part, h4))
                    r = slice(64 * (h4 % 2), 64 * (h4 % 2) + 64)
                    at = 0
                    for kb in PART_BLOCKS[part]:
                        w = T - kb * P
                        mm = nc.tensor.matmul(o[:, at:at + w], stk[r, hg % 2, 1, h4 // 2, kb * P:(kb + 1) * P],
                                              stk[r, hg % 2, 0, h4 // 2, kb * P:T], start=True, stop=True)
                        at += w
                    mm.then_inc(done, 1)

            def pv0(b, hg, half_):
                n = b * NHG + hg
                if half_ == 0:
                    acc["pv0"] = claim(("pv0", b, hg), 6)
                    emptied(pe, ("v0", b, 0), ("v0", b, 1))
                    pe.wait_ge(vaug_set, 1)
                o, done = acc["pv0"]
                for kb in (2 * half_, 2 * half_ + 1):
                    pe.wait_ge(w_mask, TT * n + kb + 1)
                    for h4 in range(HG):
                        w = T - kb * P
                        mm = nc.tensor.matmul(o[32 * h4:32 * h4 + 32, kb * P:T], vaug[:, kb, HG * hg + h4, :],
                                              wt[:, hg % 2, h4, W0_AT[kb]:W0_AT[kb] + w],
                                              start=kb == 0, stop=kb == TT - 1, skip_group_check=True)
                if half_:
                    mm.then_inc(done, 1)

            def turn0(b, hg):
                emptied(pe, ("pv0", b, hg))
                pe.wait_ge(const_in["identity"], 16)
                o, done = claim(("turn0", b, hg), 7)
                for t in range(TT):
                    mm = nc.tensor.transpose(o[:, t * P:(t + 1) * P], osb[:, t * P:(t + 1) * P], ident[:])
                mm.then_inc(done, 1)

            def at0(b):
                emptied(pe, *[("turn0", b, hg) for hg in range(NHG)])
                for kb in range(KB):
                    o, done = claim(("at0", b, kb))
                    for t in range(TT):
                        mm = nc.tensor.transpose(o[:, t * P:(t + 1) * P], an[:, t, kb * P:(kb + 1) * P], ident[:])
                    mm.then_inc(done, 1)

            def wo0(b):
                emptied(pe, *[("at0", b, kb) for kb in range(KB)])
                for half_ in range(2):
                    o, done = claim(("y", 0, b, half_))
                    for t2 in range(2):
                        t = 2 * half_ + t2
                        for kb in range(KB):
                            mm = three(o[:, t2 * C:(t2 + 1) * C],
                                       (ath[:, kb, t * P:(t + 1) * P], atl[:, kb, t * P:(t + 1) * P]),
                                       (w0h[:, 1, kb, C:2 * C], w0l[:, 1, kb, C:2 * C]), kb == 0, kb == KB - 1)
                    mm.then_inc(done, 1)

            def xt(layer, b):
                pe.wait_ge(xn_done, (layer - 1) * B + b + 1)
                for kb in range(KB):
                    o, done = claim(("xt", layer, b, kb))
                    for t in range(TT):
                        mm = nc.tensor.transpose(o[:, t * P:(t + 1) * P], xn[:, b * TT + t, kb * P:(kb + 1) * P],
                                                 ident[:])
                    mm.then_inc(done, 1)

            def prep_ug(c):
                chunk_wait(pe, ("ug0", c))
                for m in range(KB):
                    o, done = claim(("prep_ug", c, m))
                    nc.tensor.matmul(o, had[:], ph[:, m * 512:(m + 1) * 512], start=True, stop=False)
                    nc.tensor.matmul(o, had[:], pl[:, m * 512:(m + 1) * 512], start=False, stop=True).then_inc(done, 1)

            def prep_down(c):
                chunk_wait(pe, ("had", 0))
                chunk_wait(pe, ("down0", c))
                for m in range(2):
                    o, done = claim(("prep_down", c, m))
                    nc.tensor.matmul(o, had[:], ph[:, m * 512:(m + 1) * 512], start=True, stop=False)
                    nc.tensor.matmul(o, had[:], pl[:, m * 512:(m + 1) * 512], start=False,
                                     stop=True).then_inc(done, 1)

            def ffn(layer, n):
                sg, hf, hh, hl = ffn_buffers[layer]
                wh, wl, dh, dl = (ug0h, ug0l, dn0h, dn0l) if layer == 0 else (ug1h, ug1l, dn1h, dn1l)
                if n < B * NI:
                    b, i = divmod(n, NI)
                    if i == 0:
                        x_ready(1 + 2 * layer, b)
                    if layer == 0:
                        emptied(pe, *[("prep_ug", i // 2, m) for m in range(KB)])
                    else:
                        chunk_wait(pe, ("ug1", i // 2))
                    for u in (1, 0):
                        o, done = claim(("ffn", layer, n, u))
                        for kb in range(KB):
                            at = kb * 512 + (i % 2) * 256 + u * P
                            mm = three(o, (wh[:, i // 2, at:at + P], wl[:, i // 2, at:at + P]),
                                       (xh[:, b, kb, :], xl[:, b, kb, :]), kb == 0, kb == KB - 1)
                        mm.then_inc(done, 1)
                if n >= FLAG:
                    n -= FLAG
                    b, i = divmod(n, NI)
                    if i == 0:
                        for half_ in range(2):
                            acc[half_] = claim(("y", 1 + 2 * layer, b, half_), 6 + half_)
                    if layer == 0:
                        pe.wait_ge(dn_lo, i // 2 + 1)
                    else:
                        chunk_wait(pe, ("down1", i // 4))
                    pe.wait_ge(hl_done, layer * B * NI + n + 1)
                    for t in range(TT):
                        o, done = acc[t // 2]
                        at = (i % 4) * C
                        mm = three(o[:, (t % 2) * C:(t % 2) * C + C],
                                   (hh[:, n % 3, t * P:(t + 1) * P], hl[:, n % 3, t * P:(t + 1) * P]),
                                   (dh[:, i // 4, at:at + C], dl[:, i // 4, at:at + C]),
                                   i == 0 and t % 2 == 0, i == NI - 1, skip_group_check=True)
                        if i == NI - 1 and t % 2:
                            mm.then_inc(done, 1)

            def proj1(k, t):
                b, g = divmod(k, KV)
                if t == 0:
                    if g == 0:
                        x_ready(2, b)
                    chunk_wait(pe, ("qkv", g))
                o, done = claim(("proj1", k, t))
                for kb in range(KB):
                    mm = three(o[:, 0:GV], (xh[:, b, kb, t * P:(t + 1) * P], xl[:, b, kb, t * P:(t + 1) * P]),
                               (qkvh[:, g, kb * GV:(kb + 1) * GV], qkvl[:, g, kb * GV:(kb + 1) * GV]),
                               kb == 0, kb == KB - 1)
                mm.then_inc(done, 1)

            def turned(o, rows):
                return nc.tensor.matmul(o, rows.rearrange("p a d -> p (a d)"), identr[:], start=True, stop=True)

            def turn1k(k):
                pe.wait_ge(identr_set, 1)
                pe.wait_ge(rows_hi, k + 1)
                pe.wait_ge(rows_lo, k + 1)
                o, done = claim(("turn1k", k))
                for t in range(TT):
                    mm = turned(o[:, t * P:(t + 1) * P], khl[:, t, :, :])
                mm.then_inc(done, 1)

            def turn1q(k, t):
                o, done = claim(("turn1q", k, t))
                for h in range(REP):
                    mm = turned(o[:, h * P:(h + 1) * P], qhl[:, t, h, :, :])
                mm.then_inc(done, 1)

            def scores1(k, c):
                chunk_wait(pe, ("eye", 0))
                o, done = claim(("scores1", k, c))
                emptied(pe, ("turn1q", k, c))
                if c == 0:
                    emptied(pe, ("turn1k", k))
                nc.tensor.matmul(o, eye2[0:64, :], wmask[0:64, 0 if c == 0 else 1, :], start=True, stop=False,
                                 skip_group_check=True)
                for q2 in range(2):
                    qb = 2 * c + q2
                    k0 = max(0, (qb - 1) * WIN)
                    k1 = (qb + 1) * WIN
                    for hp in range(2):
                        at = (2 * q2 + hp) * P + P - (k1 - k0)
                        for z in range(2):
                            mm = nc.tensor.matmul(o[:, at:at + k1 - k0], qst[:, hp, qb, :], kst[:, k % 2, z, k0:k1],
                                                  start=False, stop=z == 1, skip_group_check=True)
                mm.then_inc(done, 1)

            def turn_p(k, c):
                pe.wait_ge(pr_done[c], k + 1)
                o, done = claim(("turn1p", k, c))
                for q in range(4):
                    mm = nc.tensor.transpose(o[:, q * P:(q + 1) * P], pr[:, c, q, :], ident[:])
                mm.then_inc(done, 1)

            def pv1(k, half_):
                if half_ == 0:
                    pe.wait_ge(v1_done, k + 1)
                o, done = claim(("pv1", k, half_))
                emptied(pe, ("turn1p", k, 2 * half_), ("turn1p", k, 2 * half_ + 1))
                for c2 in range(2):
                    pv = prt[:, 2 * half_ + c2, :].rearrange("p (qb hp h w) -> p qb hp h w", qb=2, hp=2, h=2)
                    for q2 in range(2):
                        for h2 in range(2):
                            at = (2 * c2 + q2) * P
                            mm = nc.tensor.matmul(o[64 * h2:64 * h2 + 64, at:at + P],
                                                  v1[:, k % 5, 1 - q2, 2 * half_ + c2, :],
                                                  pv[:, q2, :, h2, :], start=True, stop=True)
                mm.then_inc(done, 1)

            acc1 = {}

            def out1(k, half_):
                b, g = divmod(k, KV)
                if g == 0:
                    acc1[half_] = claim(("y", 2, b, half_), 6 + half_)
                if half_ == 0:
                    chunk_wait(pe, ("wout", k))
                emptied(pe, ("pv1", k, half_))
                o, done = acc1[half_]
                for t2 in range(2):
                    t = 2 * half_ + t2
                    for hp in range(2):
                        mm = three(o[:, t2 * C:(t2 + 1) * C],
                                   (ah[:, hp, t * P:(t + 1) * P], al[:, hp, t * P:(t + 1) * P]),
                                   (woh[:, k % 2, hp, :], wol[:, k % 2, hp, :]),
                                   g == 0 and hp == 0 and t2 == 0, g == KV - 1 and hp == 1,
                                   skip_group_check=True)
                if g == KV - 1:
                    mm.then_inc(done, 1)
                unmarked.append((k, half_))

            in_pass = dict(proj1=proj1, turn1k=turn1k, turn1q=turn1q, scores1=scores1, turn_p=turn_p, pv1=pv1, out1=out1)

            def attn1(k):
                for step, behind, *part in TENSOR_PASS:
                    if has(k - behind):
                        in_pass[step](k - behind, *part)

            do = dict(qk0=qk0, v0=v0, stack0=stack0, scores0=scores0, pv0=pv0, turn0=turn0, at0=at0, wo0=wo0, xt=xt,
                      prep_ug=prep_ug, prep_down=prep_down, ffn=ffn, attn1=attn1)
            for step, *args in STEPS:
                if step in do:
                    do[step](*args)

        def take(eng, key):
            bank, n = job[key]
            eng.wait_ge(full[bank], n + 1)
            return ps[:, bank, :], emptied_[bank]

        def filled(eng, key):
            bank, n = job[key]
            eng.wait_ge(full[bank], n + 1)

        def rows_free(eng, k):
            if k >= 2:
                for read in (ss_done, cos_done, sin_done, v1_done):
                    eng.wait_ge(read, k - 1)

        def raw_chunk(eng, k):
            n = LOADS.index(k)
            eng.wait_ge(ch_in[n % SLOTS], 16 * (n // SLOTS + 1))
            return raw[:, n % SLOTS, 0:CHUNK_COLS[CHUNKS[k][0]]]

        def chunk_target(name, c):
            if name == "x":
                return [a[:, c].rearrange("p k t -> p (k t)") for a in (xh, xl)]
            if name == "w0":
                return [a[:, c].rearrange("p k t -> p (k t)") for a in (w0h, w0l)]
            if name in ("ug0", "down0"):
                return [ph[:], pl[:]]
            if name == "wout":
                return [a[:, c % 2].rearrange("p k t -> p (k t)") for a in (woh, wol)]
            return [a[:, c, :] for a in {"qkv": (qkvh, qkvl), "ug1": (ug1h, ug1l), "down1": (dn1h, dn1l)}[name]]

        def to_qst(o, t):
            dst = qst[:, :, 2 * t:2 * t + 2, :].rearrange("p hp q (h w) -> p hp h q w", h=2)
            return dst, o.rearrange("p (hp h q w) -> p hp h q w", hp=2, h=2, q=2)

        @block.sync
        def _(sp):
            def load_chunk(n):
                k = LOADS[n]
                name, c = CHUNKS[k][:2]
                if n >= SLOTS:
                    chunk_wait(sp, CHUNKS[LOADS[n - SLOTS]][:2])
                sp.dma_start(raw[:, n % SLOTS, 0:CHUNK_COLS[name]],
                             dram[name][:, c % KV if name == "wout" else c, :]).then_inc(ch_in[n % SLOTS], 16)

            def load_const(tile, name):
                sp.dma_start(tile[:], dram[name]).then_inc(const_in[name], 16)

            for n in range(SLOTS):
                load_chunk(n)
            load_const(tri, "causal")
            sp.dma_start(tree[:, 0].rearrange("p a b -> p (a b)"),
                         dram["down0"].rearrange("p c n -> p (c n)")).then_inc(tree_in, 16)
            load_chunk(SLOTS)
            for tile, name in ((ident, "identity"), (scale_dp, "scale_dp"), (sign_dp, "sign_dp"),
                               (scale_ug, "scale_ug"), (sign_ug, "sign_ug")):
                load_const(tile, name)
            load_chunk(SLOTS + 1)
            sp.dma_start(xn[:, 0:TT, :], dram["x_rows"][:, 0:TT, :]).then_inc(rows_in[0], 16)
            for n in range(SLOTS + 2, len(LOADS)):
                if CHUNKS[LOADS[n]][0] == "msk":
                    chunk_wait(sp, ("ug0", 3))
                    sp.dma_start(xn[:, TT:, :], dram["x_rows"][:, TT:, :]).then_inc(rows_in[1], 16)
                    filled(sp, ("y", 0, B - 1, 1))
                    sp.dma_start(ctab[:], dram["cos_sin"]).then_inc(tables_in, 16)
                    sp.dma_start(nw[:], dram["norm_w"]).then_inc(tables_in, 16)
                load_chunk(n)
            for b in range(B):
                sp.wait_ge(xn_done, 3 * B + b + 1)
                sp.dma_start(out[:, b * TT:(b + 1) * TT, :], xn[:, b * TT:(b + 1) * TT, :]).then_inc(stored, 16)
            sp.wait_ge(stored, 16 * B)

        @block.scalar
        def _(act):
            def high(key, dst, **scale):
                o, _ = take(act, key)
                hi_no[key] = len(hi_no) + 1
                if scale:
                    nc.scalar.activation(dst, o, ACT.Copy, **scale).then_inc(hi_done, 1)
                else:
                    nc.scalar.copy(dst, o).then_inc(hi_done, 1)

            def chunk(key):
                k = CHUNK_NO[key]
                name, c, kind, low = CHUNKS[k]
                if kind == "copy":
                    return
                if kind == "split":
                    src = raw_chunk(act, k)
                elif kind == "pair":
                    act.wait_ge(pair_done, c + 1)
                    src = pair[:]
                else:
                    act.wait_ge(tree_done, 1)
                    src = tree[:, 1, 4 * c:4 * c + 4, :].rearrange("p a b -> p (a b)")
                nc.scalar.copy(chunk_target(name, c)[0], src).then_inc(ch_hi, 1)

            def qk0(b):
                for z in range(2):
                    for m in range(KB):
                        high(("qk0", b, z, m), qkh[:, z, m, :])

            def v0(b):
                act.wait_ge(vaug_zero, 1)
                for half_ in range(2):
                    o, done = take(act, ("v0", b, half_))
                    nc.scalar.copy(vaug[:, 2 * half_:2 * half_ + 2, :, 0:HD0],
                                   o.rearrange("p (t h d) -> p t h d", t=2, h=H0)).then_inc(done, 1)

            def stack0(b, hg):
                for j2 in range(2):
                    o, done = take(act, ("stack0", b, hg, 0, j2))
                    nc.scalar.copy(stk[:, hg % 2, 0, j2, :], o).then_inc(done, 1)

            def scores0(b, hg, part):
                act.wait_ge(bias_set, 1)
                at, w = PART_AT[part]
                for h4 in (0, 2):
                    o, done = take(act, ("scores0", b, hg, part, h4))
                    nc.scalar.activation(wt[:, hg % 2, h4, at:at + w], o[:, 0:w], ACT.Relu,
                                         bias=bias0[:]).then_inc(done, 1)

            def pv0(b, hg, half_):
                if half_ == 0:
                    return
                o, done = take(act, ("pv0", b, hg))
                n = b * NHG + hg
                if n:
                    filled(act, ("turn0",) + divmod(n - 1, NHG))
                nc.scalar.copy(osb[:], o).then_inc(done, 1)

            def at0(b):
                for kb in range(KB):
                    high(("at0", b, kb), ath[:, kb, :])

            def xt(layer, b):
                for kb in range(KB):
                    high(("xt", layer, b, kb), xh[:, b, kb, :])

            def prep_ug(c):
                act.wait_ge(const_in["sign_ug"], 16)
                for m in range(KB):
                    high(("prep_ug", c, m), ug0h[:, c, m * 512:(m + 1) * 512], scale=sign_ug[:, m:m + 1])

            def prep_down(c):
                for m in range(2):
                    emptied(act, ("prep_down", c, m))
                    nc.scalar.copy(dn0h[:, c, m * 512:(m + 1) * 512], dtmp[:, m, :]).then_inc(dn_hi, 1)

            def ffn(layer, n):
                sg, hf, hh, hl = ffn_buffers[layer]
                if n >= B * NI:
                    return
                i = n % NI
                o, done = take(act, ("ffn", layer, n, 1))
                if n >= 2:
                    emptied(act, ("ffn", layer, n - 2, 0))
                if layer == 0:
                    act.wait_ge(scales_set, 1)
                kw = dict(scale=scale_ug[:, NI + i:NI + i + 1]) if layer == 0 else {}
                nc.scalar.activation(sg[:, n % 2, :], o, ACT.Silu, **kw).then_inc(done, 1)
                emptied(act, ("ffn", layer, n, 0))
                nc.scalar.copy(hh[:, n % 3, :], hf[:, n % 2, :]).then_inc(hh_done, 1)

            def proj1(k, t):
                rows_free(act, k)
                o, done = take(act, ("proj1", k, t))
                nc.scalar.copy(qraw[:, k % 2, t, :], o[:, 0:GV]).then_inc(done, 1)

            def squares(k):
                for t in range(TT):
                    emptied(act, ("proj1", k, t))
                if k:
                    act.wait_ge(ss_done, k)
                nc.scalar.activation(sq[:], qraw[:, k % 2, :, 0:GW], ACT.Square).then_inc(sq_done, 1)

            def turn1k(k):
                o, _ = take(act, ("turn1k", k))
                hi_no["turn1k", k] = len(hi_no) + 1
                nc.scalar.copy(kst[0:HD1, k % 2, 0, :], o[0:HD1])
                nc.scalar.copy(kst[HD1:P, k % 2, 0, :], o[0:HD1]).then_inc(hi_done, 1)

            def turn1q(k, t):
                o, done = take(act, ("turn1q", k, t))
                nc.scalar.copy(*to_qst(o, t)).then_inc(done, 1)

            def exps(k, c):
                o, done = take(act, ("scores1", k, c))
                act.wait_ge(mx_done[c], k + 1)
                for q in range(4):
                    e = nc.scalar.activation(pr[:, c, q, :], o[:, q * P:(q + 1) * P], ACT.Exp,
                                             bias=negm[:, c, q:q + 1], scale=float(HD1) ** -0.5,
                                             accum_out=psum1[:, c, q:q + 1])
                e.then_inc(done, 1)

            def rows_high(k):
                act.wait_ge(qn_done, k + 1)
                if k:
                    for t in range(TT):
                        filled(act, ("turn1q", k - 1, t))
                nc.scalar.copy(qhl[:, :, :, 0, :], qn[:, :, 0:REP * HD1].rearrange("p t (h d) -> p t h d", h=REP))
                nc.scalar.copy(khl[:, :, 0, :], qn[:, :, REP * HD1:GW]).then_inc(rows_hi, 1)

            def turn_p(k, c):
                o, done = take(act, ("turn1p", k, c))
                nc.scalar.copy(prt[:, c, :], o).then_inc(done, 1)

            def pv1(k, half_):
                o, _ = take(act, ("pv1", k, half_))
                hi_no[("pv1", k, half_)] = len(hi_no) + 1
                nc.scalar.copy(ah[:, :, half_ * 256:(half_ + 1) * 256].rearrange("p hp (q w) -> p q hp w", q=4),
                               o.rearrange("p (q hp w) -> p q hp w", q=4, hp=2)).then_inc(hi_done, 1)

            def wout(k):
                if k >= 2:
                    for half_ in range(2):
                        filled(act, after_out[k - 2, half_])
                chunk(("wout", k))

            in_pass = dict(proj1=proj1, turn1k=turn1k, turn1q=turn1q, turn_p=turn_p, pv1=pv1, squares=squares,
                            rows_high=rows_high, exps=exps, wout=wout)

            def attn1(k):
                for step, behind, *part in SCALAR_PASS:
                    if has(k - behind):
                        in_pass[step](k - behind, *part)

            do = dict(chunk=chunk, qk0=qk0, v0=v0, stack0=stack0, scores0=scores0, pv0=pv0, at0=at0, xt=xt,
                      prep_ug=prep_ug, prep_down=prep_down, ffn=ffn, attn1=attn1)
            for step, *args in STEPS:
                if step in do:
                    do[step](*args)

        @block.vector
        def _(dve):
            links = [0]

            def link(ins):
                links[0] += 1
                ins.then_inc(vlink, 1)
                dve.wait_ge(vlink, links[0])

            def low(key, dst, hi, o=None):
                o_, done = take(dve, key)
                dve.wait_ge(hi_done, hi_no[key])
                nc.vector.tensor_tensor(dst, o_ if o is None else o(o_), hi.bitcast(F32), ALU.subtract).then_inc(
                    done, 1)

            def chunk(key):
                k = CHUNK_NO[key]
                name, c, kind, lo = CHUNKS[k]
                if lo != "dve":
                    return
                if kind == "tree":
                    dve.wait_ge(tree_done, 1)
                    r = tree[:, 1, 4 * c:4 * c + 4, :].rearrange("p a b -> p (a b)")
                elif kind == "pair":
                    dve.wait_ge(pair_done, c + 1)
                    r = pair[:]
                else:
                    r = raw_chunk(dve, k)
                if kind != "copy":
                    dve.wait_ge(ch_hi, counted(k, lambda x: x[2] != "copy"))
                    hi, dst = chunk_target(name, c)
                    last = nc.vector.tensor_tensor(dst, r, hi.bitcast(F32), ALU.subtract)
                elif name == "sel":
                    last = nc.vector.tensor_copy(sel[:, c, :], r)
                elif name == "had":
                    last = nc.vector.tensor_copy(had[:], r)
                elif name == "eye":
                    last = nc.vector.tensor_copy(eye2[:], r)
                else:
                    last = nc.vector.tensor_copy(wmask[:].rearrange("p a b -> p (a b)"), r)
                last.then_inc(ch_lo["dve"], 1)

            def qk0(b):
                for z in range(2):
                    for m in range(KB):
                        low(("qk0", b, z, m), qkl[:, z, m, :], qkh[:, z, m, :])

            def stack0(b, hg):
                for j2 in range(2):
                    o, done = take(dve, ("stack0", b, hg, 1, j2))
                    nc.vector.tensor_copy(stk[:, hg % 2, 1, j2, :], o).then_inc(done, 1)

            def scores0(b, hg, part):
                at, w = PART_AT[part]
                for h4 in (1, 3):
                    o, done = take(dve, ("scores0", b, hg, part, h4))
                    nc.vector.tensor_scalar(wt[:, hg % 2, h4, at:at + w], o[:, 0:w], -ATTN_THRESHOLD, 0.0,
                                            ALU.add, ALU.max).then_inc(done, 1)

            def turn0(b, hg):
                o, done = take(dve, ("turn0", b, hg))
                ov = o.rearrange("p (t h w) -> p t h w", t=TT, h=HG)
                link(nc.vector.tensor_scalar(rs0[:], ov[:, :, :, HD0], ATTN_EPS, None, ALU.add))
                link(nc.vector.reciprocal(ri0[:], rs0[:]))
                nc.vector.tensor_tensor(
                    an[:, :, 64 * hg:64 * hg + 64].rearrange("p t (h d) -> p t h d", h=HG), ov[:, :, :, 0:HD0],
                    ri0[:].rearrange("p t (h a) -> p t h a", a=1).to_broadcast([P, TT, HG, HD0]),
                    ALU.mult).then_inc(done, 1)

            def at0(b):
                for kb in range(KB):
                    low(("at0", b, kb), atl[:, kb, :], ath[:, kb, :])

            def xt(layer, b):
                for kb in range(KB):
                    low(("xt", layer, b, kb), xl[:, b, kb, :], xh[:, b, kb, :])

            def ln(layer, b):
                if layer == 0:
                    dve.wait_ge(rows_in[b], 16)
                for half_ in range(2):
                    o, done = take(dve, ("y", layer, b, half_))
                    at = b * TT + 2 * half_
                    nc.vector.tensor_tensor(xn[:, at:at + 2, :], o.rearrange("p (t c) -> p t c", t=2),
                                            xn[:, at:at + 2, :], ALU.add).then_inc(done, 1)
                    emptied(dve, ("y", layer, b, half_))
                    nc.vector.bn_stats(stats[:, 2 * half_, :], xn[:, at, :])
                    link(nc.vector.bn_stats(stats[:, 2 * half_ + 1, :], xn[:, at + 1, :]))
                    for t in (2 * half_, 2 * half_ + 1):
                        last = nc.vector.bn_aggr(mv[:, t, :], stats[:, t, :])
                last.then_inc(ln_var, 1)
                dve.wait_ge(ln_var, layer * B + b + 1)
                dve.wait_ge(ln_rstd, layer * B + b + 1)
                for t in range(TT):
                    at = b * TT + t
                    last = nc.vector.tensor_scalar(xn[:, at, :], xn[:, at, :], mv[:, t, 0:1], rstd[:, t:t + 1],
                                                   ALU.subtract, ALU.mult)
                last.then_inc(xn_done, 1)

            def prep_ug(c):
                dve.wait_ge(const_in["sign_ug"], 16)
                for m in range(KB):
                    key = ("prep_ug", c, m)
                    o, done = take(dve, key)
                    dve.wait_ge(hi_done, hi_no[key])
                    cols = slice(m * 512, (m + 1) * 512)
                    nc.vector.scalar_tensor_tensor(out=ug0l[:, c, cols], in0=o, scalar=sign_ug[:, m:m + 1],
                                                   in1=ug0h[:, c, cols].bitcast(F32), op0=ALU.mult,
                                                   op1=ALU.subtract).then_inc(done, 1)

            def prep_down(c):
                dve.wait_ge(const_in["sign_dp"], 16)
                dve.wait_ge(scales_set, 1)
                for m in range(2):
                    o, done = take(dve, ("prep_down", c, m))
                    if c:
                        dve.wait_ge(dn_lo, m + 1)
                    for j in range(2):
                        i = 4 * c + 2 * m + j
                        last = nc.vector.scalar_tensor_tensor(
                            out=dtmp[:, m, j * C:(j + 1) * C], in0=o[:, j * C:(j + 1) * C], scalar=sign_dp[:, i:i + 1],
                            in1=scale_dp[:], op0=ALU.mult, op1=ALU.mult)
                    last.then_inc(done, 1)

            def ffn(layer, n):
                sg, hf, hh, hl = ffn_buffers[layer]
                if n >= B * NI:
                    return
                i, nn = n % NI, layer * B * NI + n
                o, done = take(dve, ("ffn", layer, n, 0))
                emptied(dve, ("ffn", layer, n, 1))
                sc = scale_ug[:, i:i + 1] if layer == 0 else 1.0
                nc.vector.scalar_tensor_tensor(out=hf[:, n % 2, :], in0=o, scalar=sc, in1=sg[:, n % 2, :],
                                               op0=ALU.mult, op1=ALU.mult).then_inc(done, 1)
                dve.wait_ge(hh_done, nn + 1)
                nc.vector.tensor_tensor(hl[:, n % 3, :], hf[:, n % 2, :], hh[:, n % 3, :].bitcast(F32),
                                        ALU.subtract).then_inc(hl_done, 1)

            def rope_tables():
                dve.wait_ge(tables_in, 32)
                for z, tab in enumerate((cos5, sin5)):
                    for t in range(TT):
                        last = nc.vector.tensor_tensor(
                            tab[:, t, :].rearrange("p (h d) -> p h d", h=REP + 1),
                            nw[:, z, :].rearrange("p (h d) -> p h d", h=REP + 1),
                            ctab[:, z, t, :].rearrange("p (a d) -> p a d", a=1).to_broadcast([P, REP + 1, HD1]),
                            ALU.mult)
                last.then_inc(tabs_done, 1)

            def values1(k):
                slot, r = k % 5, qraw[:, k % 2]
                for t in range(TT):
                    emptied(dve, ("proj1", k, t))
                if k >= 5:
                    for half_ in range(2):
                        filled(dve, ("pv1", k - 5, half_))
                if k < 5:
                    nc.vector.memset(v1[0:HD1, slot, 1, 0, :], 0.0)
                nc.vector.tensor_copy(v1[:, slot, 0, :, :], r[:, :, GW:GV])
                nc.vector.tensor_copy(v1[0:64, slot, 1, 1:TT, :], r[64:128, 0:TT - 1, GW:GV])
                nc.vector.tensor_copy(v1[64:128, slot, 1, :, :], r[0:64, :, GW:GV]).then_inc(v1_done, 1)

            def cosines(k):
                if k:
                    dve.wait_ge(qn_done, k)
                for t in range(TT):
                    emptied(dve, ("proj1", k, t))
                if k == 0:
                    dve.wait_ge(tabs_done, 1)
                nc.vector.tensor_tensor(rot1[:], qraw[:, k % 2, :, 0:GW], cos5[:], ALU.mult).then_inc(cos_done, 1)

            def square_sums(k):
                dve.wait_ge(sq_done, k + 1)
                if k:
                    dve.wait_ge(rr_done, k)
                nc.vector.tensor_reduce(ssq[:].rearrange("p (t h) -> p t h", t=TT),
                                        sq[:].rearrange("p t (h d) -> p t h d", d=HD1), AX.X, ALU.add).then_inc(
                                            ss_done, 1)

            def rope_sums(k):
                dve.wait_ge(cos_done, k + 1)
                dve.wait_ge(sin_done, k + 1)
                nc.vector.tensor_tensor(rot1[:], rot1[:], rot2[:], ALU.add).then_inc(rope_sum, 1)

            def normed(k):
                dve.wait_ge(rope_sum, k + 1)
                dve.wait_ge(rr_done, k + 1)
                if k == 0:
                    filled(dve, ("y", 1, B - 1, 1))
                if k:
                    dve.wait_ge(rows_lo, k)
                nc.vector.tensor_tensor(
                    qn[:].rearrange("p t (h d) -> p t h d", d=HD1), rot1[:].rearrange("p t (h d) -> p t h d", d=HD1),
                    rr[:, k % 2, :].rearrange("p (t h a) -> p t h a", t=TT, a=1).to_broadcast([P, TT, REP + 1, HD1]),
                    ALU.mult).then_inc(qn_done, 1)

            def turn1k(k):
                o, done = take(dve, ("turn1k", k))
                dve.wait_ge(hi_done, hi_no["turn1k", k])
                nc.vector.tensor_copy(kst[0:HD1, k % 2, 1, :], o[HD1:P])
                nc.vector.tensor_copy(kst[HD1:P, k % 2, 1, :], o[HD1:P]).then_inc(done, 1)

            def probs(k, c):
                emptied(dve, ("scores1", k, c))
                link(nc.vector.reciprocal(pinv[:, c, :], psum1[:, c, :]))
                nc.vector.tensor_tensor(pr[:, c], pr[:, c],
                                        pinv[:, c, :].rearrange("p (q a) -> p q a", a=1).to_broadcast([P, 4, P]),
                                        ALU.mult).then_inc(pr_done[c], 1)

            def proj1(k, t):
                rows_free(dve, k)
                o, done = take(dve, ("proj1", k, t))
                nc.vector.tensor_copy(qraw[:, k % 2, t, :], o[:, 0:GV]).then_inc(done, 1)

            def maxima(k, c):
                o, done = take(dve, ("scores1", k, c))
                link(nc.vector.tensor_reduce(mx[:, c, :], o.rearrange("p (q w) -> p q w", q=4), AX.X, ALU.max))
                nc.vector.tensor_scalar(negm[:, c, :], mx[:, c, :], -float(HD1) ** -0.5, None,
                                        ALU.mult).then_inc(mx_done[c], 1)

            def pv1(k, half_):
                cols = slice(half_ * 256, (half_ + 1) * 256)
                low(("pv1", k, half_), al[:, :, cols].rearrange("p hp (q w) -> p q hp w", q=4),
                    ah[:, :, cols].rearrange("p hp (q w) -> p q hp w", q=4),
                    lambda o: o.rearrange("p (q hp w) -> p q hp w", q=4, hp=2))

            in_pass = dict(proj1=proj1, turn1k=turn1k, pv1=pv1, maxima=maxima, probs=probs, cosines=cosines,
                           square_sums=square_sums, normed=normed, values1=values1, rope_sums=rope_sums)

            def attn1(k):
                for step, behind, *part in VECTOR_PASS:
                    if has(k - behind):
                        in_pass[step](k - behind, *part)

            do = dict(chunk=chunk, qk0=qk0, stack0=stack0, scores0=scores0, turn0=turn0, at0=at0, xt=xt, ln=ln,
                      prep_ug=prep_ug, prep_down=prep_down, ffn=ffn, rope_tables=rope_tables, attn1=attn1)
            nc.vector.memset(bias0[:], -ATTN_THRESHOLD).then_inc(bias_set, 1)
            nc.vector.memset(vaug[:], 0.0).then_inc(vaug_zero, 1)
            dve.wait_ge(vaug_zero, 1)
            nc.vector.memset(vaug[:, :, :, HD0:HD0 + 1], 1.0).then_inc(vaug_set, 1)
            def tree_step():
                for name in ("identity", "scale_ug", "scale_dp"):
                    dve.wait_ge(const_in[name], 16)
                nc.vector.tensor_copy(identr[:], ident[:]).then_inc(identr_set, 1)
                nc.vector.tensor_scalar(scale_ug[:], scale_ug[:], float(C) ** -0.5, None, ALU.mult)
                nc.vector.tensor_scalar(scale_dp[:], scale_dp[:], float(INTER) ** -0.5, None,
                                        ALU.mult).then_inc(scales_set, 1)

            do["tree"] = tree_step
            for step, *args in STEPS:
                if step in do:
                    do[step](*args)

        @block.gpsimd
        def _(pool):
            links = [0]

            def link(ins):
                links[0] += 1
                ins.then_inc(plink, 1)
                pool.wait_ge(plink, links[0])

            def tree_step():
                pool.wait_ge(tree_in, 16)
                for n, st in enumerate((4, 2, 1)):
                    a = tree[:, n % 2].rearrange("p (g z s) c -> p g z (s c)", z=2, s=st)
                    o = tree[:, 1 - n % 2].rearrange("p (g z s) c -> p g z (s c)", z=2, s=st)
                    nc.gpsimd.tensor_tensor(o[:, :, 0, :], a[:, :, 0, :], a[:, :, 1, :], ALU.add)
                    last = nc.gpsimd.tensor_tensor(o[:, :, 1, :], a[:, :, 0, :], a[:, :, 1, :], ALU.subtract)
                    if st > 1:
                        link(last)
                last.then_inc(tree_done, 1)

            def pair_step(c):
                if c:
                    chunk_wait(pool, ("ug0", c - 1))
                else:
                    pool.wait_ge(dn_lo, 4)
                r = raw_chunk(pool, CHUNK_NO["ug0", c])
                nc.gpsimd.tensor_tensor(pair[:, 0:512], r[:, 0:512], r[:, 512:1024], ALU.add)
                nc.gpsimd.tensor_tensor(pair[:, 512:1024], r[:, 0:512], r[:, 512:1024], ALU.subtract).then_inc(
                    pair_done, 1)

            def chunk(key):
                k = CHUNK_NO[key]
                name, c, kind, lo = CHUNKS[k]
                if lo != "pool":
                    return
                hi, dst = chunk_target(name, c)
                r = raw_chunk(pool, k)
                pool.wait_ge(ch_hi, counted(k, lambda x: x[2] != "copy"))
                nc.gpsimd.tensor_tensor(dst, r, hi.bitcast(F32), ALU.subtract).then_inc(ch_lo["pool"], 1)

            def scores0(b, hg, part):
                if b + hg + part == 0:
                    pool.wait_ge(const_in["causal"], 16)
                emptied(pool, *[("scores0", b, hg, part, h4) for h4 in range(HG)])
                for kb in PART_BLOCKS[part]:
                    w = wt[:, hg % 2, :, W0_AT[kb]:W0_AT[kb] + P]
                    nc.gpsimd.tensor_tensor(
                        w, w, tri[:].rearrange("p (a q) -> p a q", a=1).to_broadcast([P, HG, P]),
                        ALU.mult).then_inc(w_mask, 1)

            def prep_down(c):
                for m in range(2):
                    cols = slice(m * 512, (m + 1) * 512)
                    pool.wait_ge(dn_hi, 2 * c + m + 1)
                    nc.gpsimd.tensor_tensor(dn0l[:, c, cols], dtmp[:, m, :], dn0h[:, c, cols].bitcast(F32),
                                            ALU.subtract).then_inc(dn_lo, 1)

            def ln(layer, b):
                pool.wait_ge(ln_var, layer * B + b + 1)
                link(nc.gpsimd.tensor_scalar(var_eps[:], mv[:, :, 1], LN_EPS, None, ALU.add))
                nc.gpsimd.tensor_tensor(rstd[:], var_eps[:], half[:, 0:TT], ALU.pow).then_inc(ln_rstd, 1)

            def rows_low(k):
                pool.wait_ge(rows_hi, k + 1)
                nc.gpsimd.tensor_tensor(qhl[:, :, :, 1, :],
                                        qn[:, :, 0:REP * HD1].rearrange("p t (h d) -> p t h d", h=REP),
                                        qhl[:, :, :, 0, :].bitcast(F32), ALU.subtract)
                nc.gpsimd.tensor_tensor(khl[:, :, 1, :], qn[:, :, REP * HD1:GW], khl[:, :, 0, :].bitcast(F32),
                                        ALU.subtract).then_inc(rows_lo, 1)

            def sines(k):
                for t in range(TT):
                    emptied(pool, ("proj1", k, t))
                if k:
                    pool.wait_ge(rope_sum, k)
                else:
                    pool.wait_ge(tabs_done, 1)
                rv = qraw[:, k % 2, :, 0:GW].rearrange("p t (h z d) -> p t h z d", h=REP + 1, z=2)
                sv = sin5[:].rearrange("p t (h z d) -> p t h z d", h=REP + 1, z=2)
                ov = rot2[:].rearrange("p t (h z d) -> p t h z d", h=REP + 1, z=2)
                for z in range(2):
                    last = nc.gpsimd.tensor_tensor(ov[:, :, :, z, :], rv[:, :, :, 1 - z, :], sv[:, :, :, z, :], ALU.mult)
                last.then_inc(sin_done, 1)

            def rms_inverses(k):
                pool.wait_ge(ss_done, k + 1)
                if k >= 2:
                    pool.wait_ge(qn_done, k - 1)
                r = rr[:, k % 2, :]
                link(nc.gpsimd.tensor_scalar(r, ssq[:], 1.0 / HD1, RMS_EPS, ALU.mult, ALU.add))
                nc.gpsimd.tensor_tensor(r, r, half[:], ALU.pow).then_inc(rr_done, 1)

            def wout(k):
                chunk(("wout", k))

            in_pass = dict(sines=sines, rms_inverses=rms_inverses, rows_low=rows_low, wout=wout)

            def attn1(k):
                for step, behind, *part in GPSIMD_PASS:
                    if has(k - behind):
                        in_pass[step](k - behind, *part)

            do = dict(tree=tree_step, pair=pair_step, chunk=chunk, scores0=scores0, prep_down=prep_down, ln=ln, attn1=attn1)
            nc.gpsimd.memset(half[:], -0.5).then_inc(half_set, 1)
            pool.wait_ge(half_set, 1)
            for step, *args in STEPS:
                if step in do:
                    do[step](*args)


def constants():
    f = np.float32
    p = np.arange(P)
    had = np.array([[(-1.0) ** bin(i & j).count("1") for j in range(P)] for i in range(P)], f)
    sel = np.zeros((P, 2, 4, 2, P), f)
    for j in range(4):
        for par in range(2):
            for copy in range(4):
                for i in range(HD0):
                    row, col = HD0 * (2 * j + par) + i, 64 * par + HD0 * copy + i
                    sel[row, 0, j, copy % 2, col] = 1.0
                    sel[row, 1, j, copy // 2, col] = float(HD0) ** -0.5
    q, j = np.arange(WIN)[:, None], np.arange(P)[None, :]
    near = (j > q) & (j <= q + WIN)
    plain = np.where(near, 0.0, MASKED).astype(f)
    first = np.where(near & (j >= WIN), 0.0, MASKED).astype(f)
    msk = np.zeros((P, 1, 1024), f)
    msk[:WIN, 0] = np.concatenate([first, first] + [plain] * 6, axis=1)
    eye = np.zeros((P, 1, P), f)
    eye[:WIN, 0] = np.concatenate([np.eye(WIN, dtype=f)] * 2, axis=1)
    inv = (f(1.0) / f(10000.0) ** (np.arange(0, HD1, 2, dtype=f) / f(HD1))).astype(f)
    ang = np.arange(T, dtype=f)[:, None] * inv[None, :]
    emb = np.concatenate([ang, ang], axis=-1)
    sign = np.where(np.arange(HD1) < HD1 // 2, f(-1.0), f(1.0))
    tab = np.stack([np.cos(emb), np.sin(emb) * sign])
    return {
        "identity": np.eye(P, dtype=f),
        "causal": (p[None, :] >= p[:, None]).astype(f),
        "had": had.reshape(P, 1, P),
        "sel": sel.reshape(P, 2, 1024),
        "msk": msk,
        "eye": eye,
        "cos_sin": np.ascontiguousarray(tab.reshape(2, TT, P, HD1).transpose(2, 0, 1, 3)).astype(f),
    }


def kernel(L0_attn_x, L0_attn_Wq, L0_attn_Wk, L0_attn_Wv, L0_attn_Wo, L0_ffn_SU_ug, L0_ffn_SU_dp, L0_ffn_Wscale_ug,
           L0_ffn_Wscale_dp, L0_ffn_W_up, L0_ffn_W_gate, L0_ffn_W_down, L1_attn_w_qkv, L1_attn_w_out,
           L1_attn_q_norm_w, L1_attn_k_norm_w, L1_ffn_w_gate, L1_ffn_w_up, L1_ffn_w_down):
    import concourse.bacc as bacc
    from concourse.bass_utils import run_bass_kernel_spmd

    a = np.asarray

    def k_rows(w):
        w = a(w).T
        return w.reshape(w.shape[0] // P, P, w.shape[1]).transpose(1, 0, 2)

    def up_gate(up, gate):
        w = np.stack([k_rows(up), k_rows(gate)], axis=2)
        w = w.reshape(P, KB, 2, 4, 2, P).transpose(0, 3, 1, 4, 2, 5)
        return w.reshape(P, 4, 1024)

    nq, nk = KV * REP * HD1, KV * HD1
    qkv = k_rows(L1_attn_w_qkv)
    qkv = np.concatenate([qkv[:, :, :nq].reshape(P, KB, KV, REP * HD1),
                          qkv[:, :, nq:nq + nk].reshape(P, KB, KV, HD1),
                          qkv[:, :, nq + nk:].reshape(P, KB, KV, HD1)], axis=3)
    w0 = np.stack([np.concatenate([k_rows(L0_attn_Wq), k_rows(L0_attn_Wk)], axis=2),
                   np.concatenate([k_rows(L0_attn_Wv), k_rows(L0_attn_Wo)], axis=2)], axis=1)
    qw, kw = a(L1_attn_q_norm_w), a(L1_attn_k_norm_w)
    qr, kr = np.roll(qw, HD1 // 2), np.roll(kw, HD1 // 2)
    norm_w = np.stack([np.concatenate([qw] * REP + [kw]), np.concatenate([qr] * REP + [kr])])
    x = a(L0_attn_x)
    arrays = dict(constants())
    arrays.update({
        "x": x.reshape(B, T, KB, P).transpose(3, 0, 2, 1).reshape(P, B, KB * T),
        "w0": w0.reshape(P, 2, 1024),
        "ug0": up_gate(L0_ffn_W_up, L0_ffn_W_gate),
        "down0": k_rows(L0_ffn_W_down).reshape(P, 2, 1024),
        "qkv": qkv.transpose(0, 2, 1, 3).reshape(P, KV, KB * GV),
        "wout": k_rows(L1_attn_w_out).reshape(P, KV, 512),
        "ug1": up_gate(L1_ffn_w_up, L1_ffn_w_gate),
        "down1": k_rows(L1_ffn_w_down).reshape(P, 2, 1024),
        "sign_ug": a(L0_ffn_SU_ug).reshape(KB, P).T,
        "sign_dp": a(L0_ffn_SU_dp).reshape(NI, P).T,
        "scale_ug": a(L0_ffn_Wscale_ug).reshape(2 * NI, P).T,
        "scale_dp": np.broadcast_to(a(L0_ffn_Wscale_dp), (P, C)),
        "norm_w": np.broadcast_to(norm_w, (P, 2, GW)),
        "x_rows": x.reshape(B * TT, P, C).transpose(1, 0, 2),
    })
    nc = bacc.Bacc("TRN2", target_bir_lowering=False, num_devices=1)
    feed, dram = {}, {}
    for name, v in arrays.items():
        v = np.ascontiguousarray(v)
        feed["in_" + name] = v
        dram[name] = nc.dram_tensor("in_" + name, v.shape, mybir.dt.from_np(v.dtype), kind="ExternalInput").ap()
    out = nc.dram_tensor("out", (B, T, C), F32, kind="ExternalOutput").ap()
    post_ln_two_layers(nc, dram, out.rearrange("b (t p) c -> p (b t) c", p=P))
    r = run_bass_kernel_spmd(nc, [feed], core_ids=[0])
    return r.results[0]["out"]
```
